# Optimizing a Trainium2 kernel written in Bass

```python
import numpy as np
import jax
import jax.numpy as jnp

def _softmax(x, axis=-1):
    return jax.nn.softmax(x, axis=axis)

def _gelu(x):
    return jax.nn.gelu(x, approximate=True)

def _silu(x):
    return jax.nn.silu(x)

def _sigmoid(x):
    return jax.nn.sigmoid(x)

def _layernorm(x, axis=-1, eps=1e-05):
    m = jnp.mean(x, axis=axis, keepdims=True)
    v = jnp.var(x, axis=axis, keepdims=True)
    return (x - m) / jnp.sqrt(v + eps)

def _scatter_add(tgt, idx, src, axis=0):
    return tgt.at[idx].add(src)

def _segment_sum(src, seg, n):
    return jax.ops.segment_sum(src, seg, n)
kernel_name = 'mk_gnn_resnorm_d4_gnn_r32_d0b686'

def setup_inputs(seed: int=0):
    np.random.seed(seed)
    _w = jnp.asarray

    def _rec_inputs():
        import jax
        import jax.numpy as jnp
        _gk = jax.random.key(seed)
        x = -0.0002117 + 1 * jax.random.normal(jax.random.fold_in(_gk, 1), (3125, 256), jnp.float32)
        src = jax.random.randint(jax.random.fold_in(_gk, 2), (50000,), 0, 3125, jnp.int32)
        dst = jax.random.randint(jax.random.fold_in(_gk, 3), (50000,), 0, 3125, jnp.int32)
        _o = jnp.argsort(dst, stable=True)
        src = src[_o]
        dst = dst[_o]
        edge_attr_3 = -1.09012e-05 + 0.99985 * jax.random.normal(jax.random.fold_in(_gk, 12), (50000, 3), jnp.float32)
        edge_weight = jax.random.uniform(jax.random.fold_in(_gk, 14), (50000,), jnp.float32, 0.0, 1)
        return (x, src, dst, edge_attr_3, edge_weight)
    x, src, dst, edge_attr_3, edge_weight = _rec_inputs()

    def _L0_gnn_setup():
        import jax, jax.numpy as jnp
        import numpy as np
        N_NODES = 3125
        N_EDGES = 100000
        D_IN = 256
        D_OUT = 256
        key = jax.random.key(seed)
        k1, k2, k3, k4, k5, k6 = jax.random.split(key, 6)
        x = jax.random.normal(k1, (N_NODES, D_IN), dtype=jnp.float32)
        edge_row = jax.random.randint(k2, (N_EDGES,), 0, N_NODES, dtype=jnp.int32)
        edge_col = jax.random.randint(k3, (N_EDGES,), 0, N_NODES, dtype=jnp.int32)
        edge_weight = jax.random.uniform(k4, (N_EDGES,), dtype=jnp.float32)
        stdv = 1.0 / np.sqrt(D_OUT)
        weight = jax.random.uniform(k5, (2 * D_IN, D_OUT), minval=-stdv, maxval=stdv, dtype=jnp.float32)
        bias = jax.random.uniform(k6, (D_OUT,), minval=-stdv, maxval=stdv, dtype=jnp.float32)
        return {'x': x, 'edge_row': edge_row, 'edge_col': edge_col, 'edge_weight': edge_weight, 'weight': weight, 'bias': bias}
    _L0_gnn_all = _L0_gnn_setup()
    _L0_gnn_in = {k: v for k, v in _L0_gnn_all.items() if k in ('weight', 'bias')}
    del _L0_gnn_all

    def _L1_gnn_setup():
        import jax, jax.numpy as jnp
        import numpy as np
        N = 50000
        E = 12500
        IN = 256
        H = 8
        D = 32
        EF = 3
        key = jax.random.key(seed)
        ks = jax.random.split(key, 8)
        x = jax.random.normal(ks[0], (N, IN), dtype=jnp.float32)
        edge_index = jax.random.randint(ks[1], (2, E), 0, N, dtype=jnp.int64)
        edge_attr = jax.random.normal(ks[2], (E, EF), dtype=jnp.float32)
        W = jax.random.normal(ks[3], (H * D, IN), dtype=jnp.float32) * np.float32(np.sqrt(2.0 / (IN + H * D)))
        a_src = jax.random.normal(ks[4], (H, D), dtype=jnp.float32) * np.float32(np.sqrt(2.0 / (H + D)))
        a_dst = jax.random.normal(ks[5], (H, D), dtype=jnp.float32) * np.float32(np.sqrt(2.0 / (H + D)))
        edge_W = jax.random.normal(ks[6], (H * D, EF), dtype=jnp.float32) * np.float32(np.sqrt(2.0 / (EF + H * D)))
        edge_b = jnp.zeros((H * D,), dtype=jnp.float32)
        bias = jnp.zeros((H * D,), dtype=jnp.float32)
        return {'x': x, 'W': W, 'a_src': a_src, 'a_dst': a_dst, 'edge_W': edge_W, 'edge_b': edge_b, 'bias': bias, 'edge_attr': edge_attr, 'edge_index': edge_index}
    _L1_gnn_all = _L1_gnn_setup()
    _L1_gnn_in = {k: v for k, v in _L1_gnn_all.items() if k in ('W', 'a_src', 'a_dst', 'edge_W', 'edge_b', 'bias')}
    del _L1_gnn_all

    def _L2_gnn_setup():
        import jax, jax.numpy as jnp
        import numpy as np
        N = 3125
        E = 25000
        F_IN = 256
        HID = 64
        H = 4
        NEG_SLOPE = 0.2
        BN_EPS = 1e-05

        def _add_self_loops(edge_index, n):
            loop = jnp.arange(n, dtype=edge_index.dtype)
            src = jnp.concatenate([edge_index[0], loop])
            dst = jnp.concatenate([edge_index[1], loop])
            return (src, dst)

        def _batch_norm(x, g, b):
            m = x.mean(0)
            v = x.var(0)
            return g * (x - m) * jax.lax.rsqrt(v + BN_EPS) + b

        def _gcn_conv(x, src, dst, W, b, n):
            deg = jax.ops.segment_sum(jnp.ones_like(dst, jnp.float32), dst, n)
            dinv = jax.lax.rsqrt(jnp.maximum(deg, 1.0))
            norm = dinv[src] * dinv[dst]
            h = x @ W
            out = jax.ops.segment_sum(h[src] * norm[:, None], dst, n)
            return out + b

        def _gat_conv(x, src, dst, W, a_src, a_dst, b, n):
            h = (x @ W).reshape(n, H, HID)
            alpha_s = jnp.einsum('nhc,hc->nh', h, a_src)
            alpha_d = jnp.einsum('nhc,hc->nh', h, a_dst)
            e = alpha_s[src] + alpha_d[dst]
            e = jnp.where(e > 0, e, NEG_SLOPE * e)
            emax = jax.ops.segment_max(e, dst, n)
            w = jnp.exp(e - emax[dst])
            wsum = jax.ops.segment_sum(w, dst, n)
            att = w / wsum[dst]
            out = jax.ops.segment_sum(att[:, :, None] * h[src], dst, n)
            return out.reshape(n, H * HID) + b
        key = jax.random.key(seed)
        ks = jax.random.split(key, 20)
        s = 0.05
        return {'x': jax.random.normal(ks[0], (N, F_IN), jnp.float32), 'edge_index': jax.random.randint(ks[1], (2, E), 0, N, jnp.int64), 'W_gcn': jax.random.normal(ks[2], (F_IN, HID), jnp.float32) * s, 'b_gcn': jnp.zeros((HID,), jnp.float32), 'g0': jnp.ones((HID,), jnp.float32), 'beta0': jnp.zeros((HID,), jnp.float32), 'W1': jax.random.normal(ks[3], (HID, H * HID), jnp.float32) * s, 'a_src1': jax.random.normal(ks[4], (H, HID), jnp.float32) * s, 'a_dst1': jax.random.normal(ks[5], (H, HID), jnp.float32) * s, 'b1': jnp.zeros((H * HID,), jnp.float32), 'g1': jnp.ones((H * HID,), jnp.float32), 'beta1': jnp.zeros((H * HID,), jnp.float32), 'W2': jax.random.normal(ks[6], (H * HID, H * HID), jnp.float32) * s, 'a_src2': jax.random.normal(ks[7], (H, HID), jnp.float32) * s, 'a_dst2': jax.random.normal(ks[8], (H, HID), jnp.float32) * s, 'b2': jnp.zeros((H * HID,), jnp.float32), 'g2': jnp.ones((H * HID,), jnp.float32), 'beta2': jnp.zeros((H * HID,), jnp.float32)}
    _L2_gnn_all = _L2_gnn_setup()
    _L2_gnn_in = {k: v for k, v in _L2_gnn_all.items() if k in ('W_gcn', 'b_gcn', 'g0', 'beta0', 'W1', 'a_src1', 'a_dst1', 'b1', 'g1', 'beta1', 'W2', 'a_src2', 'a_dst2', 'b2', 'g2', 'beta2')}
    del _L2_gnn_all

    def _L3_gnn_setup():
        import jax, jax.numpy as jnp
        import numpy as np
        N, E, D = (3125, 50000, 256)
        BN_EPS = 1e-05

        def _bn(x, g, b):
            m = jnp.mean(x, axis=0)
            v = jnp.var(x, axis=0)
            return (x - m) * jax.lax.rsqrt(v + BN_EPS) * g + b

        def _gin_layer(h, src, dst, w1, b1, g1, be1, w2, b2, g2=None, be2=None):
            agg = h + jax.ops.segment_sum(h[src], dst, num_segments=N)
            z = jax.nn.relu(_bn(agg @ w1 + b1, g1, be1))
            z = z @ w2 + b2
            if g2 is not None:
                z = jax.nn.relu(_bn(z, g2, be2))
            return z
        key = jax.random.key(seed)
        ks = jax.random.split(key, 16)
        inp = {}
        inp['x'] = jax.random.normal(ks[0], (N, D), jnp.float32)
        inp['src'] = jax.random.randint(ks[1], (E,), 0, N)
        inp['dst'] = jax.random.randint(ks[2], (E,), 0, N)
        i = 3
        for l in range(3):
            inp[f'l{l}_w1'] = jax.random.normal(ks[i], (D, D), jnp.float32) * 0.02
            i += 1
            inp[f'l{l}_b1'] = jnp.zeros((D,), jnp.float32)
            inp[f'l{l}_g1'] = jnp.ones((D,), jnp.float32)
            inp[f'l{l}_be1'] = jnp.zeros((D,), jnp.float32)
            inp[f'l{l}_w2'] = jax.random.normal(ks[i], (D, D), jnp.float32) * 0.02
            i += 1
            inp[f'l{l}_b2'] = jnp.zeros((D,), jnp.float32)
            if l < 2:
                inp[f'l{l}_g2'] = jnp.ones((D,), jnp.float32)
                inp[f'l{l}_be2'] = jnp.zeros((D,), jnp.float32)
        return inp
    _L3_gnn_all = _L3_gnn_setup()
    _L3_gnn_in = {k: v for k, v in _L3_gnn_all.items() if k in ('l0_w1', 'l0_b1', 'l0_g1', 'l0_be1', 'l0_w2', 'l0_b2', 'l0_g2', 'l0_be2', 'l1_w1', 'l1_b1', 'l1_g1', 'l1_be1', 'l1_w2', 'l1_b2', 'l1_g2', 'l1_be2', 'l2_w1', 'l2_b1', 'l2_g1', 'l2_be1', 'l2_w2', 'l2_b2')}
    del _L3_gnn_all
    return {'x': x, 'src': src, 'dst': dst, 'edge_attr_3': edge_attr_3, 'edge_weight': edge_weight, 'L0_gnn_weight': _L0_gnn_in['weight'], 'L0_gnn_bias': _L0_gnn_in['bias'], 'L1_gnn_W': _L1_gnn_in['W'], 'L1_gnn_a_src': _L1_gnn_in['a_src'], 'L1_gnn_a_dst': _L1_gnn_in['a_dst'], 'L1_gnn_edge_W': _L1_gnn_in['edge_W'], 'L1_gnn_edge_b': _L1_gnn_in['edge_b'], 'L1_gnn_bias': _L1_gnn_in['bias'], 'L2_gnn_W_gcn': _L2_gnn_in['W_gcn'], 'L2_gnn_b_gcn': _L2_gnn_in['b_gcn'], 'L2_gnn_g0': _L2_gnn_in['g0'], 'L2_gnn_beta0': _L2_gnn_in['beta0'], 'L2_gnn_W1': _L2_gnn_in['W1'], 'L2_gnn_a_src1': _L2_gnn_in['a_src1'], 'L2_gnn_a_dst1': _L2_gnn_in['a_dst1'], 'L2_gnn_b1': _L2_gnn_in['b1'], 'L2_gnn_g1': _L2_gnn_in['g1'], 'L2_gnn_beta1': _L2_gnn_in['beta1'], 'L2_gnn_W2': _L2_gnn_in['W2'], 'L2_gnn_a_src2': _L2_gnn_in['a_src2'], 'L2_gnn_a_dst2': _L2_gnn_in['a_dst2'], 'L2_gnn_b2': _L2_gnn_in['b2'], 'L2_gnn_g2': _L2_gnn_in['g2'], 'L2_gnn_beta2': _L2_gnn_in['beta2'], 'L3_gnn_l0_w1': _L3_gnn_in['l0_w1'], 'L3_gnn_l0_b1': _L3_gnn_in['l0_b1'], 'L3_gnn_l0_g1': _L3_gnn_in['l0_g1'], 'L3_gnn_l0_be1': _L3_gnn_in['l0_be1'], 'L3_gnn_l0_w2': _L3_gnn_in['l0_w2'], 'L3_gnn_l0_b2': _L3_gnn_in['l0_b2'], 'L3_gnn_l0_g2': _L3_gnn_in['l0_g2'], 'L3_gnn_l0_be2': _L3_gnn_in['l0_be2'], 'L3_gnn_l1_w1': _L3_gnn_in['l1_w1'], 'L3_gnn_l1_b1': _L3_gnn_in['l1_b1'], 'L3_gnn_l1_g1': _L3_gnn_in['l1_g1'], 'L3_gnn_l1_be1': _L3_gnn_in['l1_be1'], 'L3_gnn_l1_w2': _L3_gnn_in['l1_w2'], 'L3_gnn_l1_b2': _L3_gnn_in['l1_b2'], 'L3_gnn_l1_g2': _L3_gnn_in['l1_g2'], 'L3_gnn_l1_be2': _L3_gnn_in['l1_be2'], 'L3_gnn_l2_w1': _L3_gnn_in['l2_w1'], 'L3_gnn_l2_b1': _L3_gnn_in['l2_b1'], 'L3_gnn_l2_g1': _L3_gnn_in['l2_g1'], 'L3_gnn_l2_be1': _L3_gnn_in['l2_be1'], 'L3_gnn_l2_w2': _L3_gnn_in['l2_w2'], 'L3_gnn_l2_b2': _L3_gnn_in['l2_b2']}

def reference(x, src, dst, edge_attr_3, edge_weight, L0_gnn_weight, L0_gnn_bias, L1_gnn_W, L1_gnn_a_src, L1_gnn_a_dst, L1_gnn_edge_W, L1_gnn_edge_b, L1_gnn_bias, L2_gnn_W_gcn, L2_gnn_b_gcn, L2_gnn_g0, L2_gnn_beta0, L2_gnn_W1, L2_gnn_a_src1, L2_gnn_a_dst1, L2_gnn_b1, L2_gnn_g1, L2_gnn_beta1, L2_gnn_W2, L2_gnn_a_src2, L2_gnn_a_dst2, L2_gnn_b2, L2_gnn_g2, L2_gnn_beta2, L3_gnn_l0_w1, L3_gnn_l0_b1, L3_gnn_l0_g1, L3_gnn_l0_be1, L3_gnn_l0_w2, L3_gnn_l0_b2, L3_gnn_l0_g2, L3_gnn_l0_be2, L3_gnn_l1_w1, L3_gnn_l1_b1, L3_gnn_l1_g1, L3_gnn_l1_be1, L3_gnn_l1_w2, L3_gnn_l1_b2, L3_gnn_l1_g2, L3_gnn_l1_be2, L3_gnn_l2_w1, L3_gnn_l2_b1, L3_gnn_l2_g1, L3_gnn_l2_be1, L3_gnn_l2_w2, L3_gnn_l2_b2):
    import jax
    import jax.numpy as jnp

    def _L0_gnn_ref(x, edge_row, edge_col, edge_weight, weight, bias):
        import jax, jax.numpy as jnp
        import numpy as np
        N_NODES = 3125
        N_EDGES = 100000
        D_IN = 256
        D_OUT = 256
        gathered = edge_weight[:, None] * x[edge_col]
        neigh = jax.ops.segment_sum(gathered, edge_row, num_segments=N_NODES)
        w_self, w_neigh = (weight[:D_IN], weight[D_IN:])
        out = x @ w_self + neigh @ w_neigh + bias
        return out

    def _L1_gnn_ref(x, W, a_src, a_dst, edge_W, edge_b, bias, edge_attr, edge_index):
        import jax, jax.numpy as jnp
        import numpy as np
        N = 50000
        E = 12500
        IN = 256
        H = 8
        D = 32
        EF = 3
        n = x.shape[0]
        h = (x @ W.T).reshape(n, H, D)
        src, dst = (edge_index[0], edge_index[1])
        h_src = h[src]
        h_dst = h[dst]
        alpha = jnp.einsum('ehd,hd->eh', h_src, a_src) + jnp.einsum('ehd,hd->eh', h_dst, a_dst)
        enc = jax.nn.relu(edge_attr @ edge_W.T + edge_b).reshape(-1, H, D)
        alpha = alpha + jnp.sum(enc * h_dst, axis=-1)
        alpha = jnp.where(alpha >= 0, alpha, 0.2 * alpha)
        amax = jax.ops.segment_max(alpha, dst, num_segments=n)
        ex = jnp.exp(alpha - amax[dst])
        denom = jax.ops.segment_sum(ex, dst, num_segments=n)
        attn = ex / jnp.maximum(denom[dst], 1e-10)
        out = jax.ops.segment_sum(h_src * attn[..., None], dst, num_segments=n)
        return out.reshape(n, H * D) + bias

    def _L2_gnn_ref(x, edge_index, W_gcn, b_gcn, g0, beta0, W1, a_src1, a_dst1, b1, g1, beta1, W2, a_src2, a_dst2, b2, g2, beta2):
        import jax, jax.numpy as jnp
        import numpy as np
        N = 3125
        E = 25000
        F_IN = 256
        HID = 64
        H = 4
        NEG_SLOPE = 0.2
        BN_EPS = 1e-05

        def _add_self_loops(edge_index, n):
            loop = jnp.arange(n, dtype=edge_index.dtype)
            src = jnp.concatenate([edge_index[0], loop])
            dst = jnp.concatenate([edge_index[1], loop])
            return (src, dst)

        def _batch_norm(x, g, b):
            m = x.mean(0)
            v = x.var(0)
            return g * (x - m) * jax.lax.rsqrt(v + BN_EPS) + b

        def _gcn_conv(x, src, dst, W, b, n):
            deg = jax.ops.segment_sum(jnp.ones_like(dst, jnp.float32), dst, n)
            dinv = jax.lax.rsqrt(jnp.maximum(deg, 1.0))
            norm = dinv[src] * dinv[dst]
            h = x @ W
            out = jax.ops.segment_sum(h[src] * norm[:, None], dst, n)
            return out + b

        def _gat_conv(x, src, dst, W, a_src, a_dst, b, n):
            h = (x @ W).reshape(n, H, HID)
            alpha_s = jnp.einsum('nhc,hc->nh', h, a_src)
            alpha_d = jnp.einsum('nhc,hc->nh', h, a_dst)
            e = alpha_s[src] + alpha_d[dst]
            e = jnp.where(e > 0, e, NEG_SLOPE * e)
            emax = jax.ops.segment_max(e, dst, n)
            w = jnp.exp(e - emax[dst])
            wsum = jax.ops.segment_sum(w, dst, n)
            att = w / wsum[dst]
            out = jax.ops.segment_sum(att[:, :, None] * h[src], dst, n)
            return out.reshape(n, H * HID) + b
        n = x.shape[0]
        src, dst = _add_self_loops(edge_index, n)
        h = jax.nn.relu(_gcn_conv(x, src, dst, W_gcn, b_gcn, n))
        h = _batch_norm(h, g0, beta0)
        h = _gat_conv(h, src, dst, W1, a_src1, a_dst1, b1, n)
        h = jax.nn.elu(_batch_norm(h, g1, beta1))
        h = _gat_conv(h, src, dst, W2, a_src2, a_dst2, b2, n)
        h = jax.nn.elu(_batch_norm(h, g2, beta2))
        return h

    def _L3_gnn_ref(x, src, dst, l0_w1, l0_b1, l0_g1, l0_be1, l0_w2, l0_b2, l0_g2, l0_be2, l1_w1, l1_b1, l1_g1, l1_be1, l1_w2, l1_b2, l1_g2, l1_be2, l2_w1, l2_b1, l2_g1, l2_be1, l2_w2, l2_b2):
        import jax, jax.numpy as jnp
        import numpy as np
        N, E, D = (3125, 50000, 256)
        BN_EPS = 1e-05

        def _bn(x, g, b):
            m = jnp.mean(x, axis=0)
            v = jnp.var(x, axis=0)
            return (x - m) * jax.lax.rsqrt(v + BN_EPS) * g + b

        def _gin_layer(h, src, dst, w1, b1, g1, be1, w2, b2, g2=None, be2=None):
            agg = h + jax.ops.segment_sum(h[src], dst, num_segments=N)
            z = jax.nn.relu(_bn(agg @ w1 + b1, g1, be1))
            z = z @ w2 + b2
            if g2 is not None:
                z = jax.nn.relu(_bn(z, g2, be2))
            return z
        h = _gin_layer(x, src, dst, l0_w1, l0_b1, l0_g1, l0_be1, l0_w2, l0_b2, l0_g2, l0_be2)
        h = _gin_layer(h, src, dst, l1_w1, l1_b1, l1_g1, l1_be1, l1_w2, l1_b2, l1_g2, l1_be2)
        h = _gin_layer(h, src, dst, l2_w1, l2_b1, l2_g1, l2_be1, l2_w2, l2_b2)
        return h
    edge_index = jnp.stack([src, dst])
    x = _layernorm(x + _L0_gnn_ref(x, src, dst, edge_weight, L0_gnn_weight, L0_gnn_bias), axis=-1)
    x = _layernorm(x + _L1_gnn_ref(x, L1_gnn_W, L1_gnn_a_src, L1_gnn_a_dst, L1_gnn_edge_W, L1_gnn_edge_b, L1_gnn_bias, edge_attr_3, edge_index), axis=-1)
    x = _layernorm(x + _L2_gnn_ref(x, edge_index, L2_gnn_W_gcn, L2_gnn_b_gcn, L2_gnn_g0, L2_gnn_beta0, L2_gnn_W1, L2_gnn_a_src1, L2_gnn_a_dst1, L2_gnn_b1, L2_gnn_g1, L2_gnn_beta1, L2_gnn_W2, L2_gnn_a_src2, L2_gnn_a_dst2, L2_gnn_b2, L2_gnn_g2, L2_gnn_beta2), axis=-1)
    x = _layernorm(x + _L3_gnn_ref(x, src, dst, L3_gnn_l0_w1, L3_gnn_l0_b1, L3_gnn_l0_g1, L3_gnn_l0_be1, L3_gnn_l0_w2, L3_gnn_l0_b2, L3_gnn_l0_g2, L3_gnn_l0_be2, L3_gnn_l1_w1, L3_gnn_l1_b1, L3_gnn_l1_g1, L3_gnn_l1_be1, L3_gnn_l1_w2, L3_gnn_l1_b2, L3_gnn_l1_g2, L3_gnn_l1_be2, L3_gnn_l2_w1, L3_gnn_l2_b1, L3_gnn_l2_g1, L3_gnn_l2_be1, L3_gnn_l2_w2, L3_gnn_l2_b2), axis=-1)
    return x

_drawn_inputs = setup_inputs


def setup_inputs(seed=0):
    import zlib

    import numpy as np

    out = dict(_drawn_inputs(seed))
    spreads = {'L1_gnn_edge_b': (0.0, 0.1),
     'L1_gnn_bias': (0.0, 0.1),
     'L2_gnn_b_gcn': (0.0, 0.1),
     'L2_gnn_g0': (1.0, 0.2),
     'L2_gnn_beta0': (0.0, 2.0),
     'L2_gnn_b1': (0.0, 2.0),
     'L2_gnn_g1': (1.0, 0.2),
     'L2_gnn_beta1': (0.0, 0.289),
     'L2_gnn_b2': (0.0, 2.0),
     'L2_gnn_g2': (1.0, 0.2),
     'L2_gnn_beta2': (0.0, 0.1),
     'L3_gnn_l0_b1': (0.0, 2.0),
     'L3_gnn_l0_g1': (1.0, 0.2),
     'L3_gnn_l0_be1': (0.0, 0.369),
     'L3_gnn_l0_b2': (0.0, 2.0),
     'L3_gnn_l0_g2': (1.0, 0.2),
     'L3_gnn_l0_be2': (0.0, 0.293),
     'L3_gnn_l1_b1': (0.0, 2.0),
     'L3_gnn_l1_g1': (1.0, 0.2),
     'L3_gnn_l1_be1': (0.0, 0.407),
     'L3_gnn_l1_b2': (0.0, 2.0),
     'L3_gnn_l1_g2': (1.0, 0.2),
     'L3_gnn_l1_be2': (0.0, 0.377),
     'L3_gnn_l2_b1': (0.0, 2.0),
     'L3_gnn_l2_g1': (1.0, 0.2),
     'L3_gnn_l2_be1': (0.0, 0.376),
     'L3_gnn_l2_b2': (0.0, 0.1)}
    factors = {}
    for name, (base, spread) in spreads.items():
        noise = np.random.default_rng([zlib.crc32(name.encode()), seed]).standard_normal(out[name].shape)
        drawn = base * np.exp(spread * noise) if base else spread * noise
        out[name] = jnp.asarray(drawn.astype(out[name].dtype))
    for name, factor in factors.items():
        out[name] = (out[name] * factor).astype(out[name].dtype)
    return out
```

```python
from contextlib import ExitStack

import concourse.bass as bass
from concourse import mybir

P = 128
N = 3125
NT = 25
NP = NT * P
E = 50000
ET = 392
EB, EQ = 4, 98
S = ET + NT - 1
SB, SQ = 4, 104
UN, HU = 16, 8
D = 256
GW = 272
DC = D // P
BIG = 1.0e30
LN_EPS = 1e-5
BN_EPS = 1e-5
L0U, L0H = 8, 4
L0IT = ET // L0U
ETX = ET + L0U
TRASH = NP
NACC = 4
NODE_CHUNKS = [(c * 512, min(512, NP - c * 512)) for c in range((NP + 511) // 512)]
BN_CHUNKS = [(c * 512, min(512, N - c * 512)) for c in range((N + 511) // 512)]

F32 = mybir.dt.float32
I32 = mybir.dt.int32
ALU = mybir.AluOpType
ACT = mybir.ActivationFunctionType
AX = mybir.AxisListType

ROWS = ["L0_gnn_bias", "L1_gnn_a_src", "L1_gnn_a_dst", "L1_gnn_bias", "L2_gnn_a_src1", "L2_gnn_a_dst1", "L2_gnn_b1",
        "L2_gnn_a_src2", "L2_gnn_a_dst2", "L2_gnn_b2", "L3_gnn_l2_b2", "L2_gnn_b_gcn"]
COLS = ["L2_gnn_g1", "L2_gnn_beta1", "L2_gnn_g2", "L2_gnn_beta2"] + [
    f"L3_gnn_l{l}_{v}" for l in range(3) for v in ("b1", "g1", "be1", "b2", "g2", "be2") if l < 2 or v in ("b1", "g1", "be1")
] + ["L2_gnn_g0", "L2_gnn_beta0"]


def build(nc, a):
    with ExitStack() as ctx:
        def sb(name, shape, dt=F32):
            return ctx.enter_context(nc.sbuf_tensor(name, shape, dt))

        def sem(name):
            return ctx.enter_context(nc.semaphore(name))

        def dram(name, shape, dt=F32):
            return nc.dram_tensor(name, shape, dt).ap()

        cols = sb("cols", [P, 2, NP])
        resid = sb("resid", [P, NT, D])
        accum = sb("accum", [P, NT, GW])
        hrows = sb("hrows", [P, NT, GW])
        accum_t = accum[:, :, :].rearrange("p t w -> p (t w)")[:, 0:2 * NP].rearrange("p (c n) -> p c n", c=2)
        slots = sb("slots", [P, UN, GW])
        onehot = sb("onehot", [P, UN, P])
        alpha = sb("alpha", [P, S, 8])
        peak = sb("peak", [P, S, 8])
        src_x = sb("src_x", [P, S], I32)
        dst_x = sb("dst_x", [P, S], I32)
        drel = sb("drel", [P, S])
        tn_i = sb("tn_i", [P, S], I32)
        te_i = sb("te_i", [SQ, SB], I32)
        reset_f = sb("reset_f", [SQ, SB, P])
        reset_r = sb("reset_r", [SQ, SB, P])
        with_first = sb("with_first", [SQ, SB, P])
        with_last = sb("with_last", [SQ, SB, P])
        carry_ok = sb("carry_ok", [8, S + 1])
        through_f = sb("through_f", [8, S])
        through_r = sb("through_r", [8, S])
        iota = sb("iota", [P, S])
        iota_p = sb("iota_p", [P, 1])
        ident = sb("ident", [P, P])
        before = sb("before", [P, P])
        ones = sb("ones", [P, P])
        idx_a = sb("idx_a", [P, UN], I32)
        idx_b = sb("idx_b", [P, UN], I32)
        node_s = sb("node_s", [P, NT, 16])
        small = sb("small", [P, NT, 8])
        deg = sb("deg", [P, NT, 2])
        weights = sb("weights", [P, 4, D])
        rows = sb("rows", [P, len(ROWS), D])
        vecs = sb("vecs", [P, len(COLS), 2])
        stats = sb("stats", [P, NT, 8])
        mv = sb("mv", [P, NT, 2])
        bnst = sb("bnst", [P, 2, len(BN_CHUNKS), 6])
        bnmv = sb("bnmv", [P, 2, 2])
        bnsc = sb("bnsc", [P, 2, 4])
        attr_w = sb("attr_w", [4, D])
        carry = sb("carry", [8, S + 2])
        carry2 = sb("carry2", [8, S])
        carry_c = sb("carry_c", [SQ, SB, 8])
        te_last_i = sb("te_last_i", [EQ, EB, 1], I32)
        te_last = sb("te_last", [EQ, EB])
        attr_c = slots[0:4, :, :].rearrange("p u w -> p (u w)")[:, 0:2 * HU * P].rearrange("p (h k e) -> p h k e", h=2, k=HU)
        as_ring = sb("as_ring", [P, UN, 8])
        ad_ring = sb("ad_ring", [P, UN, 8])
        enc = accum[:, 0:16, 0:D]
        hd_ring = hrows[:, 0:16, :]
        segs = accum[0:SQ, :, :].rearrange("p t w -> p (t w)")[:, 0:8 * SB * P].rearrange("p (h b e) -> p h b e", h=8, b=SB)
        flat_a = accum[:, :, :].rearrange("p t w -> p (t w)")
        flat_h = hrows[:, :, :].rearrange("p t w -> p (t w)")
        key = flat_h[0:SQ, 0:SB * P].rearrange("p (b e) -> p b e", b=SB)
        srow = flat_h[0:SQ, 512:1024].rearrange("p (b e) -> p b e", b=SB)
        drow = flat_h[0:SQ, 1024:1536].rearrange("p (b e) -> p b e", b=SB)
        key_i = flat_h[0:SQ, 1536:2048].rearrange("p (b e) -> p b e", b=SB).bitcast(I32)
        srow_i = flat_h[0:SQ, 2048:2560].rearrange("p (b e) -> p b e", b=SB).bitcast(I32)
        attr_g = flat_h[0:SQ, 2560:4608].rearrange("p (b e) -> p b e", b=SB)
        mask_t = flat_h[0:EQ, 4608:4608 + EB * S].rearrange("p (b s) -> p b s", b=EB)
        tmp = flat_a[:, 0:2048]
        edge_keys = flat_h[0:SQ, 6272:6272 + 2 * SB * 8].rearrange("p (n b e) -> p n b e", n=2, b=SB)
        neigh_t = flat_h[:, 0:2 * NP].rearrange("p (c n) -> p c n", c=2)
        dst_t = sb("dst_t", [P, ETX], I32)
        l0 = resid[:, :, :].rearrange("p t d -> p (t d)")
        src_f = l0[:, 0:ETX]
        ew_t = l0[:, 512:512 + ETX]
        src_i0 = l0[:, 1024:1024 + ETX].bitcast(I32)
        eq = l0[:, 1536:1536 + L0U * P].rearrange("p (u e) -> p u e", u=L0U)
        src_b = l0[:, 2560:2560 + L0U * P].rearrange("p (u e) -> p u e", u=L0U)
        msg = l0[:, 3584:3584 + L0U * 256].rearrange("p (u e) -> p u e", u=L0U)
        cnt = l0[:, 5632:5640]
        l0d = l0[:, 5640:5648]
        l0m = l0[:, 5648:5656]
        trash_p = l0[:, 5656:5657]
        pre4 = l0[:, 5660:5664]

        ps = ctx.enter_context(nc.psum_tensor("ps", [P, 8, 512], F32))

        table = [dram(f"table{k}", (NP, D)) for k in range(7)]
        t_gcn = dram("t_gcn", (NP, 64))
        t_as = [dram(f"t_as{k}", (NP, 8)) for k in range(3)]
        t_ad = [dram("t_ad0", (NP, GW))] + [dram(f"t_ad{k}", (NP, 8)) for k in (1, 2)]
        t_neigh = [dram(f"t_neigh{k}", (NP + P, D)) for k in range(NACC)]
        t_attr = dram("t_attr", (S, 4 * P))

        gath = [sem(f"gath{u}") for u in range(UN)]
        gath2 = [sem(f"gath2_{u}") for u in range(UN)]
        idx_ready = sem("idx_ready")
        msg_ready = sem("msg_ready")
        oh_ready = sem("oh_ready")
        step_mm = sem("step_mm")
        step_acc = sem("step_acc")
        dv = sem("dv")
        scat = [sem(f"scat{k}") for k in range(NACC)]
        attr_in = [sem(f"attr_in{h}") for h in range(2)]

        def runs(end, *names):
            return [(n + end, c) for n, c in names]

        def by_layer(name, *counts):
            return [(f"{name}{k}", c) for k, c in enumerate(counts)]

        turns = [(n, NT) for n in ("l0n", "x1", "x2", "gcnt", "gatt1", "gatt2", "l2r", "x3", "gint0", "gint1")]
        products = [(n, NT) for n in ("l0", "l1", "gcn", "gat1", "gat2", "gin_last")]
        gin = [(n, 2 * len(NODE_CHUNKS)) for n in ("gin_mm1_0", "gin_mm2_0", "gin_mm1_1", "gin_mm2_1", "gin_mm1_2")]
        norms = [(n, 1) for n in ("gcn", "gat1", "gat2", "gin0a", "gin0b", "gin1a", "gin1b", "gin2a")]
        rooted = [(n, 1) for n in ("ln0", "deg", "ln1", "bn_gcn", "bn_gat1", "bn_gat2", "ln2", "bn_gin0a", "bn_gin0b",
                                   "bn_gin1a", "bn_gin1b", "bn_gin2a", "ln3")]
        shared = [runs("_tp", *turns), runs("_ev", *turns), runs("_mm", *products), runs("_ev", *products),
                  gin, runs("_ev", *gin), [("var_" + n, c) for n, c in rooted], [("std_" + n, c) for n, c in rooted],
                  [("bnsc_" + n, c) for n, c in norms],
                  by_layer("al_t", 8, 4, 4), by_layer("scan_f", 8, 4, 4), by_layer("scan_r", 8, 4, 4), by_layer("peak_t", 8, 4, 4),
                  by_layer("peak_ev", 8, 4, 4), by_layer("ends", 2, 2, 2), by_layer("carried", 2, 2, 2), by_layer("carry_t", 2, 2, 2),
                  by_layer("segs_done", 1, 1, 1), by_layer("lrelu", 1, 1, 1), by_layer("alpha_sub", 1, 1, 1), by_layer("exp", 1, 1, 1),
                  by_layer("scores", 1, 1, 1), by_layer("ln", 1, 1, 1, 1), by_layer("gin_z", 1, 1, 1), by_layer("gin_h", 1, 1),
                  [(f"elu_neg{k}", 2) for k in (1, 2)], [(f"elu_exp{k}", 2) for k in (1, 2)],
                  [(f"{n}{k}", 1) for k in (1, 2) for n in ("gat_in", "self_sub", "gat_out")] + [("elu2", 1)],
                  [("self_w1", 1), ("self_w2", 1)]]
        stage = {}
        for group in shared:
            base, signal = 0, sem("s_" + group[0][0])
            for name, n in group:
                stage[name] = (signal, base)
                base += n

        def done(name):
            if name not in stage:
                stage[name] = (sem("s_" + name), 0)
            return stage[name][0]

        def count(name, n):
            return done(name), stage[name][1] + n

        block = ctx.enter_context(nc.Block())

        IDX = {n: i for i, n in enumerate(ROWS)}
        COL = {n: i for i, n in enumerate(COLS)}

        def gath_base(u, g):
            return 16 * (L0IT + 1 if u < L0U else 0) + 16 * (S // UN) * g

        def row(name, w=D):
            return rows[:, IDX[name], 0:w]

        def vec(name, c, p=P):
            return vecs[0:p, COL[name], c:c + 1]

        roots = {f"ln{k}": (small[:, :, 0], small[:, :, 1]) for k in range(4)}
        roots["deg"] = (deg[:, :, 0], deg[:, :, 1])
        for n in ["gat1", "gat2"] + [f"gin{l}{w}" for l in range(3) for w in "ab"]:
            roots[f"bn_{n}"] = (bnsc[:, :, 2], bnsc[:, :, 3])
        roots["bn_gcn"] = (bnsc[0:64, 0:1, 2], bnsc[0:64, 0:1, 3])

        @block.sync
        def _(sp):
            def put(dst, src, s, **how):
                sp.dma_start(dst, src, **how).then_inc(s, 16)

            put(te_last_i[:, :, :], a["dst2"].rearrange("(b q) e -> q b e", b=EB)[:, :, P - 1:P], done("ld_last"), allow_slow_non_contiguous=True)
            put(src_i0, a["src_t"], done("ld_src"))
            put(dst_t[:, :], a["dst_t"], done("ld_dst"))
            put(ew_t, a["ew_t"], done("ld_ew"))
            put(rows[:, :, :], a["rows"], done("ld_rows"))
            put(vecs[:, :, :], a["vecs"], done("ld_vecs"))
            put(attr_w[:, :], a["attr_w"], done("ld_attrw"))
            put(weights[:, :, :], a["L0_gnn_weight"].rearrange("(c p) n -> p c n", p=P), done("ld_w0"))
            put(cols[:, :, :], a["x_cols"].rearrange("(c p) n -> p c n", p=P), done("ld_x"))
            sp.wait_ge(*count("zeroed", 1))
            for k in range(NACC):
                for c in range((NP + P) // P):
                    put(t_neigh[k][c * P:(c + 1) * P, :], flat_a[:, 6400:6400 + D], done("zero_tab"))
            sp.wait_ge(*count("attr_rows", SB * 16))
            put(t_attr.rearrange("(b q) e -> q b e", b=SB), attr_g, done("attr_out"))
            sp.wait_ge(*count("attr_out", 16))
            for k in range(NACC):
                sp.wait_ge(*count("l0_scat_all", 1))
                if k >= 2:
                    sp.wait_ge(*count("l0_summed", k - 1))
                into = [flat_a[:, 0:NT * D], flat_h[:, 0:NT * D]][min(k, 1)] if k < 2 else flat_h[:, 0:NT * D]
                put(into.rearrange("p (t d) -> p t d", t=NT), t_neigh[k][0:NP, :].rearrange("(t p) d -> p t d", p=P), done(f"ld_neigh{k}"))
            for name, n in (("l0_pre", 2 * L0IT + 2), ("l0_msg", 2 * L0IT), ("l0_sidx", 2 * L0IT)):
                sp.wait_ge(*count(name, n))
            put(resid[:, :, :], a["x_pad"].rearrange("(t p) d -> p t d", p=P), done("ld_xrow"))
            sp.wait_ge(*count("l0_mm", NT))
            put(weights[:, 0:2, :], a["L1_gnn_W"].rearrange("(c p) n -> p c n", p=P), done("ld_w1"))

            def put_tables(k, w_ad):
                sp.wait_ge(*count(["l1_ev", "gat1_ev", "gat2_ev"][k], NT))
                put(table[k].rearrange("(t p) d -> p t d", p=P), hrows[:, :, 0:D], done(f"table{k}"))
                sp.wait_ge(*count(f"scores{k}", 1))
                put(t_as[k].rearrange("(t p) d -> p t d", p=P), node_s[:, :, 0:8], done(f"table{k}"))
                if k == 0:
                    put(t_ad[0].rearrange("(t p) d -> p t d", p=P), hrows[:, :, :], done(f"table{k}"))
                else:
                    put(t_ad[k].rearrange("(t p) d -> p t d", p=P), node_s[:, :, 8:16], done(f"table{k}"))

            put_tables(0, GW)
            sp.wait_ge(*count("attr_out", 16))
            with sp.Fori(0, S // UN) as i:
                for h in range(2):
                    sp.wait_ge(*count("enc_free", 2 * i + h + 1))
                    sp.dma_start(attr_c[:, h, :, :],
                                 t_attr.rearrange("s (f e) -> f s e", f=4)[:, bass.ds(i * UN + h * HU, HU), :]
                                 ).then_inc(attr_in[h], 16)
            sp.wait_ge(*count("l1_mm", NT))
            put(weights[:, 2:4, 0:64], a["L2_gnn_W_gcn"].rearrange("(c p) n -> p c n", p=P), done("ld_gcn"))
            sp.wait_ge(*count("gcn_ev", NT))
            put(t_gcn.rearrange("(t p) d -> p t d", p=P), hrows[:, :, 0:64], done("table_gcn"))
            put(weights[0:64, 0, :], a["L2_gnn_W1"], done("ld_gat1"))
            put_tables(1, 8)
            sp.wait_ge(*count("gcn_mm", NT))
            put(weights[:, 2:4, :], a["L2_gnn_W2"].rearrange("(c p) n -> p c n", p=P), done("ld_gat2"))
            put_tables(2, 8)
            for l in range(3):
                if l == 0:
                    sp.wait_ge(*count("ln2", 1))
                    put(table[3].rearrange("(t p) d -> p t d", p=P), resid[:, :, :], done("table3"))
                    sp.wait_ge(*count("gat2_mm", NT))
                else:
                    sp.wait_ge(*count(f"gint{l - 1}_ev", NT))
                    put(table[3 + l].rearrange("(t p) d -> p t d", p=P), hrows[:, :, 0:D], done(f"table{3 + l}"))
                    sp.wait_ge(*count(f"gin_mm2_{l - 1}", 2 * len(NODE_CHUNKS)))
                put(weights[:, 0:2, :], a[f"L3_gnn_l{l}_w1"].rearrange("(c p) n -> p c n", p=P), done(f"ld_gin{l}"))
                put(weights[:, 2:4, :], a[f"L3_gnn_l{l}_w2"].rearrange("(c p) n -> p c n", p=P), done(f"ld_gin{l}"))
            sp.wait_ge(*count("ln3", 1))
            whole = N // P
            put(a["out"][0:whole * P, :].rearrange("(t p) d -> p t d", p=P), resid[:, 0:whole, :], done("out"))
            put(a["out"][whole * P:N, :], resid[0:N - whole * P, whole, :], done("out"))
            sp.wait_ge(*count("out", 32))

        @block.gpsimd
        def _(pool):
            pool.memset(flat_a[:, 6400:6400 + D], 0.0).then_inc(done("zeroed"), 1)
            pool.iota(iota[:, :], [[1, S]], 0, 0, allow_small_or_imprecise_dtypes=True).then_inc(done("iota"), 1)
            pool.iota(iota_p[:, :], [[0, 1]], 0, 1, allow_small_or_imprecise_dtypes=True).then_inc(done("iota"), 1)
            pool.memset(ones[:, :], 1.0).then_inc(done("iota"), 1)
            pool.memset(node_s[:, :, :], 0.0).then_inc(done("iota"), 1)
            pool.wait_ge(*count("te", 1))
            for b in range(SB):
                at = bass.IndirectOffsetOnAxis(ap=te_i[:, b:b + 1], axis=0)
                pool.indirect_dma_start(key_i[:, b, :], None, a["dst2"], at).then_inc(done("key_rows"), 16)
                pool.indirect_dma_start(srow_i[:, b, :], None, a["src2"], at).then_inc(done("src_rows"), 16)
                pool.indirect_dma_start(attr_g[:, b, :], None, a["attr"], at).then_inc(done("attr_rows"), 16)

            def l0_gather(k, h):
                pool.wait_ge(*count("l0_idx", k + 1))
                pool.sem_inc(done("pool_go"), 1)
                for u in range(h * L0H, h * L0H + L0H):
                    pool.indirect_dma_start(slots[:, u, 0:D], None, a["x_pad"],
                                            bass.IndirectOffsetOnAxis(ap=idx_a[:, u:u + 1], axis=0)).then_inc(gath[u], 16)

            def l0_scatter(k, h):
                pool.wait_ge(*count("l0_evac", k + 3))
                pool.wait_ge(*count("l0_sidx", k + 1))
                pool.sem_inc(done("pool_go"), 1)
                for u in range(L0H):
                    pool.indirect_dma_start(t_neigh[u], bass.IndirectOffsetOnAxis(ap=idx_b[:, h * L0H + u:h * L0H + u + 1], axis=0),
                                            msg[:, h * L0H + u, :], None, compute_op=ALU.add).then_inc(scat[u], 16)

            def l0_landed(k):
                for u in range(L0H):
                    pool.wait_ge(scat[u], 16 * k + 16)
                pool.sem_inc(done("l0_prev"), 1)

            pool.sem_inc(done("l0_prev"), 2)
            pool.wait_ge(*count("zero_tab", 16 * NACC * (NT + 1)))
            l0_gather(0, 0)
            l0_gather(1, 1)
            with pool.Fori(0, L0IT) as i:
                for h in range(2):
                    l0_scatter(2 * i + h, h)
                    l0_gather(2 * i + h + 2, h)
                    l0_landed(2 * i + h)
            for u in range(L0H):
                pool.wait_ge(scat[u], 16 * 2 * L0IT)
            for u in range(L0U):
                pool.wait_ge(gath[u], 16 * (L0IT + 1))
            pool.sem_inc(done("l0_scat_all"), 1)

            def scores(k):
                pool.wait_ge(*count(f"table{k}", 48))
                with pool.Fori(0, S // UN) as i:
                    for h in range(2):
                        pool.wait_ge(*count("idx2_ready", 52 * k + 2 * i + h + 1))
                        pool.sem_inc(done("pool_go"), 1)
                        for u in range(h * HU, h * HU + HU):
                            pool.indirect_dma_start(as_ring[:, u, :], None, t_as[k],
                                                    bass.IndirectOffsetOnAxis(ap=idx_a[:, u:u + 1], axis=0)).then_inc(gath2[u], 16)
                            into = hd_ring[:, u, :] if k == 0 else ad_ring[:, u, :]
                            pool.indirect_dma_start(into, None, t_ad[k],
                                                    bass.IndirectOffsetOnAxis(ap=idx_b[:, u:u + 1], axis=0)).then_inc(gath2[u], 16)

            def gathers(g, tab, w, ready, n):
                pool.wait_ge(*count(ready, n))
                with pool.Fori(0, S // UN) as i:
                    for h in range(2):
                        pool.wait_ge(idx_ready, 52 * g + 2 * i + h + 1)
                        pool.sem_inc(done("pool_go"), 1)
                        for u in range(h * HU, h * HU + HU):
                            pool.indirect_dma_start(slots[:, u, 0:w], None, tab,
                                                    bass.IndirectOffsetOnAxis(ap=idx_a[:, u:u + 1], axis=0)).then_inc(gath[u], 16)

            scores(0)
            gathers(0, table[0], D, "table0", 48)
            gathers(1, t_gcn, 64, "table_gcn", 16)
            for k in (1, 2):
                scores(k)
                gathers(k + 1, table[k], D, f"table{k}", 48)
            for l in range(3):
                gathers(4 + l, table[3 + l], D, f"table{3 + l}", 16)

        @block.tensor
        def _(pe):
            pe.sem_inc(step_mm, UN)
            pe.sem_inc(done("l0_pre"), 2)
            pe.sem_inc(done("enc_free"), 2)

            def turn(name, t_count, f_in, p_out, src, free_after):
                for t in range(t_count):
                    if t >= 4:
                        pe.wait_ge(*count(name + "_ev", t - 3))
                    for c in range(max(1, f_in // P)):
                        w = min(f_in, P)
                        last = pe.transpose(ps[0:w, t % 4, c * P:c * P + P], src(t, c), ident[:, :])
                    last.then_inc(done(name + "_tp"), 1)

            pe.wait_ge(*count("step_mask", EB))
            pe.wait_ge(*count("iota", 4))
            for b in range(EB):
                mm = pe.matmul(ps[:, 0, 0:S], ones[0:EQ, :], mask_t[:, b, :], start=(b == 0), stop=(b == EB - 1))
            for o in range(SB):
                for b in range(EB):
                    mm = pe.matmul(ps[0:SQ, 1, o:o + 1], mask_t[:, b, o * SQ:(o + 1) * SQ], ones[0:EQ, 0:1],
                                   start=(b == 0), stop=(b == EB - 1))
            mm.then_inc(done("te_ps"), 1)
            pe.wait_ge(*count("keys", 1))
            for n, t in enumerate((srow, key, drow)):
                for b in range(SB):
                    mm = pe.transpose(ps[:, 2 + n, b * SQ:(b + 1) * SQ], t[:, b, :], ident[0:SQ, 0:SQ])
            for n in range(2):
                for b in range(SB):
                    mm = pe.matmul(ps[0:8, 5 + n, b * SQ:(b + 1) * SQ], edge_keys[:, n, b, :], ident[0:SQ, 0:SQ], start=True, stop=True)
            mm.then_inc(done("steps_ps"), 1)

            pe.wait_ge(*count("pre", 1))

            def l0_half(k, h):
                pe.wait_ge(*count("l0_srcb", k + 1))
                for u in range(L0H):
                    mm = pe.matmul(ps[:, 2 + h, u * P:(u + 1) * P], src_b[:, h * L0H + u, :], ident[:, :], start=True, stop=True)
                mm.then_inc(done("l0_rowb"), 1)
                pe.wait_ge(*count("l0_eq", k + 1))
                pe.wait_ge(*count("l0_msg", k + 1))
                pe.wait_ge(*count("l0_evac", k + 1))
                for u in range(L0H):
                    mm = pe.matmul(ps[:, 4 + 2 * h + u // 2, (u % 2) * D:(u % 2) * D + D], eq[:, h * L0H + u, :],
                                   slots[:, h * L0H + u, 0:D], start=True, stop=True)
                mm.then_inc(done("l0_pre"), 1)

            with pe.Fori(0, L0IT) as i:
                l0_half(2 * i, 0)
                l0_half(2 * i + 1, 1)
            pe.wait_ge(*count("l0_evac", 2 * L0IT + 2))
            pe.wait_ge(*count("l0_summed", NACC - 1))
            turn("l0n", NT, D, P, lambda t, c: flat_a[:, t * D + c * P:t * D + c * P + P], 0)
            pe.wait_ge(*count("l0n_ev", NT))
            pe.wait_ge(*count("ld_x", 16))
            pe.wait_ge(*count("ld_w0", 16))
            for t in range(NT):
                if t >= 4:
                    pe.wait_ge(*count("l0_ev", t - 3))
                n0 = t * P
                for c in range(DC):
                    pe.matmul(ps[:, 4 + t % 4, 0:D], cols[:, c, n0:n0 + P], weights[:, c, :], start=(c == 0), stop=False)
                for c in range(DC):
                    mm = pe.matmul(ps[:, 4 + t % 4, 0:D], neigh_t[:, c, n0:n0 + P], weights[:, DC + c, :], start=False, stop=(c == DC - 1))
                mm.then_inc(done("l0_mm"), 1)

            def turn_resid(name, ready):
                pe.wait_ge(*count(ready, 1))
                turn(name, NT, D, P, lambda t, c: resid[:, t, c * P:c * P + P], 0)
                pe.wait_ge(*count(name + "_ev", NT))

            def node_rows(name, chunks, p, w, wait, n):
                pe.wait_ge(*count(wait, n))
                for t in range(NT):
                    if t >= 4:
                        pe.wait_ge(*count(name + "_ev", t - 3))
                    for j, c in enumerate(chunks):
                        mm = pe.matmul(ps[:, 4 + t % 4, 0:w], cols[0:p, j, t * P:(t + 1) * P], weights[0:p, c, 0:w],
                                       start=(j == 0), stop=(j == len(chunks) - 1))
                    mm.then_inc(done(name + "_mm"), 1)
                pe.wait_ge(*count(name + "_ev", NT))

            def max_segments(k, H):
                pe.wait_ge(*count(f"lrelu{k}", 1))
                for h in range(H):
                    if h >= 4:
                        pe.wait_ge(*count(f"scan_f{k}", h - 3))
                    for b in range(SB):
                        mm = pe.transpose(ps[0:SQ, h % 4, b * P:(b + 1) * P], alpha[:, b * SQ:(b + 1) * SQ, h], ident[:, :])
                    mm.then_inc(done(f"al_t{k}"), 1)
                for way, at in (("f", P - 1), ("r", 0)):
                    pe.wait_ge(*count(f"scan_{way}{k}", H))
                    for b in range(SB):
                        mm = pe.transpose(ps[0:H, 4, b * SQ:(b + 1) * SQ], segs[:, 0:H, b, at], ident[0:SQ, 0:SQ])
                    mm.then_inc(done(f"ends{k}"), 1)
                    pe.wait_ge(*count(f"carried{k}", 1 if way == "f" else 2))
                    for b in range(SB):
                        mm = pe.transpose(ps[0:SQ, 5, b * 8:b * 8 + H], carry2[0:H, b * SQ:(b + 1) * SQ], ident[0:H, 0:H])
                    mm.then_inc(done(f"carry_t{k}"), 1)
                pe.wait_ge(*count(f"segs_done{k}", 1))
                for h in range(H):
                    if h >= 4:
                        pe.wait_ge(*count(f"peak_ev{k}", h - 3))
                    for b in range(SB):
                        mm = pe.transpose(ps[:, h % 4, b * SQ:(b + 1) * SQ], segs[:, h, b, :], ident[0:SQ, 0:SQ])
                    mm.then_inc(done(f"peak_t{k}"), 1)
                pe.wait_ge(*count(f"peak_ev{k}", H))

            def add_up(g, w, weighted, transposed=False):
                with pe.Fori(0, S // UN) as i:
                    for u in range(UN):
                        h = u // HU
                        if u % HU == 0:
                            pe.wait_ge(oh_ready, 52 * g + 2 * i + h + 1)
                            if weighted is not None:
                                pe.wait_ge(msg_ready, 52 * weighted + 2 * i + h + 1)
                        if weighted is None:
                            pe.wait_ge(gath[u], gath_base(u, g) + 16 * i + 16)
                        pe.wait_ge(step_acc, S * g + UN * i + u + 1)
                        if transposed:
                            for c in range(DC):
                                mm = pe.matmul(ps[:, u % 4, c * P:c * P + P], slots[:, u, c * P:c * P + P], onehot[:, u, :],
                                               start=True, stop=True)
                        else:
                            mm = pe.matmul(ps[:, u % 4, 0:w], onehot[:, u, :], slots[:, u, 0:w], start=True, stop=True)
                        mm.then_inc(step_mm, 1)
                pe.wait_ge(step_acc, S * (g + 1) + 4)

            turn_resid("x1", "ln0")
            node_rows("l1", (0, 1), P, D, "ld_w1", 16)
            pe.wait_ge(*count("ld_attrw", 16))
            pe.wait_ge(*count("scores0", 1))
            with pe.Fori(0, S // UN) as i:
                for h in range(2):
                    pe.wait_ge(attr_in[h], 16 * i + 16)
                    pe.wait_ge(*count("enc_done", 2 * i + h + 1))
                    for j in range(HU):
                        mm = pe.matmul(ps[:, 4 * h + j // 2, (j % 2) * D:(j % 2) * D + D], attr_c[:, h, j, :], attr_w[:, :],
                                       start=True, stop=True)
                    mm.then_inc(done("enc_free"), 1)
            pe.wait_ge(*count("enc_done", 2 * (S // UN) + 2))
            max_segments(0, 8)
            add_up(0, D + 9, 0)
            turn_resid("x2", "ln1")
            node_rows("gcn", (2, 3), P, 64, "ld_gcn", 16)
            add_up(1, 64, None)
            pe.wait_ge(*count("gcn_out", 1))
            turn("gcnt", NT, 64, 64, lambda t, c: accum[:, t, 0:64], 0)
            pe.wait_ge(*count("gcnt_ev", NT))
            for k in (1, 2):
                pe.wait_ge(*count(f"ld_gat{k}", 16))
                node_rows(f"gat{k}", (0,) if k == 1 else (2, 3), 64 if k == 1 else P, D, f"gat_in{k}", 1)
                max_segments(k, 4)
                add_up(k + 1, D + 8, k)
                pe.wait_ge(*count(f"gat_out{k}", 1))
                turn(f"gatt{k}", NT, D, P, lambda t, c: accum[:, t, c * P:c * P + P], 0)
                pe.wait_ge(*count(f"gatt{k}_ev", NT))
            pe.wait_ge(*count("elu2", 1))
            turn("l2r", NT, D, P, lambda t, c: cols[:, c, t * P:(t + 1) * P], 0)
            pe.wait_ge(*count("l2r_ev", NT))
            turn_resid("x3", "ln2")
            for l in range(3):
                add_up(4 + l, D, None, transposed=True)
                pe.wait_ge(*count(f"ld_gin{l}", 32))

                def gin_mm(name, w0, src):
                    n = 0
                    for n0, w in NODE_CHUNKS:
                        for m in range(DC):
                            if n >= 4:
                                pe.wait_ge(*count(name + "_ev", n - 3))
                            for c in range(DC):
                                mm = pe.matmul(ps[:, 4 + n % 4, 0:w], weights[:, w0 + c, m * P:(m + 1) * P], src[:, c, n0:n0 + w],
                                               start=(c == 0), stop=(c == DC - 1))
                            mm.then_inc(done(name), 1)
                            n += 1
                    pe.wait_ge(*count(name + "_ev", n))

                gin_mm(f"gin_mm1_{l}", 0, accum_t)
                pe.wait_ge(*count(f"gin_z{l}", 1))
                if l < 2:
                    gin_mm(f"gin_mm2_{l}", 2, cols)
                    pe.wait_ge(*count(f"gin_h{l}", 1))
                    turn(f"gint{l}", NT, D, P, lambda t, c: accum_t[:, c, t * P:(t + 1) * P], 0)
                    pe.wait_ge(*count(f"gint{l}_ev", NT))
                else:
                    node_rows("gin_last", (2, 3), P, D, f"gin_z{l}", 1)

        @block.scalar
        def _(act):
            act.sem_inc(done("l0_evac"), 2)
            act.sem_inc(done("enc_done"), 2)

            def l0_index(k, h):
                act.wait_ge(*count("l0_pre", k + 1))
                act.activation(idx_a[:, h * L0H:h * L0H + L0H], dst_t[:, bass.ds(k * L0H, L0H)], ACT.Copy).then_inc(done("l0_idx"), 1)

            def l0_out_of_psum(k, h):
                act.wait_ge(*count("l0_pre", k + 3))
                act.wait_ge(*count("l0_prev", k + 1))
                act.activation(msg[:, h * L0H:h * L0H + L0H, :].rearrange("p u d -> p (u d)"),
                               ps[:, 4 + 2 * h:6 + 2 * h, :].rearrange("p b d -> p (b d)"), ACT.Copy).then_inc(done("l0_evac"), 1)

            act.wait_ge(*count("ld_dst", 16))
            l0_index(0, 0)
            l0_index(1, 1)
            with act.Fori(0, L0IT) as i:
                for h in range(2):
                    l0_out_of_psum(2 * i + h, h)
                    l0_index(2 * i + h + 2, h)

            def turned(name, n_tiles, p, c, dst):
                for t in range(n_tiles):
                    act.wait_ge(*count(name + "_tp", t + 1))
                    act.activation(dst[0:p, 0:c, t * P:(t + 1) * P], ps[0:p, t % 4, 0:c * P].rearrange("p (c n) -> p c n", c=c),
                                   ACT.Copy).then_inc(done(name + "_ev"), 1)

            def root(name):
                act.wait_ge(*count("var_" + name, 1))
                src, dst = roots[name]
                act.activation(dst, src, ACT.Sqrt).then_inc(done("std_" + name), 1)

            def rows_out(name, w, scale=None):
                for t in range(NT):
                    act.wait_ge(*count(name + "_mm", t + 1))
                    act.activation(hrows[:, t, 0:w], ps[:, 4 + t % 4, 0:w], ACT.Copy,
                                   scale=1.0 if scale is None else scale(t)).then_inc(done(name + "_ev"), 1)

            def score_indices(k):
                with act.Fori(0, S // UN) as i:
                    for h in range(2):
                        half = slice(h * HU, h * HU + HU)
                        now = bass.ds(i * UN + h * HU, HU)
                        act.wait_ge(*count("sc_used", 52 * k + 2 * i + h + 1))
                        act.activation(idx_a[:, half], src_x[:, now], ACT.Copy)
                        act.activation(idx_b[:, half], dst_x[:, now], ACT.Copy).then_inc(done("idx2_ready"), 1)
                        if k == 0:
                            act.wait_ge(*count("enc_free", 2 * i + h + 3))
                            act.activation(enc[:, half, :], ps[:, 4 * h:4 * h + 4, :].rearrange("p b (j d) -> p (b j) d", j=2),
                                           ACT.Relu).then_inc(done("enc_done"), 1)

            def indices(g):
                with act.Fori(0, S // UN) as i:
                    for h in range(2):
                        act.wait_ge(step_mm, S * g + UN * i + HU * h + HU)
                        act.activation(idx_a[:, h * HU:h * HU + HU], src_x[:, bass.ds(i * UN + h * HU, HU)],
                                       ACT.Copy).then_inc(idx_ready, 1)

            def weights_of(k, H):
                for h in range(H):
                    act.wait_ge(*count(f"peak_t{k}", h + 1))
                    act.activation(peak[:, :, h], ps[:, h % 4, 0:S], ACT.Copy).then_inc(done(f"peak_ev{k}"), 1)
                act.wait_ge(*count(f"alpha_sub{k}", 1))
                act.activation(alpha[:, :, 0:H], alpha[:, :, 0:H], ACT.Exp).then_inc(done(f"exp{k}"), 1)

            turned("l0n", NT, P, 2, neigh_t)
            root("ln0")
            turned("x1", NT, P, 2, cols)
            rows_out("l1", D)
            score_indices(0)
            weights_of(0, 8)
            indices(0)
            root("deg")
            root("ln1")
            turned("x2", NT, P, 2, cols)
            act.wait_ge(*count("dinv", 1))
            rows_out("gcn", 64, lambda t: deg[:, t, 1:2])
            indices(1)
            turned("gcnt", NT, 64, 1, cols)
            root("bn_gcn")
            act.wait_ge(*count("bnsc_gcn", 1))
            act.activation(cols[0:64, 0, :], cols[0:64, 0, :], ACT.Identity, bias=bnsc[0:64, 0, 1:2],
                           scale=bnsc[0:64, 0, 0:1]).then_inc(done("gat_in1"), 1)
            for k in (1, 2):
                rows_out(f"gat{k}", D)
                score_indices(k)
                weights_of(k, 4)
                indices(k + 1)
                act.wait_ge(*count(f"self_sub{k}", 1))
                act.activation(small[:, :, 0:4], small[:, :, 0:4], ACT.Exp).then_inc(done(f"self_w{k}"), 1)
                turned(f"gatt{k}", NT, P, 2, cols)
                root(f"bn_gat{k}")
                for c in range(DC):
                    act.wait_ge(*count(f"elu_neg{k}", c + 1))
                    act.activation(accum_t[:, c, :], accum_t[:, c, :], ACT.Exp).then_inc(done(f"elu_exp{k}"), 1)
            root("ln2")
            turned("x3", NT, P, 2, accum_t)

            def biased(name, dst, bias):
                n = 0
                for n0, w in NODE_CHUNKS:
                    for m in range(DC):
                        act.wait_ge(*count(name, n + 1))
                        act.activation(dst[:, m, n0:n0 + w], ps[:, 4 + n % 4, 0:w], ACT.Identity,
                                       bias=vec(bias, m)).then_inc(done(name + "_ev"), 1)
                        n += 1

            def relu_scaled(name, buf, ready):
                act.wait_ge(*count("bnsc_" + name, 1))
                for c in range(DC):
                    last = act.activation(buf[:, c, :], buf[:, c, :], ACT.Relu, bias=bnsc[:, c, 1:2], scale=bnsc[:, c, 0:1])
                last.then_inc(done(ready), 1)

            for l in range(3):
                indices(4 + l)
                biased(f"gin_mm1_{l}", cols, f"L3_gnn_l{l}_b1")
                root(f"bn_gin{l}a")
                relu_scaled(f"gin{l}a", cols, f"gin_z{l}")
                if l < 2:
                    biased(f"gin_mm2_{l}", accum_t, f"L3_gnn_l{l}_b2")
                    root(f"bn_gin{l}b")
                    relu_scaled(f"gin{l}b", accum_t, f"gin_h{l}")
                    for t in range(NT):
                        act.wait_ge(*count(f"gint{l}_tp", t + 1))
                        act.activation(hrows[:, t, 0:D], ps[:, t % 4, 0:D], ACT.Copy).then_inc(done(f"gint{l}_ev"), 1)
            root("ln3")

        @block.vector
        def _(dve):
            chain = [0]

            def link(ins):
                chain[0] += 1
                ins.then_inc(dv, 1)
                dve.wait_ge(dv, chain[0])

            dve.sem_inc(step_acc, 4)
            dve.sem_inc(done("sc_used"), 2)
            tn_regs = [dve.alloc_register(f"tn{u}") for u in range(HU)]

            dve.wait_ge(*count("iota", 4))
            link(dve.tensor_scalar(ident[:, :], iota[:, 0:P], iota_p[:, :], None, ALU.is_equal))
            link(dve.tensor_scalar(before[:, :], iota[:, 0:P], iota_p[:, :], None, ALU.is_lt))
            dve.wait_ge(*count("ld_last", 16))
            link(dve.tensor_scalar(te_last_i[:, :, :], te_last_i[:, :, :], 7, None, ALU.logical_shift_right))
            link(dve.tensor_copy(te_last[:, :], te_last_i[:, :, 0]))
            for b in range(EB):
                link(dve.tensor_scalar(te_last[:, b:b + 1], te_last[:, b:b + 1], iota_p[0:EQ, :], float(EQ * b + 1), ALU.add, ALU.add))
                dve.tensor_scalar(mask_t[:, b, :], iota[0:EQ, :], te_last[:, b:b + 1], None, ALU.is_ge).then_inc(done("step_mask"), 1)
            dve.wait_ge(*count("te_ps", 1))
            dve.tensor_copy(te_i[:, :], ps[0:SQ, 1, 0:SB]).then_inc(done("te"), 1)
            link(dve.tensor_tensor(tn_i[:, :], iota[:, :], ps[:, 0, 0:S], ALU.subtract))
            for b in range(SB):
                link(dve.tensor_scalar(pre4[0:SQ, b:b + 1], ps[0:SQ, 1, b:b + 1], iota_p[0:SQ, :], float(-SQ * b), ALU.subtract, ALU.add))
            link(dve.tensor_scalar(pre4[0:SQ, :], pre4[0:SQ, :], float(P), None, ALU.mult))
            dve.wait_ge(*count("key_rows", 16 * SB))
            dve.wait_ge(*count("src_rows", 16 * SB))
            link(dve.tensor_copy(key, key_i))
            link(dve.tensor_copy(srow, srow_i))
            for b in range(SB):
                link(dve.tensor_scalar(drow[:, b, :], key[:, b, :], pre4[0:SQ, b:b + 1], None, ALU.add))
            link(dve.tensor_copy(edge_keys[:, 0, :, :], key[:, :, 0:1].to_broadcast([SQ, SB, 8])))
            dve.tensor_copy(edge_keys[:, 1, :, :], key[:, :, P - 1:P].to_broadcast([SQ, SB, 8])).then_inc(done("keys"), 1)
            def barrier_of(out):
                link(dve.tensor_scalar(out, out, 1.0, BIG, ALU.subtract, ALU.mult))

            link(dve.memset(reset_f[:, :, 0:1], 0.0))
            link(dve.memset(reset_r[:, :, P - 1:P], 0.0))
            link(dve.tensor_tensor(reset_f[:, :, 1:P], key[:, :, 1:P], key[:, :, 0:P - 1], ALU.is_equal))
            barrier_of(reset_f[:, :, 1:P])
            link(dve.tensor_copy(reset_r[:, :, 0:P - 1], reset_f[:, :, 1:P]))
            for b in range(SB):
                link(dve.tensor_scalar(with_first[:, b, :], key[:, b, :], key[:, b, 0:1], None, ALU.is_equal))
                link(dve.tensor_scalar(with_last[:, b, :], key[:, b, :], key[:, b, P - 1:P], None, ALU.is_equal))
            barrier_of(with_first[:, :, :])
            barrier_of(with_last[:, :, :])
            dve.wait_ge(*count("steps_ps", 1))
            link(dve.tensor_copy(src_x[:, :], ps[:, 2, 0:S]))
            link(dve.tensor_copy(dst_x[:, :], ps[:, 3, 0:S]))
            link(dve.tensor_copy(drel[:, :], ps[:, 4, 0:S]))
            link(dve.tensor_copy(carry[:, 0:S], ps[0:8, 5, 0:S]))
            link(dve.tensor_tensor(carry2[:, :], carry[:, 0:S], ps[0:8, 6, 0:S], ALU.is_equal))
            link(dve.memset(carry_ok[:, :], 0.0))
            link(dve.tensor_tensor(carry_ok[:, 1:S], carry[:, 1:S], ps[0:8, 6, 0:S - 1], ALU.is_equal))
            link(dve.tensor_tensor(through_f[:, :], carry_ok[:, 0:S], carry2[:, :], ALU.mult))
            link(dve.tensor_tensor(through_r[:, :], carry_ok[:, 1:S + 1], carry2[:, :], ALU.mult))
            barrier_of(carry_ok[:, :])
            barrier_of(through_f[:, :])
            barrier_of(through_r[:, :])
            dve.wait_ge(*count("ld_src", 16))
            dve.wait_ge(*count("ld_ew", 16))
            link(dve.tensor_copy(src_f, src_i0))
            dve.tensor_scalar(trash_p, iota_p[:, :], float(TRASH), None, ALU.add).then_inc(done("pre"), 1)
            dve.wait_ge(*count("pre", 1))

            def l0_half(k, h):
                half = slice(h * L0H, h * L0H + L0H)
                now = bass.ds(k * L0H, L0H)
                dve.wait_ge(*count("l0_pre", k + 1))
                dve.tensor_copy(src_b[:, half, :], src_f[:, now].unsqueeze(2).to_broadcast([P, L0H, P])).then_inc(done("l0_srcb"), 1)
                dve.wait_ge(*count("l0_srcb", k + 1))
                dve.wait_ge(*count("l0_rowb", k + 1))
                dve.tensor_tensor(eq[:, half, :], ps[:, 2 + h, :].rearrange("p (u e) -> p u e", u=L0H), src_b[:, half, :],
                                  ALU.is_equal).then_inc(done("l0_eq"), 1)
                dve.wait_ge(*count("l0_eq", k + 1))
                v = tmp[:, 0:L0H * P].rearrange("p (u e) -> p u e", u=L0H)
                dve.tensor_tensor(v, eq[:, half, :], before[:, :].unsqueeze(1).to_broadcast([P, L0H, P]), ALU.mult).then_inc(done("l0_dv"), 1)
                dve.wait_ge(*count("l0_dv", 4 * k + 1))
                c0 = h * L0H
                dve.tensor_reduce(cnt[:, c0:c0 + L0H], v, AX.X, ALU.add).then_inc(done("l0_dv"), 1)
                dve.tensor_scalar(l0d[:, c0:c0 + L0H], src_f[:, now], -1.0, trash_p, ALU.mult, ALU.add).then_inc(done("l0_dv"), 1)
                dve.wait_ge(*count("l0_dv", 4 * k + 3))
                dve.scalar_tensor_tensor(l0m[:, c0:c0 + L0H], cnt[:, c0:c0 + L0H], 1.0, l0d[:, c0:c0 + L0H], ALU.min,
                                         ALU.mult).then_inc(done("l0_dv"), 1)
                dve.wait_ge(*count("l0_dv", 4 * k + 4))
                dve.wait_ge(*count("l0_prev", k + 1))
                dve.tensor_tensor(idx_b[:, half], l0m[:, c0:c0 + L0H], src_f[:, now], ALU.add).then_inc(done("l0_sidx"), 1)
                for u in range(h * L0H, h * L0H + L0H):
                    dve.wait_ge(gath[u], 8 * (k - h) + 16)
                dve.tensor_tensor(slots[:, half, 0:D], slots[:, half, 0:D], ew_t[:, now].unsqueeze(2).to_broadcast([P, L0H, D]),
                                  ALU.mult).then_inc(done("l0_msg"), 1)

            with dve.Fori(0, L0IT) as i:
                l0_half(2 * i, 0)
                l0_half(2 * i + 1, 1)

            sums = flat_a[:, 0:NT * D]
            for k in range(1, NACC):
                dve.wait_ge(*count(f"ld_neigh{k}", 16))
                if k == 1:
                    dve.wait_ge(*count("ld_neigh0", 16))
                else:
                    dve.wait_ge(*count("l0_summed", k - 1))
                dve.tensor_tensor(sums, sums, flat_h[:, 0:NT * D], ALU.add).then_inc(done("l0_summed"), 1)
            dve.wait_ge(*count("ld_xrow", 16))
            dve.wait_ge(*count("ld_rows", 16))
            all_rows = lambda v, w=D: v.unsqueeze(1).to_broadcast([P, NT, w])
            link(dve.tensor_tensor(resid[:, :, :], resid[:, :, :], all_rows(row("L0_gnn_bias")), ALU.add))
            for t in range(NT):
                dve.wait_ge(*count("l0_mm", t + 1))
                dve.tensor_tensor(resid[:, t, :], resid[:, t, :], ps[:, 4 + t % 4, 0:D], ALU.add).then_inc(done("l0_ev"), 1)
            dve.wait_ge(*count("l0_ev", NT))

            def layer_norm(k):
                for t in range(NT):
                    last = dve.bn_stats(stats[:, t, 0:6], resid[:, t, :])
                link(last)
                for t in range(NT):
                    last = dve.bn_aggr(mv[:, t, :], stats[:, t, 0:6])
                link(last)
                dve.tensor_scalar(small[:, :, 0], mv[:, :, 1], LN_EPS, None, ALU.add).then_inc(done(f"var_ln{k}"), 1)
                dve.wait_ge(*count(f"std_ln{k}", 1))
                link(dve.reciprocal(small[:, :, 2], small[:, :, 1]))
                for t in range(NT):
                    last = dve.tensor_scalar(resid[:, t, :], resid[:, t, :], mv[:, t, 0:1], small[:, t, 2:3], ALU.subtract, ALU.mult)
                last.then_inc(done(f"ln{k}"), 1)

            def node_scores(k, H, src_row, dst_row, name):
                dve.wait_ge(*count(name, NT))
                prod = flat_a[:, 0:NT * D].rearrange("p (t d) -> p t d", t=NT)
                for n, r in enumerate((src_row, dst_row)):
                    link(dve.tensor_tensor(prod, hrows[:, :, 0:D], all_rows(row(r)), ALU.mult))
                    link(dve.tensor_reduce(node_s[:, :, 8 * n:8 * n + H], prod.rearrange("p t (h d) -> p t h d", h=H), AX.X, ALU.add))
                if H == 8:
                    dve.tensor_copy(hrows[:, :, D:D + 16], node_s[:, :, :]).then_inc(done(f"scores{k}"), 1)
                else:
                    link(dve.tensor_tensor(node_s[:, :, 12:16], node_s[:, :, 0:4], node_s[:, :, 8:12], ALU.add))
                    dve.scalar_tensor_tensor(node_s[:, :, 12:16], node_s[:, :, 12:16], 0.2, node_s[:, :, 12:16], ALU.mult,
                                             ALU.max).then_inc(done(f"scores{k}"), 1)

            def edge_scores(k):
                with dve.Fori(0, S // UN) as i:
                    for h in range(2):
                        half = slice(h * HU, h * HU + HU)
                        now = bass.ds(i * UN + h * HU, HU)
                        for u in range(h * HU, h * HU + HU):
                            dve.wait_ge(gath2[u], 32 * ((S // UN) * k + i) + 32)
                        if k == 0:
                            dve.wait_ge(*count("enc_done", 2 * i + h + 3))
                            dve.tensor_tensor(enc[:, half, :], enc[:, half, :], hd_ring[:, half, 0:D], ALU.mult).then_inc(done("sc_dv"), 1)
                            dve.wait_ge(*count("sc_dv", 6 * i + 3 * h + 1))
                            v = peak[:, now, :]
                            dve.tensor_reduce(v, enc[:, half, :].rearrange("p u (h d) -> p u h d", h=8), AX.X, ALU.add).then_inc(done("sc_dv"), 1)
                            dve.wait_ge(*count("sc_dv", 6 * i + 3 * h + 2))
                            dve.tensor_tensor(v, v, hd_ring[:, half, D + 8:D + 16], ALU.add).then_inc(done("sc_dv"), 1)
                            dve.wait_ge(*count("sc_dv", 6 * i + 3 * h + 3))
                            dve.tensor_tensor(alpha[:, now, :], v, as_ring[:, half, :], ALU.add).then_inc(done("sc_used"), 1)
                        else:
                            dve.tensor_copy(peak[:, now, 4:8], ad_ring[:, half, 4:8])
                            dve.tensor_tensor(alpha[:, now, 0:4], as_ring[:, half, 0:4], ad_ring[:, half, 0:4], ALU.add).then_inc(done("sc_used"), 1)
                dve.wait_ge(*count("sc_used", 52 * (k + 1) + 2))

            def softmax(k, H):
                al = alpha[:, :, 0:H]
                dve.scalar_tensor_tensor(al, al, 0.2, al, ALU.mult, ALU.max).then_inc(done(f"lrelu{k}"), 1)
                dve.wait_ge(*count(f"lrelu{k}", 1))
                for h in range(H):
                    dve.wait_ge(*count(f"al_t{k}", h + 1))
                    for b in range(SB):
                        last = dve.tensor_tensor_scan(segs[:, h, b, :], reset_f[:, b, :], ps[0:SQ, h % 4, b * P:(b + 1) * P], -BIG, ALU.add, ALU.max)
                    last.then_inc(done(f"scan_f{k}"), 1)
                dve.wait_ge(*count(f"scan_f{k}", H))
                for way in (0, 1):
                    dve.wait_ge(*count(f"ends{k}", way + 1))
                    if way == 0:
                        link(dve.memset(carry[:, 0:1], -BIG))
                        link(dve.tensor_tensor_scan(carry[0:H, 1:S + 1], through_f[0:H, :], ps[0:H, 4, 0:S], -BIG, ALU.add, ALU.max))
                        dve.tensor_tensor(carry2[0:H, :], carry[0:H, 0:S], carry_ok[0:H, 0:S], ALU.add).then_inc(done(f"carried{k}"), 1)
                    else:
                        link(dve.memset(carry[:, S:S + 1], -BIG))
                        link(dve.tensor_tensor_scan(carry[0:H, S - 1::-1], through_r[0:H, ::-1], ps[0:H, 4, S - 1::-1], -BIG, ALU.add, ALU.max))
                        dve.tensor_tensor(carry2[0:H, :], carry[0:H, 1:S + 1], carry_ok[0:H, 1:S + 1], ALU.add).then_inc(done(f"carried{k}"), 1)
                    dve.wait_ge(*count(f"carry_t{k}", way + 1))
                    link(dve.tensor_copy(carry_c[:, :, 0:H], ps[0:SQ, 5, 0:8 * SB].rearrange("p (b h) -> p b h", b=SB)[:, :, 0:H]))
                    same = with_first if way == 0 else with_last
                    for h in range(H):
                        for b in range(SB):
                            last = dve.scalar_tensor_tensor(segs[:, h, b, :], same[:, b, :], carry_c[:, b, h:h + 1], segs[:, h, b, :], ALU.add, ALU.max)
                    if way == 1:
                        last.then_inc(done(f"segs_done{k}"), 1)
                        break
                    link(last)
                    for h in range(H):
                        for b in range(SB):
                            last = dve.tensor_tensor_scan(segs[:, h, b, ::-1], reset_r[:, b, ::-1], segs[:, h, b, ::-1], -BIG, ALU.add, ALU.max)
                    last.then_inc(done(f"scan_r{k}"), H)
                    dve.wait_ge(*count(f"scan_r{k}", H))
                dve.wait_ge(*count(f"peak_ev{k}", H))
                if H == 4:
                    link(dve.tensor_tensor(peak[:, :, 0:4], peak[:, :, 0:4], peak[:, :, 4:8], ALU.max))
                dve.tensor_tensor(al, al, peak[:, :, 0:H], ALU.subtract).then_inc(done(f"alpha_sub{k}"), 1)
                dve.wait_ge(*count(f"exp{k}", 1))
                if H == 4:
                    link(dve.tensor_tensor(peak[:, :, 4:8], al, peak[:, :, 0:4], ALU.mult))
                link(dve.memset(accum[:, :, :], 0.0))

            def add_up(g, w, weighted, H=8, transposed=False):
                with dve.Fori(0, S // UN) as i:
                    for h in range(2):
                        half = slice(h * HU, h * HU + HU)
                        now = bass.ds(i * UN + h * HU, HU)
                        dve.load(tn_regs, tn_i[0:1, now])
                        dve.wait_ge(step_mm, S * g + UN * i + HU * h + HU)
                        dve.tensor_tensor(onehot[:, half, :], iota[:, 0:P].unsqueeze(1).to_broadcast([P, HU, P]),
                                          drel[:, now].unsqueeze(2).to_broadcast([P, HU, P]), ALU.is_equal).then_inc(oh_ready, 1)
                        if weighted is not None:
                            for u in range(h * HU, h * HU + HU):
                                dve.wait_ge(gath[u], gath_base(u, g) + 16 * i + 16)
                            v = slots[:, half, 0:D].rearrange("p u (h d) -> p u h d", h=H)
                            dve.tensor_tensor(v, v, alpha[:, now, 0:H].unsqueeze(3).to_broadcast([P, HU, H, D // H]), ALU.mult)
                            last = dve.tensor_copy(slots[:, half, D:D + H], alpha[:, now, 0:H])
                            if H == 4:
                                last = dve.tensor_copy(slots[:, half, D + 4:D + 8], peak[:, now, 4:8])
                            last.then_inc(msg_ready, 1)
                        for u in range(HU):
                            at = dve.snap(tn_regs[u], min_val=0, max_val=NT - 1)
                            dve.wait_ge(step_mm, S * g + UN * i + HU * h + u + UN + 1)
                            dve.wait_ge(step_acc, S * g + UN * i + HU * h + u + 4)
                            bank = ps[:, (h * HU + u) % 4, 0:w]
                            if transposed:
                                to = accum_t[:, :, bass.ds(at * P, P)]
                                bank = bank.rearrange("p (c n) -> p c n", c=DC)
                            else:
                                to = accum[:, bass.ds(at, 1), 0:w]
                                bank = bank.unsqueeze(1)
                            dve.tensor_tensor(to, to, bank, ALU.add).then_inc(step_acc, 1)
                dve.wait_ge(step_acc, S * (g + 1) + 4)

            heads = lambda v, H, w: v.unsqueeze(3).to_broadcast([P, NT, H, w])

            def batch_norm(name, buf, p, n_c, g, be):
                for c in range(n_c):
                    for j, (n0, w) in enumerate(BN_CHUNKS):
                        last = dve.bn_stats(bnst[0:p, c, j, :], buf[0:p, c, n0:n0 + w])
                link(last)
                for c in range(n_c):
                    last = dve.bn_aggr(bnmv[0:p, c, :], bnst[0:p, c, :, :].rearrange("p j s -> p (j s)"))
                link(last)
                dve.tensor_scalar(bnsc[0:p, 0:n_c, 2], bnmv[0:p, 0:n_c, 1], BN_EPS, None, ALU.add).then_inc(done(f"var_bn_{name}"), 1)
                dve.wait_ge(*count(f"std_bn_{name}", 1))
                link(dve.reciprocal(bnsc[0:p, 0:n_c, 2], bnsc[0:p, 0:n_c, 3]))
                gi, bi = COL[g], COL[be]
                link(dve.tensor_tensor(bnsc[0:p, 0:n_c, 0], bnsc[0:p, 0:n_c, 2], vecs[0:p, gi, 0:n_c], ALU.mult))
                link(dve.tensor_tensor(bnsc[0:p, 0:n_c, 2], bnsc[0:p, 0:n_c, 0], bnmv[0:p, 0:n_c, 0], ALU.mult))
                dve.tensor_tensor(bnsc[0:p, 0:n_c, 1], vecs[0:p, bi, 0:n_c], bnsc[0:p, 0:n_c, 2], ALU.subtract).then_inc(done(f"bnsc_{name}"), 1)
                dve.wait_ge(*count(f"bnsc_{name}", 1))

            layer_norm(0)
            node_scores(0, 8, "L1_gnn_a_src", "L1_gnn_a_dst", "l1_ev")
            edge_scores(0)
            softmax(0, 8)
            link(dve.memset(slots[:, :, D + 8:D + 9], 1.0))
            add_up(0, D + 9, 0, 8)
            link(dve.tensor_scalar(small[:, :, :], accum[:, :, D:D + 8], 1e-10, None, ALU.max))
            link(dve.reciprocal(small[:, :, :], small[:, :, :]))
            acc4 = accum[:, :, 0:D].rearrange("p t (h d) -> p t h d", h=8)
            link(dve.tensor_tensor(acc4, acc4, heads(small[:, :, :], 8, 32), ALU.mult))
            link(dve.tensor_tensor(accum[:, :, 0:D], accum[:, :, 0:D], all_rows(row("L1_gnn_bias")), ALU.add))
            link(dve.tensor_tensor(resid[:, :, :], resid[:, :, :], accum[:, :, 0:D], ALU.add))
            link(dve.tensor_scalar(deg[:, :, 0], accum[:, :, D + 8], 1.0, 1.0, ALU.add, ALU.max))
            dve.sem_inc(done("var_deg"), 1)
            layer_norm(1)
            dve.wait_ge(*count("std_deg", 1))
            dve.reciprocal(deg[:, :, 1], deg[:, :, 1]).then_inc(done("dinv"), 1)
            link(dve.memset(accum[:, :, :], 0.0))
            add_up(1, 64, None)
            g64 = accum[:, :, 0:64]
            link(dve.tensor_tensor(g64, g64, hrows[:, :, 0:64], ALU.add))
            link(dve.tensor_tensor(g64, g64, deg[:, :, 1:2].to_broadcast([P, NT, 64]), ALU.mult))
            link(dve.tensor_tensor(g64, g64, all_rows(row("L2_gnn_b_gcn", 64), 64), ALU.add))
            dve.tensor_scalar(g64, g64, 0.0, None, ALU.max).then_inc(done("gcn_out"), 1)
            dve.wait_ge(*count("gcnt_ev", NT))
            batch_norm("gcn", cols, 64, 1, "L2_gnn_g0", "L2_gnn_beta0")
            for k in (1, 2):
                node_scores(k, 4, f"L2_gnn_a_src{k}", f"L2_gnn_a_dst{k}", f"gat{k}_ev")
                edge_scores(k)
                softmax(k, 4)
                add_up(k + 1, D + 8, k, 4)
                self_s, m = node_s[:, :, 12:16], small[:, :, 4:8]
                link(dve.tensor_scalar(small[:, :, 0:4], accum[:, :, D:D + 4], 1e-30, None, ALU.max))
                link(dve.reciprocal(small[:, :, 0:4], small[:, :, 0:4]))
                link(dve.tensor_tensor(m, accum[:, :, D + 4:D + 8], small[:, :, 0:4], ALU.mult))
                link(dve.tensor_scalar(small[:, :, 0:4], accum[:, :, D:D + 4], 0.0, None, ALU.is_gt))
                link(dve.tensor_tensor(m, m, self_s, ALU.subtract))
                link(dve.tensor_tensor(m, m, small[:, :, 0:4], ALU.mult))
                link(dve.tensor_scalar(small[:, :, 0:4], m, 0.0, -1.0, ALU.max, ALU.mult))
                dve.sem_inc(done(f"self_sub{k}"), 1)
                dve.wait_ge(*count(f"self_w{k}", 1))
                h4 = hrows[:, :, 0:D].rearrange("p t (h d) -> p t h d", h=4)
                a4 = accum[:, :, 0:D].rearrange("p t (h d) -> p t h d", h=4)
                link(dve.tensor_tensor(h4, h4, heads(small[:, :, 0:4], 4, 64), ALU.mult))
                link(dve.tensor_tensor(a4, a4, h4, ALU.add))
                link(dve.tensor_tensor(m, accum[:, :, D:D + 4], small[:, :, 0:4], ALU.add))
                link(dve.reciprocal(m, m))
                link(dve.tensor_tensor(a4, a4, heads(m, 4, 64), ALU.mult))
                dve.tensor_tensor(accum[:, :, 0:D], accum[:, :, 0:D], all_rows(row(f"L2_gnn_b{k}")), ALU.add).then_inc(done(f"gat_out{k}"), 1)
                dve.wait_ge(*count(f"gatt{k}_ev", NT))
                batch_norm(f"gat{k}", cols, P, 2, f"L2_gnn_g{k}", f"L2_gnn_beta{k}")
                for c in range(DC):
                    link(dve.tensor_scalar(cols[:, c, :], cols[:, c, :], bnsc[:, c, 0:1], bnsc[:, c, 1:2], ALU.mult, ALU.add))
                    dve.tensor_scalar(accum_t[:, c, :], cols[:, c, :], 0.0, None, ALU.min).then_inc(done(f"elu_neg{k}"), 1)
                for c in range(DC):
                    link(dve.tensor_scalar(cols[:, c, :], cols[:, c, :], 0.0, None, ALU.max))
                    dve.wait_ge(*count(f"elu_exp{k}", c + 1))
                    link(dve.scalar_tensor_tensor(cols[:, c, :], accum_t[:, c, :], -1.0, cols[:, c, :], ALU.add, ALU.add))
                dve.sem_inc(done("gat_in2" if k == 1 else "elu2"), 1)
            for t in range(NT):
                dve.wait_ge(*count("l2r_tp", t + 1))
                dve.tensor_tensor(resid[:, t, :], resid[:, t, :], ps[:, t % 4, 0:D], ALU.add).then_inc(done("l2r_ev"), 1)
            dve.wait_ge(*count("l2r_ev", NT))
            layer_norm(2)
            dve.wait_ge(*count("x3_ev", NT))
            for l in range(3):
                add_up(4 + l, D, None, transposed=True)
                dve.wait_ge(*count(f"gin_mm1_{l}_ev", 2 * len(NODE_CHUNKS)))
                batch_norm(f"gin{l}a", cols, P, 2, f"L3_gnn_l{l}_g1", f"L3_gnn_l{l}_be1")
                if l < 2:
                    dve.wait_ge(*count(f"gin_mm2_{l}_ev", 2 * len(NODE_CHUNKS)))
                    batch_norm(f"gin{l}b", accum_t, P, 2, f"L3_gnn_l{l}_g2", f"L3_gnn_l{l}_be2")
                    dve.wait_ge(*count(f"gin_h{l}", 1))
            link(dve.tensor_tensor(resid[:, :, :], resid[:, :, :], all_rows(row("L3_gnn_l2_b2")), ALU.add))
            for t in range(NT):
                dve.wait_ge(*count("gin_last_mm", t + 1))
                dve.tensor_tensor(resid[:, t, :], resid[:, t, :], ps[:, 4 + t % 4, 0:D], ALU.add).then_inc(done("gin_last_ev"), 1)
            dve.wait_ge(*count("gin_last_ev", NT))
            layer_norm(3)


def kernel(**inputs):
    import numpy as np
    import concourse.bacc as bacc
    from concourse.bass_utils import run_bass_kernel_spmd

    v = {k: np.ascontiguousarray(x) for k, x in inputs.items()}
    arrays = {}

    def tiles(x, fill, n):
        out = np.full((n * P,) + x.shape[1:], fill, x.dtype)
        out[:E] = x
        return out.reshape((n, P) + x.shape[1:])

    src, dst = v["src"].astype(np.int32), v["dst"].astype(np.int32)
    arrays["src2"] = tiles(src, NP - 1, ET)
    arrays["dst2"] = tiles(dst, NP - 1, ET)
    arrays["src_t"] = np.ascontiguousarray(tiles(src, NP - 1, ETX).T)
    arrays["dst_t"] = np.ascontiguousarray(tiles(dst, NP - 1, ETX).T)
    arrays["ew_t"] = np.ascontiguousarray(tiles(v["edge_weight"], 0, ETX).T)
    attr = np.ones((ET, 4, P), np.float32)
    attr[:, 0:3, :] = tiles(v["edge_attr_3"], 0, ET).transpose(0, 2, 1)
    arrays["attr"] = attr.reshape(ET, 4 * P)
    arrays["attr_w"] = np.concatenate([v["L1_gnn_edge_W"].T, v["L1_gnn_edge_b"][None]], 0)
    xp = np.zeros((NP, D), np.float32)
    xp[:N] = v["x"]
    arrays["x_pad"] = xp
    arrays["x_cols"] = np.ascontiguousarray(xp.T)
    rows = np.zeros((len(ROWS), D), np.float32)
    for i, name in enumerate(ROWS):
        rows[i, :v[name].size] = v[name].reshape(-1)
    arrays["rows"] = np.ascontiguousarray(np.broadcast_to(rows, (P,) + rows.shape))
    vecs = np.zeros((P, len(COLS), 2), np.float32)
    for i, name in enumerate(COLS):
        f = v[name].reshape(-1, P).T if v[name].size == D else v[name].reshape(-1, 1)
        vecs[:f.shape[0], i, :f.shape[1]] = f
    arrays["vecs"] = vecs
    arrays["L1_gnn_W"] = np.ascontiguousarray(v["L1_gnn_W"].T)
    for name in ["L0_gnn_weight", "L2_gnn_W_gcn", "L2_gnn_W1", "L2_gnn_W2"] + [f"L3_gnn_l{l}_w{j}" for l in range(3) for j in (1, 2)]:
        arrays[name] = v[name]
    nc = bacc.Bacc("TRN2", target_bir_lowering=False, num_devices=1)
    aps = {k: nc.dram_tensor("in_" + k, x.shape, mybir.dt.from_np(x.dtype), kind="ExternalInput").ap() for k, x in arrays.items()}
    aps["out"] = nc.dram_tensor("out_0", (N, D), F32, kind="ExternalOutput").ap()
    build(nc, aps)
    r = run_bass_kernel_spmd(nc, [{"in_" + k: x for k, x in arrays.items()}], core_ids=[0])
    return r.results[0]["out_0"]
```

```python
from contextlib import ExitStack

import concourse.bass as bass
from concourse import mybir

P = 128
N = 3125
NT = 25
NP = NT * P
E = 50000
ET = 392
EB, EQ = 4, 98
S = ET + NT - 1
SB, SQ = 4, 104
UN, HU = 16, 8
D = 256
GW = 272
DC = D // P
BIG = 1.0e30
LN_EPS = 1e-5
BN_EPS = 1e-5
L0U, L0H = 8, 4
L0IT = S // L0U
QU = 4
SX = S + L0H
TRASH = NP
NACC = 4
NODE_CHUNKS = [(c * 512, min(512, NP - c * 512)) for c in range((NP + 511) // 512)]
BN_CHUNKS = [(c * 512, min(512, N - c * 512)) for c in range((N + 511) // 512)]

F32 = mybir.dt.float32
I32 = mybir.dt.int32
BF16 = mybir.dt.bfloat16
ALU = mybir.AluOpType
ACT = mybir.ActivationFunctionType
AX = mybir.AxisListType

ROWS = ["L0_gnn_bias", "L1_gnn_a_src", "L1_gnn_a_dst", "L1_gnn_bias", "L2_gnn_a_src1", "L2_gnn_a_dst1", "L2_gnn_b1",
        "L2_gnn_a_src2", "L2_gnn_a_dst2", "L2_gnn_b2", "L3_gnn_l2_b2", "L2_gnn_b_gcn"]
COLS = ["L2_gnn_g1", "L2_gnn_beta1", "L2_gnn_g2", "L2_gnn_beta2"] + [
    f"L3_gnn_l{l}_{v}" for l in range(3) for v in ("b1", "g1", "be1", "b2", "g2", "be2") if l < 2 or v in ("b1", "g1", "be1")
] + ["L2_gnn_g0", "L2_gnn_beta0"]


def build(nc, a):
    with ExitStack() as ctx:
        def sb(name, shape, dt=F32):
            return ctx.enter_context(nc.sbuf_tensor(name, shape, dt))

        def sem(name):
            return ctx.enter_context(nc.semaphore(name))

        def dram(name, shape, dt=F32):
            return nc.dram_tensor(name, shape, dt).ap()

        cols = sb("cols", [P, 2, NP])
        resid = sb("resid", [P, NT, D])
        accum = sb("accum", [P, NT, GW])
        hrows = sb("hrows", [P, NT, GW])
        accum_t = accum[:, :, :].rearrange("p t w -> p (t w)")[:, 0:2 * NP].rearrange("p (c n) -> p c n", c=2)
        slots = sb("slots", [P, UN, GW])
        onehot = sb("onehot", [P, UN, P])
        alpha = sb("alpha", [P, S, 8])
        peak = sb("peak", [P, S, 8])
        src_x = sb("src_x", [P, S], I32)
        src_xf = sb("src_xf", [P, SX])
        src_lo = sb("src_lo", [P, S])
        ew_x = sb("ew_x", [P, S])
        drel = sb("drel", [P, S])
        tn_i = sb("tn_i", [P, S], I32)
        te_i = sb("te_i", [SQ, SB], I32)
        reset_f = sb("reset_f", [SQ, SB, P])
        reset_r = sb("reset_r", [SQ, SB, P])
        with_first = sb("with_first", [SQ, SB, P])
        with_last = sb("with_last", [SQ, SB, P])
        carry_ok = sb("carry_ok", [8, S + 1])
        through_f = sb("through_f", [8, S])
        through_r = sb("through_r", [8, S])
        iota = sb("iota", [P, S])
        iota_p = sb("iota_p", [P, 1])
        ident = sb("ident", [P, P])
        before = sb("before", [P, P])
        ones = sb("ones", [P, P])
        idx_a = sb("idx_a", [P, UN], I32)
        idx_b = sb("idx_b", [P, L0U], I32)
        node_s = sb("node_s", [P, NT, 16])
        small = sb("small", [P, NT, 8])
        deg = sb("deg", [P, NT, 2])
        weights = sb("weights", [P, 4, D])
        rows = sb("rows", [P, len(ROWS), D])
        vecs = sb("vecs", [P, len(COLS), 2])
        stats = sb("stats", [P, NT, 8])
        mv = sb("mv", [P, NT, 2])
        bnst = sb("bnst", [P, 2, len(BN_CHUNKS), 6])
        bnmv = sb("bnmv", [P, 2, 2])
        bnsc = sb("bnsc", [P, 2, 4])
        attr_w = sb("attr_w", [4, D])
        carry = sb("carry", [8, S + 2])
        carry2 = sb("carry2", [8, S])
        carry_c = sb("carry_c", [SQ, SB, 8])
        te_last_i = sb("te_last_i", [EQ, EB, 1], I32)
        te_last = sb("te_last", [EQ, EB])
        flat_s = slots[:, :, :].rearrange("p u w -> p (u w)")
        flat_o = onehot[:, :, :].rearrange("p u w -> p (u w)")
        attr_c = flat_s[0:4, 0:2 * QU * P].rearrange("p (h k e) -> p h k e", h=2, k=QU)
        wide = flat_s[:, 1024:2048].bitcast(BF16).rearrange("p (h n e) -> p h n e", h=2, n=2)
        picked = flat_s[:, 2048:2048 + QU * NT * 8]
        lo_hot = flat_s[:, 2848:2848 + QU * NT].rearrange("p (u t) -> p u t", u=QU)
        as_now = flat_s[:, 2948:2948 + QU * 8].rearrange("p (u h) -> p u h", u=QU)
        hot_t = flat_o.rearrange("p (h n e) -> p h n e", h=2, n=2)
        enc = accum[:, 0:16, 0:D]
        segs = accum[0:SQ, :, :].rearrange("p t w -> p (t w)")[:, 0:8 * SB * P].rearrange("p (h b e) -> p h b e", h=8, b=SB)
        flat_a = accum[:, :, :].rearrange("p t w -> p (t w)")
        flat_h = hrows[:, :, :].rearrange("p t w -> p (t w)")
        key = flat_h[0:SQ, 0:SB * P].rearrange("p (b e) -> p b e", b=SB)
        srow = flat_h[0:SQ, 512:1024].rearrange("p (b e) -> p b e", b=SB)
        drow = flat_h[0:SQ, 1024:1536].rearrange("p (b e) -> p b e", b=SB)
        key_i = flat_h[0:SQ, 1536:2048].rearrange("p (b e) -> p b e", b=SB).bitcast(I32)
        hi_b = flat_a[0:SQ, 0:256].bitcast(BF16).rearrange("p (b e) -> p b e", b=SB)
        drow_b = flat_a[0:SQ, 256:512].bitcast(BF16).rearrange("p (b e) -> p b e", b=SB)
        hi_i = flat_a[0:SQ, 512:1024].rearrange("p (b e) -> p b e", b=SB).bitcast(I32)
        ew_g = flat_a[0:SQ, 1024:1536].rearrange("p (b e) -> p b e", b=SB)
        srow_i = flat_h[0:SQ, 2048:2560].rearrange("p (b e) -> p b e", b=SB).bitcast(I32)
        attr_g = flat_h[0:SQ, 2560:4608].rearrange("p (b e) -> p b e", b=SB)
        mask_t = flat_h[0:EQ, 4608:4608 + EB * S].rearrange("p (b s) -> p b s", b=EB)
        tmp = flat_a[:, 0:2048]
        edge_keys = flat_h[0:SQ, 6272:6272 + 2 * SB * 8].rearrange("p (n b e) -> p n b e", n=2, b=SB)
        neigh_t = flat_h[:, 0:2 * NP].rearrange("p (c n) -> p c n", c=2)
        l0 = resid[:, :, :].rearrange("p t d -> p (t d)")
        wide0 = flat_a[:, 2048:2560].bitcast(BF16).rearrange("p (h e) -> p h e", h=2)
        hot_t0 = flat_o[:, 0:1024].rearrange("p (h e) -> p h e", h=2)
        lo_i = flat_a[:, 2560:2560 + S].bitcast(I32)
        eq = l0[:, 1536:1536 + L0U * P].rearrange("p (u e) -> p u e", u=L0U)
        src_b = l0[:, 2560:2560 + L0U * P].rearrange("p (u e) -> p u e", u=L0U)
        msg = l0[:, 3584:3584 + L0U * 256].rearrange("p (u e) -> p u e", u=L0U)
        cnt = l0[:, 5632:5640]
        l0d = l0[:, 5640:5648]
        l0m = l0[:, 5648:5656]
        trash_p = l0[:, 5656:5657]
        pre4 = l0[:, 5660:5664]

        ps = ctx.enter_context(nc.psum_tensor("ps", [P, 8, 512], F32))

        table = [dram(f"table{k}", (NP, D)) for k in range(7)]
        t_gcn = dram("t_gcn", (NP, 64))
        t_hi = dram("t_hi", (S, P), BF16)
        t_drel = dram("t_drel", (S, P), BF16)
        t_neigh = [dram(f"t_neigh{k}", (NP + P, D)) for k in range(NACC)]
        t_attr = dram("t_attr", (S, 4 * P))

        gath = [sem(f"gath{u}") for u in range(UN)]
        wide_in = [sem(f"wide_in{h}") for h in range(2)]
        wide0_in = [sem(f"wide0_in{h}") for h in range(2)]
        idx_ready = sem("idx_ready")
        msg_ready = sem("msg_ready")
        oh_ready = sem("oh_ready")
        step_mm = sem("step_mm")
        step_acc = sem("step_acc")
        dv = sem("dv")
        scat = [sem(f"scat{k}") for k in range(NACC)]
        attr_in = [sem(f"attr_in{h}") for h in range(2)]

        def runs(end, *names):
            return [(n + end, c) for n, c in names]

        def by_layer(name, *counts):
            return [(f"{name}{k}", c) for k, c in enumerate(counts)]

        turns = [(n, NT) for n in ("l0n", "x1", "x2", "gcnt", "gatt1", "gatt2", "l2r", "x3", "gint0", "gint1")]
        products = [(n, NT) for n in ("l0", "l1", "gcn", "gat1", "gat2", "gin_last")]
        gin = [(n, 2 * len(NODE_CHUNKS)) for n in ("gin_mm1_0", "gin_mm2_0", "gin_mm1_1", "gin_mm2_1", "gin_mm1_2")]
        norms = [(n, 1) for n in ("gcn", "gat1", "gat2", "gin0a", "gin0b", "gin1a", "gin1b", "gin2a")]
        rooted = [(n, 1) for n in ("ln0", "deg", "ln1", "bn_gcn", "bn_gat1", "bn_gat2", "ln2", "bn_gin0a", "bn_gin0b",
                                   "bn_gin1a", "bn_gin1b", "bn_gin2a", "ln3")]
        shared = [runs("_tp", *turns), runs("_ev", *turns), runs("_mm", *products), runs("_ev", *products),
                  gin, runs("_ev", *gin), [("var_" + n, c) for n, c in rooted], [("std_" + n, c) for n, c in rooted],
                  [("bnsc_" + n, c) for n, c in norms],
                  by_layer("al_t", 8, 4, 4), by_layer("scan_f", 8, 4, 4), by_layer("scan_r", 8, 4, 4), by_layer("peak_t", 8, 4, 4),
                  by_layer("peak_ev", 8, 4, 4), by_layer("ends", 2, 2, 2), by_layer("carried", 2, 2, 2), by_layer("carry_t", 2, 2, 2),
                  by_layer("segs_done", 1, 1, 1), by_layer("lrelu", 1, 1, 1), by_layer("alpha_sub", 1, 1, 1), by_layer("exp", 1, 1, 1),
                  by_layer("scores", 1, 1, 1), by_layer("ln", 1, 1, 1, 1), by_layer("gin_z", 1, 1, 1), by_layer("gin_h", 1, 1),
                  [(f"elu_neg{k}", 2) for k in (1, 2)], [(f"elu_exp{k}", 2) for k in (1, 2)],
                  [(f"{n}{k}", 1) for k in (1, 2) for n in ("gat_in", "self_sub", "gat_out")] + [("elu2", 1)],
                  [("self_w1", 1), ("self_w2", 1)]]
        stage = {}
        for group in shared:
            base, signal = 0, sem("s_" + group[0][0])
            for name, n in group:
                stage[name] = (signal, base)
                base += n

        def done(name):
            if name not in stage:
                stage[name] = (sem("s_" + name), 0)
            return stage[name][0]

        def count(name, n):
            return done(name), stage[name][1] + n

        block = ctx.enter_context(nc.Block())

        IDX = {n: i for i, n in enumerate(ROWS)}
        COL = {n: i for i, n in enumerate(COLS)}

        def gath_base(g):
            return 16 * (S // UN) * g

        def row(name, w=D):
            return rows[:, IDX[name], 0:w]

        def vec(name, c, p=P):
            return vecs[0:p, COL[name], c:c + 1]

        roots = {f"ln{k}": (small[:, :, 0], small[:, :, 1]) for k in range(4)}
        roots["deg"] = (deg[:, :, 0], deg[:, :, 1])
        for n in ["gat1", "gat2"] + [f"gin{l}{w}" for l in range(3) for w in "ab"]:
            roots[f"bn_{n}"] = (bnsc[:, :, 2], bnsc[:, :, 3])
        roots["bn_gcn"] = (bnsc[0:64, 0:1, 2], bnsc[0:64, 0:1, 3])

        @block.sync
        def _(sp):
            def put(dst, src, s, **how):
                sp.dma_start(dst, src, **how).then_inc(s, 16)

            put(te_last_i[:, :, :], a["dst2"].rearrange("(b q) e -> q b e", b=EB)[:, :, P - 1:P], done("ld_last"), allow_slow_non_contiguous=True)
            put(rows[:, :, :], a["rows"], done("ld_rows"))
            put(vecs[:, :, :], a["vecs"], done("ld_vecs"))
            put(attr_w[:, :], a["attr_w"], done("ld_attrw"))
            put(weights[:, :, :], a["L0_gnn_weight"].rearrange("(c p) n -> p c n", p=P), done("ld_w0"))
            put(cols[:, :, :], a["x_cols"].rearrange("(c p) n -> p c n", p=P), done("ld_x"))
            sp.wait_ge(*count("zeroed", 1))
            for k in range(NACC):
                for c in range((NP + P) // P):
                    put(t_neigh[k][c * P:(c + 1) * P, :], flat_a[:, 6400:6400 + D], done("zero_tab"))
            sp.wait_ge(*count("attr_rows", SB * 16))
            put(t_attr.rearrange("(b q) e -> q b e", b=SB), attr_g, done("attr_out"))
            sp.wait_ge(*count("keys", 1))
            put(t_hi.rearrange("(b q) e -> q b e", b=SB), hi_b, done("rows_out"))
            put(t_drel.rearrange("(b q) e -> q b e", b=SB), drow_b, done("rows_out"))
            sp.wait_ge(*count("attr_out", 16))
            sp.wait_ge(*count("rows_out", 32))
            sp.wait_ge(*count("pre", 1))
            put(hrows[:, :, 0:D], a["x_pad"].rearrange("(t p) d -> p t d", p=P), done("ld_xh"))

            def on_each(t, first, n):
                return t[bass.ds(first, n), :].rearrange("s e -> (s e)").unsqueeze(0).to_broadcast([P, n * P])

            with sp.Fori(0, L0IT) as i:
                for h in range(2):
                    sp.wait_ge(*count("l0_hot", 2 * i + h + 1))
                    sp.dma_start(wide0[:, h, :], on_each(t_drel, i * L0U + h * L0H, L0H)).then_inc(wide0_in[h], 16)
            for k in range(NACC):
                sp.wait_ge(*count("l0_scat_all", 1))
                if k >= 2:
                    sp.wait_ge(*count("l0_summed", k - 1))
                into = [flat_a[:, 0:NT * D], flat_h[:, 0:NT * D]][min(k, 1)] if k < 2 else flat_h[:, 0:NT * D]
                put(into.rearrange("p (t d) -> p t d", t=NT), t_neigh[k][0:NP, :].rearrange("(t p) d -> p t d", p=P), done(f"ld_neigh{k}"))
            for name, n in (("l0_pre", 2 * L0IT + 2), ("l0_msg", 2 * L0IT + 1), ("l0_sidx", 2 * L0IT)):
                sp.wait_ge(*count(name, n))
            put(resid[:, :, :], a["x_pad"].rearrange("(t p) d -> p t d", p=P), done("ld_xrow"))
            sp.wait_ge(*count("l0_mm", NT))
            put(weights[:, 0:2, :], a["L1_gnn_W"].rearrange("(c p) n -> p c n", p=P), done("ld_w1"))

            def put_table(k):
                sp.wait_ge(*count(["l1_ev", "gat1_ev", "gat2_ev"][k], NT))
                put(table[k].rearrange("(t p) d -> p t d", p=P), hrows[:, :, 0:D], done(f"table{k}"))
            def score_rows(k):
                sp.wait_ge(*count(f"scores{k}", 1))
                with sp.Fori(0, S // UN) as i:
                    for q in range(UN // QU):
                        n = 4 * (S // UN) * k + 4 * i + q
                        sp.wait_ge(*count("hot_t", n + 1))
                        for j, t in enumerate((t_hi, t_drel)):
                            sp.dma_start(wide[:, q % 2, j, :], on_each(t, i * UN + q * QU, QU)).then_inc(wide_in[q % 2], 16)
                        if k == 0:
                            sp.wait_ge(*count("enc_free", 4 * i + q + 1))
                            sp.dma_start(attr_c[:, q % 2, :, :],
                                         t_attr.rearrange("s (f e) -> f s e", f=4)[:, bass.ds(i * UN + q * QU, QU), :]
                                         ).then_inc(attr_in[q % 2], 16)

            put_table(0)
            score_rows(0)
            sp.wait_ge(*count("l1_mm", NT))
            put(weights[:, 2:4, 0:64], a["L2_gnn_W_gcn"].rearrange("(c p) n -> p c n", p=P), done("ld_gcn"))
            sp.wait_ge(*count("gcn_ev", NT))
            put(t_gcn.rearrange("(t p) d -> p t d", p=P), hrows[:, :, 0:64], done("table_gcn"))
            put(weights[0:64, 0, :], a["L2_gnn_W1"], done("ld_gat1"))
            put_table(1)
            score_rows(1)
            sp.wait_ge(*count("gcn_mm", NT))
            put(weights[:, 2:4, :], a["L2_gnn_W2"].rearrange("(c p) n -> p c n", p=P), done("ld_gat2"))
            put_table(2)
            score_rows(2)
            for l in range(3):
                if l == 0:
                    sp.wait_ge(*count("ln2", 1))
                    put(table[3].rearrange("(t p) d -> p t d", p=P), resid[:, :, :], done("table3"))
                    sp.wait_ge(*count("gat2_mm", NT))
                else:
                    sp.wait_ge(*count(f"gint{l - 1}_ev", NT))
                    put(table[3 + l].rearrange("(t p) d -> p t d", p=P), hrows[:, :, 0:D], done(f"table{3 + l}"))
                    sp.wait_ge(*count(f"gin_mm2_{l - 1}", 2 * len(NODE_CHUNKS)))
                put(weights[:, 0:2, :], a[f"L3_gnn_l{l}_w1"].rearrange("(c p) n -> p c n", p=P), done(f"ld_gin{l}"))
                put(weights[:, 2:4, :], a[f"L3_gnn_l{l}_w2"].rearrange("(c p) n -> p c n", p=P), done(f"ld_gin{l}"))
            sp.wait_ge(*count("ln3", 1))
            whole = N // P
            put(a["out"][0:whole * P, :].rearrange("(t p) d -> p t d", p=P), resid[:, 0:whole, :], done("out"))
            put(a["out"][whole * P:N, :], resid[0:N - whole * P, whole, :], done("out"))
            sp.wait_ge(*count("out", 32))

        @block.gpsimd
        def _(pool):
            pool.memset(flat_a[:, 6400:6400 + D], 0.0).then_inc(done("zeroed"), 1)
            pool.iota(iota[:, :], [[1, S]], 0, 0, allow_small_or_imprecise_dtypes=True).then_inc(done("iota"), 1)
            pool.iota(iota_p[:, :], [[0, 1]], 0, 1, allow_small_or_imprecise_dtypes=True).then_inc(done("iota"), 1)
            pool.memset(ones[:, :], 1.0).then_inc(done("iota"), 1)
            pool.memset(node_s[:, :, :], 0.0).then_inc(done("iota"), 1)
            pool.wait_ge(*count("te", 1))
            for b in range(SB):
                at = bass.IndirectOffsetOnAxis(ap=te_i[:, b:b + 1], axis=0)
                pool.indirect_dma_start(key_i[:, b, :], None, a["dst2"], at).then_inc(done("key_rows"), 16)
                pool.indirect_dma_start(srow_i[:, b, :], None, a["src2"], at).then_inc(done("src_rows"), 16)
                pool.indirect_dma_start(ew_g[:, b, :], None, a["ew2"], at).then_inc(done("ew_rows"), 16)
                pool.indirect_dma_start(attr_g[:, b, :], None, a["attr"], at).then_inc(done("attr_rows"), 16)

            pool.sem_inc(done("hot_t"), 2)
            def l0_scatter(k, h):
                pool.wait_ge(*count("l0_evac", k + 3))
                pool.wait_ge(*count("l0_sidx", k + 1))
                pool.sem_inc(done("pool_go"), 1)
                for u in range(L0H):
                    pool.indirect_dma_start(t_neigh[u], bass.IndirectOffsetOnAxis(ap=idx_b[:, h * L0H + u:h * L0H + u + 1], axis=0),
                                            msg[:, h * L0H + u, :], None, compute_op=ALU.add).then_inc(scat[u], 16)

            def l0_landed(k):
                for u in range(L0H):
                    pool.wait_ge(scat[u], 16 * k + 16)
                pool.sem_inc(done("l0_prev"), 1)

            pool.sem_inc(done("l0_prev"), 2)
            pool.wait_ge(*count("zero_tab", 16 * NACC * (NT + 1)))
            with pool.Fori(0, L0IT) as i:
                for h in range(2):
                    l0_scatter(2 * i + h, h)
                    l0_landed(2 * i + h)
            pool.sem_inc(done("l0_scat_all"), 1)

            def one_hots(k):
                with pool.Fori(0, S // UN) as i:
                    for q in range(UN // QU):
                        n = 4 * (S // UN) * k + 4 * i + q
                        pool.wait_ge(wide_in[q % 2], 32 * (2 * (S // UN) * k + 2 * i + q // 2 + 1))
                        pool.wait_ge(*count("dst_mm", n + 1))
                        pool.sem_inc(done("pool_go"), 1)
                        for j in range(2):
                            last = pool.tensor_scalar(hot_t[:, q % 2, j, :], wide[:, q % 2, j, :], iota_p[:, :], None, ALU.is_equal)
                        last.then_inc(done("hot_t"), 1)

            def gathers(g, tab, w, ready, n):
                pool.wait_ge(*count(ready, n))
                with pool.Fori(0, S // UN) as i:
                    for h in range(2):
                        pool.wait_ge(idx_ready, 52 * g + 2 * i + h + 1)
                        pool.sem_inc(done("pool_go"), 1)
                        for u in range(h * HU, h * HU + HU):
                            pool.indirect_dma_start(slots[:, u, 0:w], None, tab,
                                                    bass.IndirectOffsetOnAxis(ap=idx_a[:, u:u + 1], axis=0)).then_inc(gath[u], 16)

            one_hots(0)
            gathers(0, table[0], D, "table0", 16)
            gathers(1, t_gcn, 64, "table_gcn", 16)
            for k in (1, 2):
                one_hots(k)
                gathers(k + 1, table[k], D, f"table{k}", 16)
            for l in range(3):
                gathers(4 + l, table[3 + l], D, f"table{3 + l}", 16)

        @block.tensor
        def _(pe):
            pe.sem_inc(step_mm, UN)
            pe.sem_inc(done("l0_pre"), 2)
            pe.sem_inc(done("enc_free"), 2)
            pe.sem_inc(done("dst_mm"), 2)
            pe.sem_inc(done("l0_x"), 2)
            tn_regs = [pe.alloc_register(f"pe_tn{u}") for u in range(QU)]

            def tiles_of(now):
                pe.load(tn_regs, tn_i[0:1, now])
                return [pe.snap(r, min_val=0, max_val=NT - 1) for r in tn_regs]


            def turn(name, t_count, f_in, p_out, src, free_after):
                for t in range(t_count):
                    if t >= 4:
                        pe.wait_ge(*count(name + "_ev", t - 3))
                    for c in range(max(1, f_in // P)):
                        w = min(f_in, P)
                        last = pe.transpose(ps[0:w, t % 4, c * P:c * P + P], src(t, c), ident[:, :])
                    last.then_inc(done(name + "_tp"), 1)

            pe.wait_ge(*count("step_mask", EB))
            pe.wait_ge(*count("iota", 4))
            for b in range(EB):
                mm = pe.matmul(ps[:, 0, 0:S], ones[0:EQ, :], mask_t[:, b, :], start=(b == 0), stop=(b == EB - 1))
            for o in range(SB):
                for b in range(EB):
                    mm = pe.matmul(ps[0:SQ, 1, o:o + 1], mask_t[:, b, o * SQ:(o + 1) * SQ], ones[0:EQ, 0:1],
                                   start=(b == 0), stop=(b == EB - 1))
            mm.then_inc(done("te_ps"), 1)
            pe.wait_ge(*count("keys", 1))
            pe.wait_ge(*count("ew_rows", 16 * SB))
            for n, t in enumerate((srow, ew_g, drow)):
                for b in range(SB):
                    mm = pe.transpose(ps[:, 2 + n, b * SQ:(b + 1) * SQ], t[:, b, :], ident[0:SQ, 0:SQ])
            for n in range(2):
                for b in range(SB):
                    mm = pe.matmul(ps[0:8, 5 + n, b * SQ:(b + 1) * SQ], edge_keys[:, n, b, :], ident[0:SQ, 0:SQ], start=True, stop=True)
            mm.then_inc(done("steps_ps"), 1)

            pe.wait_ge(*count("pre", 1))

            def l0_rows(k, h):
                pe.wait_ge(*count("l0_srcb", k + 1))
                pe.wait_ge(*count("l0_eq", k + 1))
                for u in range(L0H):
                    mm = pe.matmul(ps[:, 2 + h, u * P:(u + 1) * P], src_b[:, h * L0H + u, :], ident[:, :], start=True, stop=True)
                mm.then_inc(done("l0_rowb"), 1)

            def l0_x(k, h, now):
                at = tiles_of(now)
                pe.wait_ge(*count("l0_hot", k + 3))
                pe.wait_ge(*count("l0_msg", k + 1))
                for u in range(L0H):
                    mm = pe.matmul(ps[:, u // 2, (u % 2) * D:(u % 2) * D + D], hot_t0[:, h, u * P:(u + 1) * P],
                                   hrows[:, bass.ds(at[u], 1), 0:D], start=True, stop=True)
                mm.then_inc(done("l0_x"), 1)

            def l0_sums(k, h):
                pe.wait_ge(*count("l0_eq", k + 3))
                pe.wait_ge(*count("l0_msg", k + 2))
                pe.wait_ge(*count("l0_evac", k + 1))
                for u in range(L0H):
                    mm = pe.matmul(ps[:, 4 + 2 * h + u // 2, (u % 2) * D:(u % 2) * D + D], eq[:, h * L0H + u, :],
                                   slots[:, h * L0H + u, 0:D], start=True, stop=True)
                mm.then_inc(done("l0_pre"), 1)

            pe.wait_ge(*count("ld_xh", 16))
            l0_rows(0, 0)
            with pe.Fori(0, L0IT) as i:
                for h in range(2):
                    l0_x(2 * i + h, h, bass.ds(i * L0U + h * L0H, L0H))
                    l0_rows(2 * i + h + 1, 1 - h)
                    l0_sums(2 * i + h, h)
            pe.wait_ge(*count("l0_evac", 2 * L0IT + 2))
            pe.wait_ge(*count("l0_summed", NACC - 1))
            turn("l0n", NT, D, P, lambda t, c: flat_a[:, t * D + c * P:t * D + c * P + P], 0)
            pe.wait_ge(*count("l0n_ev", NT))
            pe.wait_ge(*count("ld_x", 16))
            pe.wait_ge(*count("ld_w0", 16))
            for t in range(NT):
                if t >= 4:
                    pe.wait_ge(*count("l0_ev", t - 3))
                n0 = t * P
                for c in range(DC):
                    pe.matmul(ps[:, 4 + t % 4, 0:D], cols[:, c, n0:n0 + P], weights[:, c, :], start=(c == 0), stop=False)
                for c in range(DC):
                    mm = pe.matmul(ps[:, 4 + t % 4, 0:D], neigh_t[:, c, n0:n0 + P], weights[:, DC + c, :], start=False, stop=(c == DC - 1))
                mm.then_inc(done("l0_mm"), 1)

            def turn_resid(name, ready):
                pe.wait_ge(*count(ready, 1))
                turn(name, NT, D, P, lambda t, c: resid[:, t, c * P:c * P + P], 0)
                pe.wait_ge(*count(name + "_ev", NT))

            def node_rows(name, chunks, p, w, wait, n):
                pe.wait_ge(*count(wait, n))
                for t in range(NT):
                    if t >= 4:
                        pe.wait_ge(*count(name + "_ev", t - 3))
                    for j, c in enumerate(chunks):
                        mm = pe.matmul(ps[:, 4 + t % 4, 0:w], cols[0:p, j, t * P:(t + 1) * P], weights[0:p, c, 0:w],
                                       start=(j == 0), stop=(j == len(chunks) - 1))
                    mm.then_inc(done(name + "_mm"), 1)
                pe.wait_ge(*count(name + "_ev", NT))

            def look_up(k, H):
                pe.wait_ge(*count(f"scores{k}", 1))
                ahead = 2 if k == 0 else 1
                with pe.Fori(0, S // UN) as i:
                    for q in range(UN // QU):
                        n = 4 * (S // UN) * k + 4 * i + q
                        at = tiles_of(bass.ds(i * UN + q * QU, QU))
                        pe.wait_ge(*count("hot_t", n + 3))
                        pe.wait_ge(*count("src_used", n + ahead))
                        for j in range(QU):
                            out = ps[:, j // 2, (j % 2) * NT * H:(j % 2 + 1) * NT * H] if k == 0 else ps[:, q % 2, j * NT * H:(j + 1) * NT * H]
                            mm = pe.matmul(out, hot_t[:, q % 2, 0, j * P:(j + 1) * P], node_s[:, :, 0:H], start=True, stop=True)
                        mm.then_inc(done("src_mm"), 1)
                        if k == 0:
                            pe.wait_ge(attr_in[q % 2], 16 * (2 * i + q // 2 + 1))
                            pe.wait_ge(*count("enc_done", 4 * i + q + 2))
                            for j in range(QU):
                                mm = pe.matmul(ps[:, 2 + j // 2, (j % 2) * D:(j % 2) * D + D], attr_c[:, q % 2, j, :], attr_w[:, :],
                                               start=True, stop=True)
                            mm.then_inc(done("enc_free"), 1)
                        pe.wait_ge(*count("dst_used", n + ahead))
                        for j in range(QU):
                            hot = hot_t[:, q % 2, 1, j * P:(j + 1) * P]
                            if k == 0:
                                mm = pe.matmul(ps[:, 4 + j, 0:GW], hot, hrows[:, bass.ds(at[j], 1), :], start=True, stop=True)
                            else:
                                mm = pe.matmul(ps[:, 2 + q % 2, 8 * j:8 * j + 8], hot, node_s[:, bass.ds(at[j], 1), 8:16], start=True, stop=True)
                        mm.then_inc(done("dst_mm"), 1)
                pe.wait_ge(*count("dst_used", 4 * (S // UN) * (k + 1) + 2))

            def max_segments(k, H):
                pe.wait_ge(*count(f"lrelu{k}", 1))
                for h in range(H):
                    if h >= 4:
                        pe.wait_ge(*count(f"scan_f{k}", h - 3))
                    for b in range(SB):
                        mm = pe.transpose(ps[0:SQ, h % 4, b * P:(b + 1) * P], alpha[:, b * SQ:(b + 1) * SQ, h], ident[:, :])
                    mm.then_inc(done(f"al_t{k}"), 1)
                for way, at in (("f", P - 1), ("r", 0)):
                    pe.wait_ge(*count(f"scan_{way}{k}", H))
                    for b in range(SB):
                        mm = pe.transpose(ps[0:H, 4, b * SQ:(b + 1) * SQ], segs[:, 0:H, b, at], ident[0:SQ, 0:SQ])
                    mm.then_inc(done(f"ends{k}"), 1)
                    pe.wait_ge(*count(f"carried{k}", 1 if way == "f" else 2))
                    for b in range(SB):
                        mm = pe.transpose(ps[0:SQ, 5, b * 8:b * 8 + H], carry2[0:H, b * SQ:(b + 1) * SQ], ident[0:H, 0:H])
                    mm.then_inc(done(f"carry_t{k}"), 1)
                pe.wait_ge(*count(f"segs_done{k}", 1))
                for h in range(H):
                    if h >= 4:
                        pe.wait_ge(*count(f"peak_ev{k}", h - 3))
                    for b in range(SB):
                        mm = pe.transpose(ps[:, h % 4, b * SQ:(b + 1) * SQ], segs[:, h, b, :], ident[0:SQ, 0:SQ])
                    mm.then_inc(done(f"peak_t{k}"), 1)
                pe.wait_ge(*count(f"peak_ev{k}", H))

            def add_up(g, w, weighted, transposed=False):
                with pe.Fori(0, S // UN) as i:
                    for u in range(UN):
                        h = u // HU
                        if u % HU == 0:
                            pe.wait_ge(oh_ready, 52 * g + 2 * i + h + 1)
                            if weighted is not None:
                                pe.wait_ge(msg_ready, 52 * weighted + 2 * i + h + 1)
                        if weighted is None:
                            pe.wait_ge(gath[u], gath_base(g) + 16 * i + 16)
                        pe.wait_ge(step_acc, S * g + UN * i + u + 1)
                        if transposed:
                            for c in range(DC):
                                mm = pe.matmul(ps[:, u % 4, c * P:c * P + P], slots[:, u, c * P:c * P + P], onehot[:, u, :],
                                               start=True, stop=True)
                        else:
                            mm = pe.matmul(ps[:, u % 4, 0:w], onehot[:, u, :], slots[:, u, 0:w], start=True, stop=True)
                        mm.then_inc(step_mm, 1)
                pe.wait_ge(step_acc, S * (g + 1) + 4)

            turn_resid("x1", "ln0")
            node_rows("l1", (0, 1), P, D, "ld_w1", 16)
            pe.wait_ge(*count("ld_attrw", 16))
            look_up(0, 8)
            max_segments(0, 8)
            add_up(0, D + 9, 0)
            turn_resid("x2", "ln1")
            node_rows("gcn", (2, 3), P, 64, "ld_gcn", 16)
            add_up(1, 64, None)
            pe.wait_ge(*count("gcn_out", 1))
            turn("gcnt", NT, 64, 64, lambda t, c: accum[:, t, 0:64], 0)
            pe.wait_ge(*count("gcnt_ev", NT))
            for k in (1, 2):
                pe.wait_ge(*count(f"ld_gat{k}", 16))
                node_rows(f"gat{k}", (0,) if k == 1 else (2, 3), 64 if k == 1 else P, D, f"gat_in{k}", 1)
                look_up(k, 4)
                max_segments(k, 4)
                add_up(k + 1, D + 8, k)
                pe.wait_ge(*count(f"gat_out{k}", 1))
                turn(f"gatt{k}", NT, D, P, lambda t, c: accum[:, t, c * P:c * P + P], 0)
                pe.wait_ge(*count(f"gatt{k}_ev", NT))
            pe.wait_ge(*count("elu2", 1))
            turn("l2r", NT, D, P, lambda t, c: cols[:, c, t * P:(t + 1) * P], 0)
            pe.wait_ge(*count("l2r_ev", NT))
            turn_resid("x3", "ln2")
            for l in range(3):
                add_up(4 + l, D, None, transposed=True)
                pe.wait_ge(*count(f"ld_gin{l}", 32))

                def gin_mm(name, w0, src):
                    n = 0
                    for n0, w in NODE_CHUNKS:
                        for m in range(DC):
                            if n >= 4:
                                pe.wait_ge(*count(name + "_ev", n - 3))
                            for c in range(DC):
                                mm = pe.matmul(ps[:, 4 + n % 4, 0:w], weights[:, w0 + c, m * P:(m + 1) * P], src[:, c, n0:n0 + w],
                                               start=(c == 0), stop=(c == DC - 1))
                            mm.then_inc(done(name), 1)
                            n += 1
                    pe.wait_ge(*count(name + "_ev", n))

                gin_mm(f"gin_mm1_{l}", 0, accum_t)
                pe.wait_ge(*count(f"gin_z{l}", 1))
                if l < 2:
                    gin_mm(f"gin_mm2_{l}", 2, cols)
                    pe.wait_ge(*count(f"gin_h{l}", 1))
                    turn(f"gint{l}", NT, D, P, lambda t, c: accum_t[:, c, t * P:(t + 1) * P], 0)
                    pe.wait_ge(*count(f"gint{l}_ev", NT))
                else:
                    node_rows("gin_last", (2, 3), P, D, f"gin_z{l}", 1)

        @block.scalar
        def _(act):
            act.sem_inc(done("l0_evac"), 2)
            act.sem_inc(done("enc_done"), 2)

            def l0_spread(k, h):
                act.wait_ge(*count("l0_eq", k + 1))
                act.activation(src_b[:, h * L0H:h * L0H + L0H, :],
                               src_xf[:, bass.ds(k * L0H, L0H)].unsqueeze(2).to_broadcast([P, L0H, P]), ACT.Copy).then_inc(done("l0_srcb"), 1)

            def l0_out_of_psum(k, h):
                act.wait_ge(*count("l0_pre", k + 3))
                act.wait_ge(*count("l0_prev", k + 1))
                act.activation(msg[:, h * L0H:h * L0H + L0H, :].rearrange("p u d -> p (u d)"),
                               ps[:, 4 + 2 * h:6 + 2 * h, :].rearrange("p b d -> p (b d)"), ACT.Copy).then_inc(done("l0_evac"), 1)

            act.wait_ge(*count("pre", 1))
            l0_spread(0, 0)
            with act.Fori(0, L0IT) as i:
                for h in range(2):
                    l0_spread(2 * i + h + 1, 1 - h)
                    l0_out_of_psum(2 * i + h, h)

            def turned(name, n_tiles, p, c, dst):
                for t in range(n_tiles):
                    act.wait_ge(*count(name + "_tp", t + 1))
                    act.activation(dst[0:p, 0:c, t * P:(t + 1) * P], ps[0:p, t % 4, 0:c * P].rearrange("p (c n) -> p c n", c=c),
                                   ACT.Copy).then_inc(done(name + "_ev"), 1)

            def root(name):
                act.wait_ge(*count("var_" + name, 1))
                src, dst = roots[name]
                act.activation(dst, src, ACT.Sqrt).then_inc(done("std_" + name), 1)

            def rows_out(name, w, scale=None):
                for t in range(NT):
                    act.wait_ge(*count(name + "_mm", t + 1))
                    act.activation(hrows[:, t, 0:w], ps[:, 4 + t % 4, 0:w], ACT.Copy,
                                   scale=1.0 if scale is None else scale(t)).then_inc(done(name + "_ev"), 1)

            def encoded():
                with act.Fori(0, S // UN) as i:
                    for q in range(UN // QU):
                        act.wait_ge(*count("dst_used", 4 * i + q + 1))
                        act.wait_ge(*count("enc_free", 4 * i + q + 3))
                        act.activation(enc[:, q * QU:q * QU + QU, :], ps[:, 2:4, :].rearrange("p b (j d) -> p (b j) d", j=2),
                                       ACT.Relu).then_inc(done("enc_done"), 1)

            def indices(g):
                with act.Fori(0, S // UN) as i:
                    for h in range(2):
                        act.wait_ge(step_mm, S * g + UN * i + HU * h + HU)
                        act.activation(idx_a[:, h * HU:h * HU + HU], src_x[:, bass.ds(i * UN + h * HU, HU)],
                                       ACT.Copy).then_inc(idx_ready, 1)

            def weights_of(k, H):
                for h in range(H):
                    act.wait_ge(*count(f"peak_t{k}", h + 1))
                    act.activation(peak[:, :, h], ps[:, h % 4, 0:S], ACT.Copy).then_inc(done(f"peak_ev{k}"), 1)
                act.wait_ge(*count(f"alpha_sub{k}", 1))
                act.activation(alpha[:, :, 0:H], alpha[:, :, 0:H], ACT.Exp).then_inc(done(f"exp{k}"), 1)

            turned("l0n", NT, P, 2, neigh_t)
            root("ln0")
            turned("x1", NT, P, 2, cols)
            rows_out("l1", D)
            act.wait_ge(*count("scores0", 1))
            encoded()
            weights_of(0, 8)
            indices(0)
            root("deg")
            root("ln1")
            turned("x2", NT, P, 2, cols)
            act.wait_ge(*count("dinv", 1))
            rows_out("gcn", 64, lambda t: deg[:, t, 1:2])
            indices(1)
            turned("gcnt", NT, 64, 1, cols)
            root("bn_gcn")
            act.wait_ge(*count("bnsc_gcn", 1))
            act.activation(cols[0:64, 0, :], cols[0:64, 0, :], ACT.Identity, bias=bnsc[0:64, 0, 1:2],
                           scale=bnsc[0:64, 0, 0:1]).then_inc(done("gat_in1"), 1)
            for k in (1, 2):
                rows_out(f"gat{k}", D)
                weights_of(k, 4)
                indices(k + 1)
                act.wait_ge(*count(f"self_sub{k}", 1))
                act.activation(small[:, :, 0:4], small[:, :, 0:4], ACT.Exp).then_inc(done(f"self_w{k}"), 1)
                turned(f"gatt{k}", NT, P, 2, cols)
                root(f"bn_gat{k}")
                for c in range(DC):
                    act.wait_ge(*count(f"elu_neg{k}", c + 1))
                    act.activation(accum_t[:, c, :], accum_t[:, c, :], ACT.Exp).then_inc(done(f"elu_exp{k}"), 1)
            root("ln2")
            turned("x3", NT, P, 2, accum_t)

            def biased(name, dst, bias):
                n = 0
                for n0, w in NODE_CHUNKS:
                    for m in range(DC):
                        act.wait_ge(*count(name, n + 1))
                        act.activation(dst[:, m, n0:n0 + w], ps[:, 4 + n % 4, 0:w], ACT.Identity,
                                       bias=vec(bias, m)).then_inc(done(name + "_ev"), 1)
                        n += 1

            def relu_scaled(name, buf, ready):
                act.wait_ge(*count("bnsc_" + name, 1))
                for c in range(DC):
                    last = act.activation(buf[:, c, :], buf[:, c, :], ACT.Relu, bias=bnsc[:, c, 1:2], scale=bnsc[:, c, 0:1])
                last.then_inc(done(ready), 1)

            for l in range(3):
                indices(4 + l)
                biased(f"gin_mm1_{l}", cols, f"L3_gnn_l{l}_b1")
                root(f"bn_gin{l}a")
                relu_scaled(f"gin{l}a", cols, f"gin_z{l}")
                if l < 2:
                    biased(f"gin_mm2_{l}", accum_t, f"L3_gnn_l{l}_b2")
                    root(f"bn_gin{l}b")
                    relu_scaled(f"gin{l}b", accum_t, f"gin_h{l}")
                    for t in range(NT):
                        act.wait_ge(*count(f"gint{l}_tp", t + 1))
                        act.activation(hrows[:, t, 0:D], ps[:, t % 4, 0:D], ACT.Copy).then_inc(done(f"gint{l}_ev"), 1)
            root("ln3")

        @block.vector
        def _(dve):
            chain = [0]

            def link(ins):
                chain[0] += 1
                ins.then_inc(dv, 1)
                dve.wait_ge(dv, chain[0])

            dve.sem_inc(step_acc, 4)
            for name, n in (("src_used", 2), ("dst_used", 2), ("l0_eq", 2), ("l0_msg", 1), ("l0_hot", 2)):
                dve.sem_inc(done(name), n)
            tn_regs = [dve.alloc_register(f"tn{u}") for u in range(HU)]

            dve.wait_ge(*count("iota", 4))
            link(dve.tensor_scalar(ident[:, :], iota[:, 0:P], iota_p[:, :], None, ALU.is_equal))
            link(dve.tensor_scalar(before[:, :], iota[:, 0:P], iota_p[:, :], None, ALU.is_lt))
            dve.wait_ge(*count("ld_last", 16))
            link(dve.tensor_scalar(te_last_i[:, :, :], te_last_i[:, :, :], 7, None, ALU.logical_shift_right))
            link(dve.tensor_copy(te_last[:, :], te_last_i[:, :, 0]))
            for b in range(EB):
                link(dve.tensor_scalar(te_last[:, b:b + 1], te_last[:, b:b + 1], iota_p[0:EQ, :], float(EQ * b + 1), ALU.add, ALU.add))
                dve.tensor_scalar(mask_t[:, b, :], iota[0:EQ, :], te_last[:, b:b + 1], None, ALU.is_ge).then_inc(done("step_mask"), 1)
            dve.wait_ge(*count("te_ps", 1))
            dve.tensor_copy(te_i[:, :], ps[0:SQ, 1, 0:SB]).then_inc(done("te"), 1)
            link(dve.tensor_tensor(tn_i[:, :], iota[:, :], ps[:, 0, 0:S], ALU.subtract))
            for b in range(SB):
                link(dve.tensor_scalar(pre4[0:SQ, b:b + 1], ps[0:SQ, 1, b:b + 1], iota_p[0:SQ, :], float(-SQ * b), ALU.subtract, ALU.add))
            link(dve.tensor_scalar(pre4[0:SQ, :], pre4[0:SQ, :], float(P), None, ALU.mult))
            dve.wait_ge(*count("key_rows", 16 * SB))
            dve.wait_ge(*count("src_rows", 16 * SB))
            link(dve.tensor_copy(key, key_i))
            link(dve.tensor_copy(srow, srow_i))
            for b in range(SB):
                link(dve.tensor_scalar(drow[:, b, :], key[:, b, :], pre4[0:SQ, b:b + 1], None, ALU.add))
            link(dve.tensor_copy(drow_b, drow))
            link(dve.tensor_scalar(hi_i, srow_i, P - 1, None, ALU.bitwise_and))
            link(dve.tensor_copy(hi_b, hi_i))
            link(dve.tensor_copy(edge_keys[:, 0, :, :], key[:, :, 0:1].to_broadcast([SQ, SB, 8])))
            dve.tensor_copy(edge_keys[:, 1, :, :], key[:, :, P - 1:P].to_broadcast([SQ, SB, 8])).then_inc(done("keys"), 1)
            def barrier_of(out):
                link(dve.tensor_scalar(out, out, 1.0, BIG, ALU.subtract, ALU.mult))

            link(dve.memset(reset_f[:, :, 0:1], 0.0))
            link(dve.memset(reset_r[:, :, P - 1:P], 0.0))
            link(dve.tensor_tensor(reset_f[:, :, 1:P], key[:, :, 1:P], key[:, :, 0:P - 1], ALU.is_equal))
            barrier_of(reset_f[:, :, 1:P])
            link(dve.tensor_copy(reset_r[:, :, 0:P - 1], reset_f[:, :, 1:P]))
            for b in range(SB):
                link(dve.tensor_scalar(with_first[:, b, :], key[:, b, :], key[:, b, 0:1], None, ALU.is_equal))
                link(dve.tensor_scalar(with_last[:, b, :], key[:, b, :], key[:, b, P - 1:P], None, ALU.is_equal))
            barrier_of(with_first[:, :, :])
            barrier_of(with_last[:, :, :])
            dve.wait_ge(*count("steps_ps", 1))
            link(dve.tensor_copy(src_x[:, :], ps[:, 2, 0:S]))
            link(dve.memset(src_xf[:, S:SX], 0.0))
            link(dve.tensor_copy(src_xf[:, 0:S], ps[:, 2, 0:S]))
            link(dve.tensor_copy(ew_x[:, :], ps[:, 3, 0:S]))
            link(dve.tensor_scalar(lo_i, src_x[:, :], 7, None, ALU.logical_shift_right))
            link(dve.tensor_copy(src_lo[:, :], lo_i))
            link(dve.tensor_copy(drel[:, :], ps[:, 4, 0:S]))
            link(dve.tensor_copy(carry[:, 0:S], ps[0:8, 5, 0:S]))
            link(dve.tensor_tensor(carry2[:, :], carry[:, 0:S], ps[0:8, 6, 0:S], ALU.is_equal))
            link(dve.memset(carry_ok[:, :], 0.0))
            link(dve.tensor_tensor(carry_ok[:, 1:S], carry[:, 1:S], ps[0:8, 6, 0:S - 1], ALU.is_equal))
            link(dve.tensor_tensor(through_f[:, :], carry_ok[:, 0:S], carry2[:, :], ALU.mult))
            link(dve.tensor_tensor(through_r[:, :], carry_ok[:, 1:S + 1], carry2[:, :], ALU.mult))
            barrier_of(carry_ok[:, :])
            barrier_of(through_f[:, :])
            barrier_of(through_r[:, :])
            dve.tensor_scalar(trash_p, iota_p[:, :], float(TRASH), None, ALU.add).then_inc(done("pre"), 1)
            dve.wait_ge(*count("pre", 1))

            def l0_half(k, h):
                half = slice(h * L0H, h * L0H + L0H)
                now = bass.ds(k * L0H, L0H)
                dve.wait_ge(wide0_in[h], 8 * (k - h) + 16)
                dve.wait_ge(*count("l0_x", k + 1))
                dve.tensor_scalar(hot_t0[:, h, :], wide0[:, h, :], iota_p[:, :], None, ALU.is_equal).then_inc(done("l0_hot"), 1)
                dve.wait_ge(*count("l0_rowb", k + 1))
                dve.wait_ge(*count("l0_pre", k + 1))
                dve.tensor_tensor(eq[:, half, :], ps[:, 2 + h, :].rearrange("p (u e) -> p u e", u=L0H),
                                  src_xf[:, now].unsqueeze(2).to_broadcast([P, L0H, P]), ALU.is_equal).then_inc(done("l0_eq"), 1)
                dve.wait_ge(*count("l0_eq", k + 3))
                v = tmp[:, 0:L0H * P].rearrange("p (u e) -> p u e", u=L0H)
                dve.tensor_tensor(v, eq[:, half, :], before[:, :].unsqueeze(1).to_broadcast([P, L0H, P]), ALU.mult).then_inc(done("l0_dv"), 1)
                dve.wait_ge(*count("l0_dv", 4 * k + 1))
                c0 = h * L0H
                dve.tensor_reduce(cnt[:, c0:c0 + L0H], v, AX.X, ALU.add).then_inc(done("l0_dv"), 1)
                dve.tensor_scalar(l0d[:, c0:c0 + L0H], src_xf[:, now], -1.0, trash_p, ALU.mult, ALU.add).then_inc(done("l0_dv"), 1)
                dve.wait_ge(*count("l0_dv", 4 * k + 3))
                dve.scalar_tensor_tensor(l0m[:, c0:c0 + L0H], cnt[:, c0:c0 + L0H], 1.0, l0d[:, c0:c0 + L0H], ALU.min,
                                         ALU.mult).then_inc(done("l0_dv"), 1)
                dve.wait_ge(*count("l0_dv", 4 * k + 4))
                dve.wait_ge(*count("l0_prev", k + 1))
                dve.tensor_tensor(idx_b[:, half], l0m[:, c0:c0 + L0H], src_xf[:, now], ALU.add).then_inc(done("l0_sidx"), 1)
                dve.wait_ge(*count("l0_x", k + 3))
                for u in range(0, L0H, 2):
                    two = slice(c0 + u, c0 + u + 2)
                    last = dve.tensor_tensor(slots[:, two, 0:D], ps[:, u // 2, :].rearrange("p (j d) -> p j d", j=2),
                                             ew_x[:, bass.ds(k * L0H + u, 2)].unsqueeze(2).to_broadcast([P, 2, D]), ALU.mult)
                last.then_inc(done("l0_msg"), 1)

            with dve.Fori(0, L0IT) as i:
                l0_half(2 * i, 0)
                l0_half(2 * i + 1, 1)

            sums = flat_a[:, 0:NT * D]
            for k in range(1, NACC):
                dve.wait_ge(*count(f"ld_neigh{k}", 16))
                if k == 1:
                    dve.wait_ge(*count("ld_neigh0", 16))
                else:
                    dve.wait_ge(*count("l0_summed", k - 1))
                dve.tensor_tensor(sums, sums, flat_h[:, 0:NT * D], ALU.add).then_inc(done("l0_summed"), 1)
            dve.wait_ge(*count("ld_xrow", 16))
            dve.wait_ge(*count("ld_rows", 16))
            all_rows = lambda v, w=D: v.unsqueeze(1).to_broadcast([P, NT, w])
            link(dve.tensor_tensor(resid[:, :, :], resid[:, :, :], all_rows(row("L0_gnn_bias")), ALU.add))
            for t in range(NT):
                dve.wait_ge(*count("l0_mm", t + 1))
                dve.tensor_tensor(resid[:, t, :], resid[:, t, :], ps[:, 4 + t % 4, 0:D], ALU.add).then_inc(done("l0_ev"), 1)
            dve.wait_ge(*count("l0_ev", NT))

            def layer_norm(k):
                for t in range(NT):
                    last = dve.bn_stats(stats[:, t, 0:6], resid[:, t, :])
                link(last)
                for t in range(NT):
                    last = dve.bn_aggr(mv[:, t, :], stats[:, t, 0:6])
                link(last)
                dve.tensor_scalar(small[:, :, 0], mv[:, :, 1], LN_EPS, None, ALU.add).then_inc(done(f"var_ln{k}"), 1)
                dve.wait_ge(*count(f"std_ln{k}", 1))
                link(dve.reciprocal(small[:, :, 2], small[:, :, 1]))
                for t in range(NT):
                    last = dve.tensor_scalar(resid[:, t, :], resid[:, t, :], mv[:, t, 0:1], small[:, t, 2:3], ALU.subtract, ALU.mult)
                last.then_inc(done(f"ln{k}"), 1)

            def node_scores(k, H, src_row, dst_row, name):
                dve.wait_ge(*count(name, NT))
                prod = flat_a[:, 0:NT * D].rearrange("p (t d) -> p t d", t=NT)
                for n, r in enumerate((src_row, dst_row)):
                    link(dve.tensor_tensor(prod, hrows[:, :, 0:D], all_rows(row(r)), ALU.mult))
                    link(dve.tensor_reduce(node_s[:, :, 8 * n:8 * n + H], prod.rearrange("p t (h d) -> p t h d", h=H), AX.X, ALU.add))
                if H == 8:
                    dve.tensor_copy(hrows[:, :, D:D + 16], node_s[:, :, :]).then_inc(done(f"scores{k}"), 1)
                else:
                    link(dve.tensor_tensor(node_s[:, :, 12:16], node_s[:, :, 0:4], node_s[:, :, 8:12], ALU.add))
                    dve.scalar_tensor_tensor(node_s[:, :, 12:16], node_s[:, :, 12:16], 0.2, node_s[:, :, 12:16], ALU.mult,
                                             ALU.max).then_inc(done(f"scores{k}"), 1)

            def edge_scores(k, H):
                per = 5 if k == 0 else 2
                with dve.Fori(0, S // UN) as i:
                    for q in range(UN // QU):
                        n = 4 * (S // UN) * k + 4 * i + q
                        linked = (0 if k == 0 else 5 * 4 * (S // UN) + 2 * 4 * (S // UN) * (k - 1)) + per * (4 * i + q)
                        now = bass.ds(i * UN + q * QU, QU)
                        part = picked[:, 0:QU * NT * H]
                        dve.tensor_tensor(lo_hot, iota[:, 0:NT].unsqueeze(1).to_broadcast([P, QU, NT]),
                                          src_lo[:, now].unsqueeze(2).to_broadcast([P, QU, NT]), ALU.is_equal).then_inc(done("sc_dv"), 1)
                        dve.wait_ge(*count("sc_dv", linked + 1))
                        dve.wait_ge(*count("src_mm", n + 1))
                        if k == 0:
                            for b in range(2):
                                last = dve.tensor_tensor(part[:, b * 2 * NT * H:(b + 1) * 2 * NT * H].rearrange("p (u t h) -> p u t h", u=2, t=NT),
                                                         ps[:, b, 0:2 * NT * H].rearrange("p (u t h) -> p u t h", u=2, t=NT),
                                                         lo_hot[:, 2 * b:2 * b + 2, :].unsqueeze(3).to_broadcast([P, 2, NT, H]), ALU.mult)
                        else:
                            last = dve.tensor_tensor(part.rearrange("p (u t h) -> p u t h", u=QU, t=NT),
                                                     ps[:, q % 2, 0:QU * NT * H].rearrange("p (u t h) -> p u t h", u=QU, t=NT),
                                                     lo_hot.unsqueeze(3).to_broadcast([P, QU, NT, H]), ALU.mult)
                        last.then_inc(done("src_used"), 1)
                        dve.wait_ge(*count("src_used", n + 3))
                        dve.tensor_reduce(as_now[:, :, 0:H], part.rearrange("p (u t h) -> p u h t", u=QU, t=NT), AX.X, ALU.add).then_inc(done("sc_dv"), 1)
                        if k == 0:
                            dve.wait_ge(*count("enc_done", 4 * i + q + 3))
                            dve.wait_ge(*count("dst_mm", n + 3))
                            e4 = enc[:, q * QU:q * QU + QU, :]
                            dve.tensor_tensor(e4, e4, ps[:, 4:8, 0:D], ALU.mult).then_inc(done("sc_dv"), 1)
                            dve.wait_ge(*count("sc_dv", linked + 3))
                            v = peak[:, now, :]
                            dve.tensor_reduce(v, e4.rearrange("p u (h d) -> p u h d", h=8), AX.X, ALU.add).then_inc(done("sc_dv"), 1)
                            dve.wait_ge(*count("sc_dv", linked + 4))
                            dve.tensor_tensor(v, v, as_now, ALU.add).then_inc(done("sc_dv"), 1)
                            dve.wait_ge(*count("sc_dv", linked + 5))
                            last = dve.tensor_tensor(alpha[:, now, :], v, ps[:, 4:8, D + 8:D + 16], ALU.add)
                        else:
                            dve.wait_ge(*count("sc_dv", linked + 2))
                            dve.wait_ge(*count("dst_mm", n + 3))
                            d4 = ps[:, 2 + q % 2, 0:8 * QU].rearrange("p (u h) -> p u h", u=QU)
                            dve.tensor_copy(peak[:, now, 4:8], d4[:, :, 4:8])
                            last = dve.tensor_tensor(alpha[:, now, 0:4], as_now[:, :, 0:4], d4[:, :, 0:4], ALU.add)
                        last.then_inc(done("dst_used"), 1)
                dve.wait_ge(*count("dst_used", 4 * (S // UN) * (k + 1) + 2))

            def softmax(k, H):
                al = alpha[:, :, 0:H]
                dve.scalar_tensor_tensor(al, al, 0.2, al, ALU.mult, ALU.max).then_inc(done(f"lrelu{k}"), 1)
                dve.wait_ge(*count(f"lrelu{k}", 1))
                for h in range(H):
                    dve.wait_ge(*count(f"al_t{k}", h + 1))
                    for b in range(SB):
                        last = dve.tensor_tensor_scan(segs[:, h, b, :], reset_f[:, b, :], ps[0:SQ, h % 4, b * P:(b + 1) * P], -BIG, ALU.add, ALU.max)
                    last.then_inc(done(f"scan_f{k}"), 1)
                dve.wait_ge(*count(f"scan_f{k}", H))
                for way in (0, 1):
                    dve.wait_ge(*count(f"ends{k}", way + 1))
                    if way == 0:
                        link(dve.memset(carry[:, 0:1], -BIG))
                        link(dve.tensor_tensor_scan(carry[0:H, 1:S + 1], through_f[0:H, :], ps[0:H, 4, 0:S], -BIG, ALU.add, ALU.max))
                        dve.tensor_tensor(carry2[0:H, :], carry[0:H, 0:S], carry_ok[0:H, 0:S], ALU.add).then_inc(done(f"carried{k}"), 1)
                    else:
                        link(dve.memset(carry[:, S:S + 1], -BIG))
                        link(dve.tensor_tensor_scan(carry[0:H, S - 1::-1], through_r[0:H, ::-1], ps[0:H, 4, S - 1::-1], -BIG, ALU.add, ALU.max))
                        dve.tensor_tensor(carry2[0:H, :], carry[0:H, 1:S + 1], carry_ok[0:H, 1:S + 1], ALU.add).then_inc(done(f"carried{k}"), 1)
                    dve.wait_ge(*count(f"carry_t{k}", way + 1))
                    link(dve.tensor_copy(carry_c[:, :, 0:H], ps[0:SQ, 5, 0:8 * SB].rearrange("p (b h) -> p b h", b=SB)[:, :, 0:H]))
                    same = with_first if way == 0 else with_last
                    for h in range(H):
                        for b in range(SB):
                            last = dve.scalar_tensor_tensor(segs[:, h, b, :], same[:, b, :], carry_c[:, b, h:h + 1], segs[:, h, b, :], ALU.add, ALU.max)
                    if way == 1:
                        last.then_inc(done(f"segs_done{k}"), 1)
                        break
                    link(last)
                    for h in range(H):
                        for b in range(SB):
                            last = dve.tensor_tensor_scan(segs[:, h, b, ::-1], reset_r[:, b, ::-1], segs[:, h, b, ::-1], -BIG, ALU.add, ALU.max)
                    last.then_inc(done(f"scan_r{k}"), H)
                    dve.wait_ge(*count(f"scan_r{k}", H))
                dve.wait_ge(*count(f"peak_ev{k}", H))
                if H == 4:
                    link(dve.tensor_tensor(peak[:, :, 0:4], peak[:, :, 0:4], peak[:, :, 4:8], ALU.max))
                dve.tensor_tensor(al, al, peak[:, :, 0:H], ALU.subtract).then_inc(done(f"alpha_sub{k}"), 1)
                dve.wait_ge(*count(f"exp{k}", 1))
                if H == 4:
                    link(dve.tensor_tensor(peak[:, :, 4:8], al, peak[:, :, 0:4], ALU.mult))
                link(dve.memset(accum[:, :, :], 0.0))

            def add_up(g, w, weighted, H=8, transposed=False):
                with dve.Fori(0, S // UN) as i:
                    for h in range(2):
                        half = slice(h * HU, h * HU + HU)
                        now = bass.ds(i * UN + h * HU, HU)
                        dve.load(tn_regs, tn_i[0:1, now])
                        dve.wait_ge(step_mm, S * g + UN * i + HU * h + HU)
                        dve.tensor_tensor(onehot[:, half, :], iota[:, 0:P].unsqueeze(1).to_broadcast([P, HU, P]),
                                          drel[:, now].unsqueeze(2).to_broadcast([P, HU, P]), ALU.is_equal).then_inc(oh_ready, 1)
                        if weighted is not None:
                            for u in range(h * HU, h * HU + HU):
                                dve.wait_ge(gath[u], gath_base(g) + 16 * i + 16)
                            v = slots[:, half, 0:D].rearrange("p u (h d) -> p u h d", h=H)
                            dve.tensor_tensor(v, v, alpha[:, now, 0:H].unsqueeze(3).to_broadcast([P, HU, H, D // H]), ALU.mult)
                            last = dve.tensor_copy(slots[:, half, D:D + H], alpha[:, now, 0:H])
                            if H == 4:
                                last = dve.tensor_copy(slots[:, half, D + 4:D + 8], peak[:, now, 4:8])
                            last.then_inc(msg_ready, 1)
                        for u in range(HU):
                            at = dve.snap(tn_regs[u], min_val=0, max_val=NT - 1)
                            dve.wait_ge(step_mm, S * g + UN * i + HU * h + u + UN + 1)
                            dve.wait_ge(step_acc, S * g + UN * i + HU * h + u + 4)
                            bank = ps[:, (h * HU + u) % 4, 0:w]
                            if transposed:
                                to = accum_t[:, :, bass.ds(at * P, P)]
                                bank = bank.rearrange("p (c n) -> p c n", c=DC)
                            else:
                                to = accum[:, bass.ds(at, 1), 0:w]
                                bank = bank.unsqueeze(1)
                            dve.tensor_tensor(to, to, bank, ALU.add).then_inc(step_acc, 1)
                dve.wait_ge(step_acc, S * (g + 1) + 4)

            heads = lambda v, H, w: v.unsqueeze(3).to_broadcast([P, NT, H, w])

            def batch_norm(name, buf, p, n_c, g, be):
                for c in range(n_c):
                    for j, (n0, w) in enumerate(BN_CHUNKS):
                        last = dve.bn_stats(bnst[0:p, c, j, :], buf[0:p, c, n0:n0 + w])
                link(last)
                for c in range(n_c):
                    last = dve.bn_aggr(bnmv[0:p, c, :], bnst[0:p, c, :, :].rearrange("p j s -> p (j s)"))
                link(last)
                dve.tensor_scalar(bnsc[0:p, 0:n_c, 2], bnmv[0:p, 0:n_c, 1], BN_EPS, None, ALU.add).then_inc(done(f"var_bn_{name}"), 1)
                dve.wait_ge(*count(f"std_bn_{name}", 1))
                link(dve.reciprocal(bnsc[0:p, 0:n_c, 2], bnsc[0:p, 0:n_c, 3]))
                gi, bi = COL[g], COL[be]
                link(dve.tensor_tensor(bnsc[0:p, 0:n_c, 0], bnsc[0:p, 0:n_c, 2], vecs[0:p, gi, 0:n_c], ALU.mult))
                link(dve.tensor_tensor(bnsc[0:p, 0:n_c, 2], bnsc[0:p, 0:n_c, 0], bnmv[0:p, 0:n_c, 0], ALU.mult))
                dve.tensor_tensor(bnsc[0:p, 0:n_c, 1], vecs[0:p, bi, 0:n_c], bnsc[0:p, 0:n_c, 2], ALU.subtract).then_inc(done(f"bnsc_{name}"), 1)
                dve.wait_ge(*count(f"bnsc_{name}", 1))

            layer_norm(0)
            node_scores(0, 8, "L1_gnn_a_src", "L1_gnn_a_dst", "l1_ev")
            edge_scores(0, 8)
            softmax(0, 8)
            link(dve.memset(slots[:, :, D + 8:D + 9], 1.0))
            add_up(0, D + 9, 0, 8)
            link(dve.tensor_scalar(small[:, :, :], accum[:, :, D:D + 8], 1e-10, None, ALU.max))
            link(dve.reciprocal(small[:, :, :], small[:, :, :]))
            acc4 = accum[:, :, 0:D].rearrange("p t (h d) -> p t h d", h=8)
            link(dve.tensor_tensor(acc4, acc4, heads(small[:, :, :], 8, 32), ALU.mult))
            link(dve.tensor_tensor(accum[:, :, 0:D], accum[:, :, 0:D], all_rows(row("L1_gnn_bias")), ALU.add))
            link(dve.tensor_tensor(resid[:, :, :], resid[:, :, :], accum[:, :, 0:D], ALU.add))
            link(dve.tensor_scalar(deg[:, :, 0], accum[:, :, D + 8], 1.0, 1.0, ALU.add, ALU.max))
            dve.sem_inc(done("var_deg"), 1)
            layer_norm(1)
            dve.wait_ge(*count("std_deg", 1))
            dve.reciprocal(deg[:, :, 1], deg[:, :, 1]).then_inc(done("dinv"), 1)
            link(dve.memset(accum[:, :, :], 0.0))
            add_up(1, 64, None)
            g64 = accum[:, :, 0:64]
            link(dve.tensor_tensor(g64, g64, hrows[:, :, 0:64], ALU.add))
            link(dve.tensor_tensor(g64, g64, deg[:, :, 1:2].to_broadcast([P, NT, 64]), ALU.mult))
            link(dve.tensor_tensor(g64, g64, all_rows(row("L2_gnn_b_gcn", 64), 64), ALU.add))
            dve.tensor_scalar(g64, g64, 0.0, None, ALU.max).then_inc(done("gcn_out"), 1)
            dve.wait_ge(*count("gcnt_ev", NT))
            batch_norm("gcn", cols, 64, 1, "L2_gnn_g0", "L2_gnn_beta0")
            for k in (1, 2):
                node_scores(k, 4, f"L2_gnn_a_src{k}", f"L2_gnn_a_dst{k}", f"gat{k}_ev")
                edge_scores(k, 4)
                softmax(k, 4)
                add_up(k + 1, D + 8, k, 4)
                self_s, m = node_s[:, :, 12:16], small[:, :, 4:8]
                link(dve.tensor_scalar(small[:, :, 0:4], accum[:, :, D:D + 4], 1e-30, None, ALU.max))
                link(dve.reciprocal(small[:, :, 0:4], small[:, :, 0:4]))
                link(dve.tensor_tensor(m, accum[:, :, D + 4:D + 8], small[:, :, 0:4], ALU.mult))
                link(dve.tensor_scalar(small[:, :, 0:4], accum[:, :, D:D + 4], 0.0, None, ALU.is_gt))
                link(dve.tensor_tensor(m, m, self_s, ALU.subtract))
                link(dve.tensor_tensor(m, m, small[:, :, 0:4], ALU.mult))
                link(dve.tensor_scalar(small[:, :, 0:4], m, 0.0, -1.0, ALU.max, ALU.mult))
                dve.sem_inc(done(f"self_sub{k}"), 1)
                dve.wait_ge(*count(f"self_w{k}", 1))
                h4 = hrows[:, :, 0:D].rearrange("p t (h d) -> p t h d", h=4)
                a4 = accum[:, :, 0:D].rearrange("p t (h d) -> p t h d", h=4)
                link(dve.tensor_tensor(h4, h4, heads(small[:, :, 0:4], 4, 64), ALU.mult))
                link(dve.tensor_tensor(a4, a4, h4, ALU.add))
                link(dve.tensor_tensor(m, accum[:, :, D:D + 4], small[:, :, 0:4], ALU.add))
                link(dve.reciprocal(m, m))
                link(dve.tensor_tensor(a4, a4, heads(m, 4, 64), ALU.mult))
                dve.tensor_tensor(accum[:, :, 0:D], accum[:, :, 0:D], all_rows(row(f"L2_gnn_b{k}")), ALU.add).then_inc(done(f"gat_out{k}"), 1)
                dve.wait_ge(*count(f"gatt{k}_ev", NT))
                batch_norm(f"gat{k}", cols, P, 2, f"L2_gnn_g{k}", f"L2_gnn_beta{k}")
                for c in range(DC):
                    link(dve.tensor_scalar(cols[:, c, :], cols[:, c, :], bnsc[:, c, 0:1], bnsc[:, c, 1:2], ALU.mult, ALU.add))
                    dve.tensor_scalar(accum_t[:, c, :], cols[:, c, :], 0.0, None, ALU.min).then_inc(done(f"elu_neg{k}"), 1)
                for c in range(DC):
                    link(dve.tensor_scalar(cols[:, c, :], cols[:, c, :], 0.0, None, ALU.max))
                    dve.wait_ge(*count(f"elu_exp{k}", c + 1))
                    link(dve.scalar_tensor_tensor(cols[:, c, :], accum_t[:, c, :], -1.0, cols[:, c, :], ALU.add, ALU.add))
                dve.sem_inc(done("gat_in2" if k == 1 else "elu2"), 1)
            for t in range(NT):
                dve.wait_ge(*count("l2r_tp", t + 1))
                dve.tensor_tensor(resid[:, t, :], resid[:, t, :], ps[:, t % 4, 0:D], ALU.add).then_inc(done("l2r_ev"), 1)
            dve.wait_ge(*count("l2r_ev", NT))
            layer_norm(2)
            dve.wait_ge(*count("x3_ev", NT))
            for l in range(3):
                add_up(4 + l, D, None, transposed=True)
                dve.wait_ge(*count(f"gin_mm1_{l}_ev", 2 * len(NODE_CHUNKS)))
                batch_norm(f"gin{l}a", cols, P, 2, f"L3_gnn_l{l}_g1", f"L3_gnn_l{l}_be1")
                if l < 2:
                    dve.wait_ge(*count(f"gin_mm2_{l}_ev", 2 * len(NODE_CHUNKS)))
                    batch_norm(f"gin{l}b", accum_t, P, 2, f"L3_gnn_l{l}_g2", f"L3_gnn_l{l}_be2")
                    dve.wait_ge(*count(f"gin_h{l}", 1))
            link(dve.tensor_tensor(resid[:, :, :], resid[:, :, :], all_rows(row("L3_gnn_l2_b2")), ALU.add))
            for t in range(NT):
                dve.wait_ge(*count("gin_last_mm", t + 1))
                dve.tensor_tensor(resid[:, t, :], resid[:, t, :], ps[:, 4 + t % 4, 0:D], ALU.add).then_inc(done("gin_last_ev"), 1)
            dve.wait_ge(*count("gin_last_ev", NT))
            layer_norm(3)


def kernel(**inputs):
    import numpy as np
    import concourse.bacc as bacc
    from concourse.bass_utils import run_bass_kernel_spmd

    v = {k: np.ascontiguousarray(x) for k, x in inputs.items()}
    arrays = {}

    def tiles(x, fill, n):
        out = np.full((n * P,) + x.shape[1:], fill, x.dtype)
        out[:E] = x
        return out.reshape((n, P) + x.shape[1:])

    src, dst = v["src"].astype(np.int32), v["dst"].astype(np.int32)
    arrays["src2"] = tiles(src, NP - 1, ET)
    arrays["dst2"] = tiles(dst, NP - 1, ET)
    arrays["ew2"] = tiles(v["edge_weight"], 0, ET)
    attr = np.ones((ET, 4, P), np.float32)
    attr[:, 0:3, :] = tiles(v["edge_attr_3"], 0, ET).transpose(0, 2, 1)
    arrays["attr"] = attr.reshape(ET, 4 * P)
    arrays["attr_w"] = np.concatenate([v["L1_gnn_edge_W"].T, v["L1_gnn_edge_b"][None]], 0)
    xp = np.zeros((NP, D), np.float32)
    xp[:N] = v["x"]
    arrays["x_pad"] = xp
    arrays["x_cols"] = np.ascontiguousarray(xp.T)
    rows = np.zeros((len(ROWS), D), np.float32)
    for i, name in enumerate(ROWS):
        rows[i, :v[name].size] = v[name].reshape(-1)
    arrays["rows"] = np.ascontiguousarray(np.broadcast_to(rows, (P,) + rows.shape))
    vecs = np.zeros((P, len(COLS), 2), np.float32)
    for i, name in enumerate(COLS):
        f = v[name].reshape(-1, P).T if v[name].size == D else v[name].reshape(-1, 1)
        vecs[:f.shape[0], i, :f.shape[1]] = f
    arrays["vecs"] = vecs
    arrays["L1_gnn_W"] = np.ascontiguousarray(v["L1_gnn_W"].T)
    for name in ["L0_gnn_weight", "L2_gnn_W_gcn", "L2_gnn_W1", "L2_gnn_W2"] + [f"L3_gnn_l{l}_w{j}" for l in range(3) for j in (1, 2)]:
        arrays[name] = v[name]
    nc = bacc.Bacc("TRN2", target_bir_lowering=False, num_devices=1)
    aps = {k: nc.dram_tensor("in_" + k, x.shape, mybir.dt.from_np(x.dtype), kind="ExternalInput").ap() for k, x in arrays.items()}
    aps["out"] = nc.dram_tensor("out_0", (N, D), F32, kind="ExternalOutput").ap()
    build(nc, aps)
    r = run_bass_kernel_spmd(nc, [{"in_" + k: x for k, x in arrays.items()}], core_ids=[0])
    return r.results[0]["out_0"]
```

```python
from contextlib import ExitStack

import concourse.bass as bass
from concourse import mybir

P = 128
N = 3125
NT = 25
NP = NT * P
E = 50000
ET = 392
EB, EQ = 4, 98
S = ET + NT - 1
SB, SQ = 4, 104
UN, HU = 16, 8
AU = 32
D = 256
GW = 272
DC = D // P
BIG = 1.0e30
LN_EPS = 1e-5
BN_EPS = 1e-5
L0U, L0H = 16, 4
L0N = L0U // L0H
L0IT = S // L0U
L0K = S // L0H
QU = 4
AK = 2 * 32 + 3 * 4
TRASH = NP
NACC = 4
NODE_CHUNKS = [(c * 512, min(512, NP - c * 512)) for c in range((NP + 511) // 512)]
BN_CHUNKS = [(c * 512, min(512, N - c * 512)) for c in range((N + 511) // 512)]

F32 = mybir.dt.float32
I32 = mybir.dt.int32
BF16 = mybir.dt.bfloat16
ALU = mybir.AluOpType
ACT = mybir.ActivationFunctionType
AX = mybir.AxisListType

ROWS = ["L0_gnn_bias", "L1_gnn_a_src", "L1_gnn_a_dst", "L1_gnn_bias", "L2_gnn_a_src1", "L2_gnn_a_dst1", "L2_gnn_b1",
        "L2_gnn_a_src2", "L2_gnn_a_dst2", "L2_gnn_b2", "L3_gnn_l2_b2", "L2_gnn_b_gcn"]
COLS = ["L2_gnn_g1", "L2_gnn_beta1", "L2_gnn_g2", "L2_gnn_beta2"] + [
    f"L3_gnn_l{l}_{v}" for l in range(3) for v in ("b1", "g1", "be1", "b2", "g2", "be2") if l < 2 or v in ("b1", "g1", "be1")
] + ["L2_gnn_g0", "L2_gnn_beta0"]


def build(nc, a):
    with ExitStack() as ctx:
        def sb(name, shape, dt=F32):
            return ctx.enter_context(nc.sbuf_tensor(name, shape, dt))

        def sem(name):
            return ctx.enter_context(nc.semaphore(name))

        def dram(name, shape, dt=F32):
            return nc.dram_tensor(name, shape, dt).ap()

        shared_sb = sb("shared_sb", [P, UN * GW + 2 * NP])
        slots = shared_sb[:, 0:AU * GW].rearrange("p (u w) -> p u w", u=AU)
        cols = shared_sb[:, UN * GW:UN * GW + 2 * NP].rearrange("p (c n) -> p c n", c=2)
        resid = sb("resid", [P, NT, D])
        accum = sb("accum", [P, NT, GW])
        hrows = sb("hrows", [P, NT, GW])
        accum_t = accum[:, :, :].rearrange("p t w -> p (t w)")[:, 0:2 * NP].rearrange("p (c n) -> p c n", c=2)
        onehot = sb("onehot", [P, UN, P])
        alpha = sb("alpha", [P, S, 8])
        peak = sb("peak", [P, S, 8])
        src_x = sb("src_x", [P, S], I32)
        src_xf = sb("src_xf", [P, S])
        src_lo = sb("src_lo", [P, S])
        ew_x = sb("ew_x", [P, S])
        drel = sb("drel", [P, S])
        tn_i = sb("tn_i", [P, S], I32)
        te_i = sb("te_i", [SQ, SB], I32)
        reset_f = sb("reset_f", [SQ, SB, P])
        reset_r = sb("reset_r", [SQ, SB, P])
        with_first = sb("with_first", [SQ, SB, P])
        with_last = sb("with_last", [SQ, SB, P])
        carry_ok = sb("carry_ok", [8, S + 1])
        through_f = sb("through_f", [8, S])
        through_r = sb("through_r", [8, S])
        iota = sb("iota", [P, S])
        iota_p = sb("iota_p", [P, 1])
        iota_m = sb("iota_m", [P, 1])
        ident = sb("ident", [P, P])
        before = sb("before", [P, P])
        ones = sb("ones", [P, P])
        idx_a = sb("idx_a", [P, AU], I32)
        idx_b = sb("idx_b", [P, L0U], I32)
        node_s = sb("node_s", [P, NT, 16])
        small = sb("small", [P, NT, 8])
        deg = sb("deg", [P, NT, 2])
        weights = sb("weights", [P, 4, D])
        rows = sb("rows", [P, len(ROWS), D])
        vecs = sb("vecs", [P, len(COLS), 2])
        stats = sb("stats", [P, NT, 8])
        mv = sb("mv", [P, NT, 2])
        bnst = sb("bnst", [P, 2, len(BN_CHUNKS), 6])
        bnmv = sb("bnmv", [P, 2, 2])
        bnsc = sb("bnsc", [P, 2, 4])
        attr_w = sb("attr_w", [AK, D])
        attr_wb = sb("attr_wb", [AK, D], BF16)
        carry = sb("carry", [8, S + 2])
        carry2 = sb("carry2", [8, S])
        carry_c = sb("carry_c", [SQ, SB, 8])
        te_last_i = sb("te_last_i", [EQ, EB, 1], I32)
        te_last = sb("te_last", [EQ, EB])
        flat_s = shared_sb[:, 0:UN * GW]
        flat_o = onehot[:, :, :].rearrange("p u w -> p (u w)")
        attr_c = flat_s[0:AK, 0:QU * P].bitcast(BF16).rearrange("p (h k e) -> p h k e", h=2, k=QU)
        picked = flat_s[:, 2048:2048 + QU * NT * 8]
        lo_hot = flat_s[:, 2848:2848 + QU * NT].rearrange("p (u t) -> p u t", u=QU)
        as_now = flat_s[:, 2948:2948 + QU * 8].rearrange("p (u h) -> p u h", u=QU)
        apart = flat_s[:, 3072:3072 + 2 * QU * P].rearrange("p (h e) -> p h e", h=2)
        hot_t = flat_o.rearrange("p (h n e) -> p h n e", h=2, n=2)
        hot_b = flat_o[:, 0:2 * QU * P].bitcast(BF16).rearrange("p (h n e) -> p h n e", h=2, n=2)
        enc = accum[:, 0:16, 0:D]
        segs = accum[0:SQ, :, :].rearrange("p t w -> p (t w)")[:, 0:8 * SB * P].rearrange("p (h b e) -> p h b e", h=8, b=SB)
        flat_a = accum[:, :, :].rearrange("p t w -> p (t w)")
        flat_h = hrows[:, :, :].rearrange("p t w -> p (t w)")
        wide = flat_a[:, 16 * GW:16 * GW + UN * P].bitcast(BF16).rearrange("p (q n e) -> p q n e", q=UN // QU, n=2)
        node_b = flat_a[:, 0:3 * NT * 8].bitcast(BF16).rearrange("p (m t h) -> p m t h", m=3, t=NT)
        rest = flat_a[:, 3 * NT * 8:3 * NT * 8 + NT * 16].rearrange("p (t h) -> p t h", t=NT)
        key = flat_h[0:SQ, 0:SB * P].rearrange("p (b e) -> p b e", b=SB)
        srow = flat_h[0:SQ, 512:1024].rearrange("p (b e) -> p b e", b=SB)
        drow = flat_h[0:SQ, 1024:1536].rearrange("p (b e) -> p b e", b=SB)
        key_i = flat_h[0:SQ, 1536:2048].rearrange("p (b e) -> p b e", b=SB).bitcast(I32)
        hi_b = flat_a[0:SQ, 0:256].bitcast(BF16).rearrange("p (b e) -> p b e", b=SB)
        drow_b = flat_a[0:SQ, 256:512].bitcast(BF16).rearrange("p (b e) -> p b e", b=SB)
        hi_i = flat_a[0:SQ, 512:1024].rearrange("p (b e) -> p b e", b=SB).bitcast(I32)
        ew_g = flat_a[0:SQ, 1024:1536].rearrange("p (b e) -> p b e", b=SB)
        srow_i = flat_h[0:SQ, 2048:2560].rearrange("p (b e) -> p b e", b=SB).bitcast(I32)
        attr_g = flat_h[0:SQ, 2560:4608].rearrange("p (b e) -> p b e", b=SB)
        attr_b = flat_a[0:SQ, 3072:3072 + SB * 6 * P].bitcast(BF16).rearrange("p (b m e) -> p b m e", b=SB, m=3)
        mask_t = flat_h[0:EQ, 4608:4608 + EB * S].rearrange("p (b s) -> p b s", b=EB)
        tmp = flat_a[:, 0:2048]
        edge_keys = flat_h[0:SQ, 6272:6272 + 2 * SB * 8].rearrange("p (n b e) -> p n b e", n=2, b=SB)
        neigh_t = flat_h[:, 0:2 * NP].rearrange("p (c n) -> p c n", c=2)
        l0 = resid[:, :, :].rearrange("p t d -> p (t d)")
        wide0 = flat_a[:, 2048:2560].bitcast(BF16).rearrange("p (h e) -> p h e", h=2)
        hot_t0 = flat_o[:, 0:1024].rearrange("p (h e) -> p h e", h=2)
        wide_src = flat_a[:, 3072:3072 + 2 * L0H * P].rearrange("p (h e) -> p h e", h=2)
        lo_i = flat_a[:, 2560:2560 + S].bitcast(I32)
        eq = l0[:, 0:2 * L0H * P].rearrange("p (u e) -> p u e", u=2 * L0H)
        msg = l0[:, 1024:1024 + L0U * D].rearrange("p (u e) -> p u e", u=L0U)
        cnt = l0[:, 5632:5632 + L0H]
        l0d = l0[:, 5640:5640 + L0H]
        l0m = l0[:, 5648:5648 + L0H]
        trash_p = l0[:, 5656:5657]
        pre4 = l0[:, 5660:5664]

        ps = ctx.enter_context(nc.psum_tensor("ps", [P, 8, 512], F32))

        table = [dram(f"table{k}", (NP, D)) for k in range(7)]
        t_gcn = dram("t_gcn", (NP, 64))
        t_hi = dram("t_hi", (S, P), BF16)
        t_drel = dram("t_drel", (S, P), BF16)
        t_src = dram("t_src", (S, P))
        t_neigh = [dram(f"t_neigh{k}", (NP + P, D)) for k in range(NACC)]
        t_attr = dram("t_attr", (S, 12 * P), BF16)

        gath = [sem(f"gath{u}") for u in range(AU)]
        wide_in = [sem(f"wide_in{q}") for q in range(UN // QU)]
        src_in = [sem(f"src_in{h}") for h in range(2)]
        wide0_in = [sem(f"wide0_in{h}") for h in range(2)]
        idx_ready = sem("idx_ready")
        msg_ready = sem("msg_ready")
        oh_ready = sem("oh_ready")
        step_mm = sem("step_mm")
        step_acc = sem("step_acc")
        dv = sem("dv")
        scat = [sem(f"scat{k}") for k in range(NACC)]
        attr_in = [sem(f"attr_in{h}") for h in range(2)]

        def runs(end, *names):
            return [(n + end, c) for n, c in names]

        def by_layer(name, *counts):
            return [(f"{name}{k}", c) for k, c in enumerate(counts)]

        turns = [(n, NT) for n in ("l0n", "x1", "x2", "gcnt", "gatt1", "gatt2", "l2r", "x3", "gint0", "gint1")]
        products = [(n, NT) for n in ("l0", "l1", "gcn", "gat1", "gat2", "gin_last")]
        gin = [(n, 2 * len(NODE_CHUNKS)) for n in ("gin_mm1_0", "gin_mm2_0", "gin_mm1_1", "gin_mm2_1", "gin_mm1_2")]
        norms = [(n, 1) for n in ("gcn", "gat1", "gat2", "gin0a", "gin0b", "gin1a", "gin1b", "gin2a")]
        rooted = [(n, 1) for n in ("ln0", "deg", "ln1", "bn_gcn", "bn_gat1", "bn_gat2", "ln2", "bn_gin0a", "bn_gin0b",
                                   "bn_gin1a", "bn_gin1b", "bn_gin2a", "ln3")]
        shared = [runs("_tp", *turns), runs("_ev", *turns), runs("_mm", *products), runs("_ev", *products),
                  gin, runs("_ev", *gin), [("var_" + n, c) for n, c in rooted], [("std_" + n, c) for n, c in rooted],
                  [("bnsc_" + n, c) for n, c in norms],
                  by_layer("al_t", 8, 4, 4), by_layer("scan_f", 8, 4, 4), by_layer("scan_r", 8, 4, 4), by_layer("peak_t", 8, 4, 4),
                  by_layer("peak_ev", 8, 4, 4), by_layer("ends", 2, 2, 2), by_layer("carried", 2, 2, 2), by_layer("carry_t", 2, 2, 2),
                  by_layer("segs_done", 1, 1, 1), by_layer("lrelu", 1, 1, 1), by_layer("alpha_sub", 1, 1, 1), by_layer("exp", 1, 1, 1),
                  by_layer("scores", 1, 1, 1), by_layer("ln", 1, 1, 1, 1), by_layer("gin_z", 1, 1, 1), by_layer("gin_h", 1, 1),
                  [(f"elu_neg{k}", 2) for k in (1, 2)], [(f"elu_exp{k}", 2) for k in (1, 2)],
                  [(f"{n}{k}", 1) for k in (1, 2) for n in ("gat_in", "self_sub", "gat_out")] + [("elu2", 1)],
                  [("self_w1", 1), ("self_w2", 1)]]
        stage = {}
        for group in shared:
            base, signal = 0, sem("s_" + group[0][0])
            for name, n in group:
                stage[name] = (signal, base)
                base += n

        def done(name):
            if name not in stage:
                stage[name] = (sem("s_" + name), 0)
            return stage[name][0]

        def count(name, n):
            return done(name), stage[name][1] + n

        block = ctx.enter_context(nc.Block())

        IDX = {n: i for i, n in enumerate(ROWS)}
        COL = {n: i for i, n in enumerate(COLS)}

        def gath_base(g):
            return 16 * (S // AU) * g

        def row(name, w=D):
            return rows[:, IDX[name], 0:w]

        def vec(name, c, p=P):
            return vecs[0:p, COL[name], c:c + 1]

        roots = {f"ln{k}": (small[:, :, 0], small[:, :, 1]) for k in range(4)}
        roots["deg"] = (deg[:, :, 0], deg[:, :, 1])
        for n in ["gat1", "gat2"] + [f"gin{l}{w}" for l in range(3) for w in "ab"]:
            roots[f"bn_{n}"] = (bnsc[:, :, 2], bnsc[:, :, 3])
        roots["bn_gcn"] = (bnsc[0:64, 0:1, 2], bnsc[0:64, 0:1, 3])

        @block.sync
        def _(sp):
            def put(dst, src, s, **how):
                sp.dma_start(dst, src, **how).then_inc(s, 16)

            put(te_last_i[:, :, :], a["dst2"].rearrange("(b q) e -> q b e", b=EB)[:, :, P - 1:P], done("ld_last"), allow_slow_non_contiguous=True)
            put(rows[:, :, :], a["rows"], done("ld_rows"))
            put(vecs[:, :, :], a["vecs"], done("ld_vecs"))
            put(attr_w[:, :], a["attr_w"], done("ld_attrw"))
            put(weights[:, :, :], a["L0_gnn_weight"].rearrange("(c p) n -> p c n", p=P), done("ld_w0"))
            put(cols[:, :, :], a["x_cols"].rearrange("(c p) n -> p c n", p=P), done("ld_x"))
            sp.wait_ge(*count("zeroed", 1))
            for k in range(NACC):
                for c in range((NP + P) // P):
                    put(t_neigh[k][c * P:(c + 1) * P, :], flat_a[:, 6400:6400 + D], done("zero_tab"))
            sp.wait_ge(*count("keys", 1))
            put(t_hi.rearrange("(b q) e -> q b e", b=SB), hi_b, done("rows_out"))
            put(t_drel.rearrange("(b q) e -> q b e", b=SB), drow_b, done("rows_out"))
            sp.wait_ge(*count("attr_split", 1))
            put(t_attr.rearrange("(b q) e -> q b e", b=SB), attr_b.rearrange("p b m e -> p b (m e)"), done("attr_out"))
            sp.wait_ge(*count("attr_out", 16))
            put(t_src.rearrange("(b q) e -> q b e", b=SB), srow, done("rows_out"))
            sp.wait_ge(*count("rows_out", 48))
            sp.wait_ge(*count("pre", 1))
            put(hrows[:, :, 0:D], a["x_pad"].rearrange("(t p) d -> p t d", p=P), done("ld_xh"))

            def on_each(t, first, n):
                return t[bass.ds(first, n), :].rearrange("s e -> (s e)").unsqueeze(0).to_broadcast([P, n * P])

            with sp.Fori(0, L0IT) as i:
                for q in range(L0N):
                    k, h = L0N * i + q, q % 2
                    sp.wait_ge(*count("l0_hot", k + 1))
                    sp.wait_ge(*count("l0_eq", k + 1))
                    sp.dma_start(wide0[:, h, :], on_each(t_drel, i * L0U + q * L0H, L0H)).then_inc(wide0_in[h], 16)
                    sp.dma_start(wide_src[:, h, :], on_each(t_src, i * L0U + q * L0H, L0H)).then_inc(src_in[h], 16)
            for k in range(NACC):
                sp.wait_ge(*count("l0_scat_all", 1))
                if k >= 2:
                    sp.wait_ge(*count("l0_summed", k - 1))
                into = [flat_a[:, 0:NT * D], flat_h[:, 0:NT * D]][min(k, 1)] if k < 2 else flat_h[:, 0:NT * D]
                put(into.rearrange("p (t d) -> p t d", t=NT), t_neigh[k][0:NP, :].rearrange("(t p) d -> p t d", p=P), done(f"ld_neigh{k}"))
            for name, n in (("l0_pre", L0K + 2), ("l0_msg", L0K + 2), ("l0_sidx", L0K)):
                sp.wait_ge(*count(name, n))
            put(resid[:, :, :], a["x_pad"].rearrange("(t p) d -> p t d", p=P), done("ld_xrow"))
            sp.wait_ge(*count("l0_mm", NT))
            put(weights[:, 0:2, :], a["L1_gnn_W"].rearrange("(c p) n -> p c n", p=P), done("ld_w1"))

            def put_table(k):
                sp.wait_ge(*count(["l1_ev", "gat1_ev", "gat2_ev"][k], NT))
                put(table[k].rearrange("(t p) d -> p t d", p=P), hrows[:, :, 0:D], done(f"table{k}"))
            def score_rows(k):
                sp.wait_ge(*count(f"scores{k}", 1))
                with sp.Fori(0, S // UN) as i:
                    for q in range(UN // QU):
                        n = 4 * (S // UN) * k + 4 * i + q
                        sp.wait_ge(*count("hot_s", n + 1))
                        sp.wait_ge(*count("hot_t", n + 1))
                        for j, t in enumerate((t_hi, t_drel)):
                            sp.dma_start(wide[:, q, j, :], on_each(t, i * UN + q * QU, QU)).then_inc(wide_in[q], 16)
                        if k == 0:
                            sp.wait_ge(*count("enc_free", 4 * i + q + 1))
                            for b in range(3):
                                sp.dma_start(attr_c[32 * b:32 * b + 12, q % 2, :, :],
                                             t_attr.rearrange("s (r e) -> r s e", r=12)[:, bass.ds(i * UN + q * QU, QU), :]
                                             ).then_inc(attr_in[q % 2], 16)

            put_table(0)
            score_rows(0)
            sp.wait_ge(*count("l1_mm", NT))
            put(weights[:, 2:4, 0:64], a["L2_gnn_W_gcn"].rearrange("(c p) n -> p c n", p=P), done("ld_gcn"))
            sp.wait_ge(*count("gcn_ev", NT))
            put(t_gcn.rearrange("(t p) d -> p t d", p=P), hrows[:, :, 0:64], done("table_gcn"))
            put(weights[0:64, 0, :], a["L2_gnn_W1"], done("ld_gat1"))
            put_table(1)
            score_rows(1)
            sp.wait_ge(*count("gcn_mm", NT))
            put(weights[:, 2:4, :], a["L2_gnn_W2"].rearrange("(c p) n -> p c n", p=P), done("ld_gat2"))
            put_table(2)
            score_rows(2)
            for l in range(3):
                if l == 0:
                    sp.wait_ge(*count("ln2", 1))
                    put(table[3].rearrange("(t p) d -> p t d", p=P), resid[:, :, :], done("table3"))
                    sp.wait_ge(*count("gat2_mm", NT))
                else:
                    sp.wait_ge(*count(f"gint{l - 1}_ev", NT))
                    put(table[3 + l].rearrange("(t p) d -> p t d", p=P), hrows[:, :, 0:D], done(f"table{3 + l}"))
                    sp.wait_ge(*count(f"gin_mm2_{l - 1}", 2 * len(NODE_CHUNKS)))
                put(weights[:, 0:2, :], a[f"L3_gnn_l{l}_w1"].rearrange("(c p) n -> p c n", p=P), done(f"ld_gin{l}"))
                put(weights[:, 2:4, :], a[f"L3_gnn_l{l}_w2"].rearrange("(c p) n -> p c n", p=P), done(f"ld_gin{l}"))
            sp.wait_ge(*count("ln3", 1))
            whole = N // P
            put(a["out"][0:whole * P, :].rearrange("(t p) d -> p t d", p=P), resid[:, 0:whole, :], done("out"))
            put(a["out"][whole * P:N, :], resid[0:N - whole * P, whole, :], done("out"))
            sp.wait_ge(*count("out", 32))

        @block.gpsimd
        def _(pool):
            pool.memset(flat_a[:, 6400:6400 + D], 0.0).then_inc(done("zeroed"), 1)
            pool.iota(iota[:, :], [[1, S]], 0, 0, allow_small_or_imprecise_dtypes=True).then_inc(done("iota"), 1)
            pool.iota(iota_p[:, :], [[0, 1]], 0, 1, allow_small_or_imprecise_dtypes=True).then_inc(done("iota"), 1)
            pool.memset(ones[:, :], 1.0).then_inc(done("iota"), 1)
            pool.memset(node_s[:, :, :], 0.0).then_inc(done("iota"), 1)
            pool.wait_ge(*count("te", 1))
            for b in range(SB):
                at = bass.IndirectOffsetOnAxis(ap=te_i[:, b:b + 1], axis=0)
                pool.indirect_dma_start(key_i[:, b, :], None, a["dst2"], at).then_inc(done("key_rows"), 16)
                pool.indirect_dma_start(srow_i[:, b, :], None, a["src2"], at).then_inc(done("src_rows"), 16)
                pool.indirect_dma_start(ew_g[:, b, :], None, a["ew2"], at).then_inc(done("ew_rows"), 16)
                pool.indirect_dma_start(attr_g[:, b, :], None, a["attr"], at).then_inc(done("attr_rows"), 16)

            pool.sem_inc(done("hot_s"), UN // QU)
            pool.sem_inc(done("hot_t"), UN // QU)
            def l0_scatter(k, q, first=False):
                pool.wait_ge(*count("l0_evac", k + 3))
                pool.wait_ge(*count("l0_sidx", k + 1))
                for u in range(L0H):
                    if not first:
                        pool.wait_ge(scat[u], 16 * k)
                    pool.sem_inc(done("l0_prev" if u == L0H - 1 else "pool_go"), 1)
                    pool.indirect_dma_start(t_neigh[u], bass.IndirectOffsetOnAxis(ap=idx_b[:, q * L0H + u:q * L0H + u + 1], axis=0),
                                            msg[:, q * L0H + u, :], None, compute_op=ALU.add).then_inc(scat[u], 16)

            pool.sem_inc(done("l0_prev"), 3)
            pool.wait_ge(*count("zero_tab", 16 * NACC * (NT + 1)))
            l0_scatter(0, 0, first=True)
            with pool.Fori(0, L0IT - 1) as i:
                for q in range(1, L0N + 1):
                    l0_scatter(L0N * i + q, q % L0N)
            for q in range(1, L0N):
                l0_scatter(L0N * (L0IT - 1) + q, q)
            for u in range(L0H):
                pool.wait_ge(scat[u], 16 * L0K)
            pool.sem_inc(done("l0_scat_all"), 1)

            def one_hots(k):
                with pool.Fori(0, S // UN) as i:
                    for q in range(UN // QU):
                        n = 4 * (S // UN) * k + 4 * i + q
                        pool.wait_ge(wide_in[q], 32 * ((S // UN) * k + i + 1))
                        pool.wait_ge(*count("dst_mm", n + 1))
                        pool.sem_inc(done("pool_go"), 1)
                        if k == 0:
                            pool.tensor_scalar(hot_t[:, q % 2, 0, :], wide[:, q, 0, :], iota_p[:, :], None, ALU.is_equal).then_inc(done("hot_s"), 1)
                        pool.tensor_scalar((hot_t if k == 0 else hot_b)[:, q % 2, 1, :], wide[:, q, 1, :], iota_p[:, :], None, ALU.is_equal).then_inc(done("hot_t"), 1)

            def gathers(g, tab, w, ready, n):
                pool.wait_ge(*count(ready, n))
                with pool.Fori(0, S // AU) as i:
                    for h in range(AU // HU):
                        pool.wait_ge(idx_ready, (S // HU) * g + 4 * i + h + 1)
                        pool.sem_inc(done("pool_go"), 1)
                        for u in range(h * HU, h * HU + HU):
                            pool.indirect_dma_start(slots[:, u, 0:w], None, tab,
                                                    bass.IndirectOffsetOnAxis(ap=idx_a[:, u:u + 1], axis=0)).then_inc(gath[u], 16)

            one_hots(0)
            gathers(0, table[0], D, "table0", 16)
            gathers(1, t_gcn, 64, "table_gcn", 16)
            for k in (1, 2):
                one_hots(k)
                gathers(k + 1, table[k], D, f"table{k}", 16)
            for l in range(3):
                gathers(4 + l, table[3 + l], D, f"table{3 + l}", 16)

        @block.tensor
        def _(pe):
            pe.sem_inc(step_mm, AU)
            pe.sem_inc(done("l0_pre"), 2)
            pe.sem_inc(done("enc_free"), 2)
            pe.sem_inc(done("src_mm"), 2)
            pe.sem_inc(done("dst_mm"), 2)
            pe.sem_inc(done("l0_x"), 2)
            tn_regs = [pe.alloc_register(f"pe_tn{u}") for u in range(UN)]

            def tiles_of(first, n):
                pe.load(tn_regs[0:n], tn_i[0:1, bass.ds(first, n)])
                return [pe.snap(r, min_val=0, max_val=NT - 1) for r in tn_regs[0:n]]

            def turn(name, t_count, f_in, p_out, src, free_after):
                for t in range(t_count):
                    if t >= 4:
                        pe.wait_ge(*count(name + "_ev", t - 3))
                    for c in range(max(1, f_in // P)):
                        w = min(f_in, P)
                        last = pe.transpose(ps[0:w, t % 4, c * P:c * P + P], src(t, c), ident[:, :])
                    last.then_inc(done(name + "_tp"), 1)

            pe.wait_ge(*count("step_mask", EB))
            pe.wait_ge(*count("iota", 4))
            for b in range(EB):
                mm = pe.matmul(ps[:, 0, 0:S], ones[0:EQ, :], mask_t[:, b, :], start=(b == 0), stop=(b == EB - 1))
            for o in range(SB):
                for b in range(EB):
                    mm = pe.matmul(ps[0:SQ, 1, o:o + 1], mask_t[:, b, o * SQ:(o + 1) * SQ], ones[0:EQ, 0:1],
                                   start=(b == 0), stop=(b == EB - 1))
            mm.then_inc(done("te_ps"), 1)
            pe.wait_ge(*count("keys", 1))
            pe.wait_ge(*count("ew_rows", 16 * SB))
            for n, t in enumerate((srow, ew_g, drow)):
                for b in range(SB):
                    mm = pe.transpose(ps[:, 2 + n, b * SQ:(b + 1) * SQ], t[:, b, :], ident[0:SQ, 0:SQ])
            for n in range(2):
                for b in range(SB):
                    mm = pe.matmul(ps[0:8, 5 + n, b * SQ:(b + 1) * SQ], edge_keys[:, n, b, :], ident[0:SQ, 0:SQ], start=True, stop=True)
            mm.then_inc(done("steps_ps"), 1)

            pe.wait_ge(*count("pre", 1))

            def l0_x(k, h):
                at = tiles_of(k * L0H, L0H)
                pe.wait_ge(*count("l0_hot", k + 3))
                pe.wait_ge(*count("l0_msg", k + 1))
                for u in range(L0H):
                    mm = pe.matmul(ps[:, 2 * h + u // 2, (u % 2) * D:(u % 2) * D + D], hot_t0[:, h, u * P:(u + 1) * P],
                                   hrows[:, bass.ds(at[u], 1), 0:D], start=True, stop=True)
                mm.then_inc(done("l0_x"), 1)

            def l0_sums(k, h):
                pe.wait_ge(*count("l0_eq", k + 3))
                pe.wait_ge(*count("l0_msg", k + 3))
                pe.wait_ge(*count("l0_evac", k + 1))
                for u in range(L0H):
                    mm = pe.matmul(ps[:, 4 + 2 * h + u // 2, (u % 2) * D:(u % 2) * D + D], eq[:, h * L0H + u, :],
                                   slots[:, h * L0H + u, 0:D], start=True, stop=True)
                mm.then_inc(done("l0_pre"), 1)

            def l0_quarter(k, q):
                if q < L0N:
                    l0_x(k + 1, (q + 1) % 2)
                l0_sums(k, q % 2)

            pe.wait_ge(*count("ld_xh", 16))
            l0_x(0, 0)
            with pe.Fori(0, L0IT - 1) as i:
                for q in range(L0N):
                    l0_quarter(L0N * i + q, q)
            for q in range(L0N):
                l0_quarter(L0K - L0N + q, q if q < L0N - 1 else L0N + 1)
            pe.wait_ge(*count("l0_evac", L0K + 2))
            pe.wait_ge(*count("l0_summed", NACC - 1))
            turn("l0n", NT, D, P, lambda t, c: flat_a[:, t * D + c * P:t * D + c * P + P], 0)
            pe.wait_ge(*count("l0n_ev", NT))
            pe.wait_ge(*count("ld_x", 16))
            pe.wait_ge(*count("ld_w0", 16))
            for t in range(NT):
                if t >= 4:
                    pe.wait_ge(*count("l0_ev", t - 3))
                n0 = t * P
                for c in range(DC):
                    pe.matmul(ps[:, 4 + t % 4, 0:D], cols[:, c, n0:n0 + P], weights[:, c, :], start=(c == 0), stop=False)
                for c in range(DC):
                    mm = pe.matmul(ps[:, 4 + t % 4, 0:D], neigh_t[:, c, n0:n0 + P], weights[:, DC + c, :], start=False, stop=(c == DC - 1))
                mm.then_inc(done("l0_mm"), 1)

            def turn_resid(name, ready):
                pe.wait_ge(*count(ready, 1))
                turn(name, NT, D, P, lambda t, c: resid[:, t, c * P:c * P + P], 0)
                pe.wait_ge(*count(name + "_ev", NT))

            def node_rows(name, chunks, p, w, wait, n):
                pe.wait_ge(*count(wait, n))
                for t in range(NT):
                    if t >= 4:
                        pe.wait_ge(*count(name + "_ev", t - 3))
                    for j, c in enumerate(chunks):
                        mm = pe.matmul(ps[:, 4 + t % 4, 0:w], cols[0:p, j, t * P:(t + 1) * P], weights[0:p, c, 0:w],
                                       start=(j == 0), stop=(j == len(chunks) - 1))
                    mm.then_inc(done(name + "_mm"), 1)
                pe.wait_ge(*count(name + "_ev", NT))

            def look_up(k, H):
                pe.wait_ge(*count(f"scores{k}", 1))
                ahead = 2 if k == 0 else 1
                with pe.Fori(0, S // UN) as i:
                    at = tiles_of(i * UN, UN)
                    for q in range(UN // QU):
                        n = 4 * (S // UN) * k + 4 * i + q
                        pe.wait_ge(*count("hot_s", n + 1 + UN // QU))
                        pe.wait_ge(*count("src_used", n + ahead))
                        for j in range(QU):
                            out = ps[:, j // 2, (j % 2) * NT * H:(j % 2 + 1) * NT * H] if k == 0 else ps[:, q % 2, j * NT * H:(j + 1) * NT * H]
                            if k == 0:
                                mm = pe.matmul(out, hot_t[:, q % 2, 0, j * P:(j + 1) * P], node_s[:, :, 0:H], start=True, stop=True)
                                continue
                            for m in range(3):
                                mm = pe.matmul(out, hot_b[:, q % 2, 0, j * P:(j + 1) * P], node_b[:, m, :, 0:H], start=(m == 0), stop=(m == 2))
                        mm.then_inc(done("src_mm"), 1)
                        if k == 0:
                            pe.wait_ge(attr_in[q % 2], 48 * (2 * i + q // 2 + 1))
                            pe.wait_ge(*count("enc_done", 4 * i + q + 2))
                            for j in range(QU):
                                mm = pe.matmul(ps[:, 2 + j // 2, (j % 2) * D:(j % 2) * D + D], attr_c[:, q % 2, j, :], attr_wb[:, :],
                                               start=True, stop=True)
                            mm.then_inc(done("enc_free"), 1)
                        pe.wait_ge(*count("hot_t", n + 1 + UN // QU))
                        pe.wait_ge(*count("dst_used", n + ahead))
                        for j in range(QU):
                            hot = (hot_t if k == 0 else hot_b)[:, q % 2, 1, j * P:(j + 1) * P]
                            if k == 0:
                                mm = pe.matmul(ps[:, 4 + j, 0:GW], hot, hrows[:, bass.ds(at[q * QU + j], 1), :], start=True, stop=True)
                            else:
                                for m in range(3):
                                    mm = pe.matmul(ps[:, 2 + q % 2, 8 * j:8 * j + 8], hot, node_b[:, m, bass.ds(at[q * QU + j], 1), 8:16],
                                                   start=(m == 0), stop=(m == 2))
                        mm.then_inc(done("dst_mm"), 1)
                pe.wait_ge(*count("dst_used", 4 * (S // UN) * (k + 1) + 2))

            def max_segments(k, H):
                pe.wait_ge(*count(f"lrelu{k}", 1))
                for h in range(H):
                    if h >= 4:
                        pe.wait_ge(*count(f"scan_f{k}", h - 3))
                    for b in range(SB):
                        mm = pe.transpose(ps[0:SQ, h % 4, b * P:(b + 1) * P], alpha[:, b * SQ:(b + 1) * SQ, h], ident[:, :])
                    mm.then_inc(done(f"al_t{k}"), 1)
                for way, at in (("f", P - 1), ("r", 0)):
                    pe.wait_ge(*count(f"scan_{way}{k}", H))
                    for b in range(SB):
                        mm = pe.transpose(ps[0:H, 4, b * SQ:(b + 1) * SQ], segs[:, 0:H, b, at], ident[0:SQ, 0:SQ])
                    mm.then_inc(done(f"ends{k}"), 1)
                    pe.wait_ge(*count(f"carried{k}", 1 if way == "f" else 2))
                    for b in range(SB):
                        mm = pe.transpose(ps[0:SQ, 5, b * 8:b * 8 + H], carry2[0:H, b * SQ:(b + 1) * SQ], ident[0:H, 0:H])
                    mm.then_inc(done(f"carry_t{k}"), 1)
                pe.wait_ge(*count(f"segs_done{k}", 1))
                for h in range(H):
                    if h >= 4:
                        pe.wait_ge(*count(f"peak_ev{k}", h - 3))
                    for b in range(SB):
                        mm = pe.transpose(ps[:, h % 4, b * SQ:(b + 1) * SQ], segs[:, h, b, :], ident[0:SQ, 0:SQ])
                    mm.then_inc(done(f"peak_t{k}"), 1)
                pe.wait_ge(*count(f"peak_ev{k}", H))

            def add_up(g, w, weighted, transposed=False):
                with pe.Fori(0, S // AU) as i:
                    for u in range(AU):
                        h = u // HU
                        if u % HU == 0:
                            pe.wait_ge(oh_ready, (S // HU) * g + 4 * i + h + 1)
                            if weighted is not None:
                                pe.wait_ge(msg_ready, (S // HU) * weighted + 4 * i + h + 1)
                        if weighted is None:
                            pe.wait_ge(gath[u], gath_base(g) + 16 * i + 16)
                        pe.wait_ge(step_acc, S * g + AU * i + u + 1)
                        if transposed:
                            for c in range(DC):
                                mm = pe.matmul(ps[:, u % 8, c * P:c * P + P], slots[:, u, c * P:c * P + P], onehot[:, u % UN, :],
                                               start=True, stop=True)
                        else:
                            mm = pe.matmul(ps[:, u % 8, 0:w], onehot[:, u % UN, :], slots[:, u, 0:w], start=True, stop=True)
                        mm.then_inc(step_mm, 1)
                pe.wait_ge(step_acc, S * (g + 1) + HU)

            turn_resid("x1", "ln0")
            node_rows("l1", (0, 1), P, D, "ld_w1", 16)
            pe.wait_ge(*count("ld_attrw", 16))
            look_up(0, 8)
            max_segments(0, 8)
            add_up(0, D + 9, 0)
            turn_resid("x2", "ln1")
            node_rows("gcn", (2, 3), P, 64, "ld_gcn", 16)
            add_up(1, 64, None)
            pe.wait_ge(*count("gcn_out", 1))
            turn("gcnt", NT, 64, 64, lambda t, c: accum[:, t, 0:64], 0)
            pe.wait_ge(*count("gcnt_ev", NT))
            for k in (1, 2):
                pe.wait_ge(*count(f"ld_gat{k}", 16))
                node_rows(f"gat{k}", (0,) if k == 1 else (2, 3), 64 if k == 1 else P, D, f"gat_in{k}", 1)
                look_up(k, 4)
                max_segments(k, 4)
                add_up(k + 1, D + 8, k)
                pe.wait_ge(*count(f"gat_out{k}", 1))
                turn(f"gatt{k}", NT, D, P, lambda t, c: accum[:, t, c * P:c * P + P], 0)
                pe.wait_ge(*count(f"gatt{k}_ev", NT))
            pe.wait_ge(*count("elu2", 1))
            turn("l2r", NT, D, P, lambda t, c: cols[:, c, t * P:(t + 1) * P], 0)
            pe.wait_ge(*count("l2r_ev", NT))
            turn_resid("x3", "ln2")
            for l in range(3):
                add_up(4 + l, D, None, transposed=True)
                pe.wait_ge(*count(f"ld_gin{l}", 32))

                def gin_mm(name, w0, src):
                    n = 0
                    for n0, w in NODE_CHUNKS:
                        for m in range(DC):
                            if n >= 4:
                                pe.wait_ge(*count(name + "_ev", n - 3))
                            for c in range(DC):
                                mm = pe.matmul(ps[:, 4 + n % 4, 0:w], weights[:, w0 + c, m * P:(m + 1) * P], src[:, c, n0:n0 + w],
                                               start=(c == 0), stop=(c == DC - 1))
                            mm.then_inc(done(name), 1)
                            n += 1
                    pe.wait_ge(*count(name + "_ev", n))

                gin_mm(f"gin_mm1_{l}", 0, accum_t)
                pe.wait_ge(*count(f"gin_z{l}", 1))
                if l < 2:
                    gin_mm(f"gin_mm2_{l}", 2, cols)
                    pe.wait_ge(*count(f"gin_h{l}", 1))
                    turn(f"gint{l}", NT, D, P, lambda t, c: accum_t[:, c, t * P:(t + 1) * P], 0)
                    pe.wait_ge(*count(f"gint{l}_ev", NT))
                else:
                    node_rows("gin_last", (2, 3), P, D, f"gin_z{l}", 1)

        @block.scalar
        def _(act):
            act.sem_inc(done("l0_evac"), 2)
            act.sem_inc(done("enc_done"), 2)

            act.wait_ge(*count("pre", 1))
            with act.Fori(0, L0IT) as i:
                for q in range(L0N):
                    k, h = L0N * i + q, q % 2
                    act.wait_ge(*count("l0_pre", k + 3))
                    act.wait_ge(*count("l0_prev", k + 1))
                    act.activation(msg[:, q * L0H:q * L0H + L0H, :].rearrange("p u d -> p (u d)"),
                                   ps[:, 4 + 2 * h:6 + 2 * h, :].rearrange("p b d -> p (b d)"), ACT.Copy).then_inc(done("l0_evac"), 1)

            def turned(name, n_tiles, p, c, dst):
                for t in range(n_tiles):
                    act.wait_ge(*count(name + "_tp", t + 1))
                    act.activation(dst[0:p, 0:c, t * P:(t + 1) * P], ps[0:p, t % 4, 0:c * P].rearrange("p (c n) -> p c n", c=c),
                                   ACT.Copy).then_inc(done(name + "_ev"), 1)

            def root(name):
                act.wait_ge(*count("var_" + name, 1))
                src, dst = roots[name]
                act.activation(dst, src, ACT.Sqrt).then_inc(done("std_" + name), 1)

            def rows_out(name, w, scale=None):
                for t in range(NT):
                    act.wait_ge(*count(name + "_mm", t + 1))
                    act.activation(hrows[:, t, 0:w], ps[:, 4 + t % 4, 0:w], ACT.Copy,
                                   scale=1.0 if scale is None else scale(t)).then_inc(done(name + "_ev"), 1)

            def encoded():
                with act.Fori(0, S // UN) as i:
                    for q in range(UN // QU):
                        act.wait_ge(*count("dst_used", 4 * i + q + 1))
                        act.wait_ge(*count("enc_free", 4 * i + q + 3))
                        act.activation(enc[:, q * QU:q * QU + QU, :], ps[:, 2:4, :].rearrange("p b (j d) -> p (b j) d", j=2),
                                       ACT.Relu).then_inc(done("enc_done"), 1)

            def src_one_hots(k):
                act.wait_ge(*count(f"scores{k}", 1))
                with act.Fori(0, S // UN) as i:
                    for q in range(UN // QU):
                        n = 4 * (S // UN) * k + 4 * i + q
                        act.wait_ge(wide_in[q], 32 * ((S // UN) * k + i + 1))
                        act.wait_ge(*count("src_mm", n + 1))
                        act.activation(apart[:, q % 2, :], wide[:, q, 0, :], ACT.Abs, bias=iota_m[:, :]).then_inc(done("apart"), 1)
                        act.wait_ge(*count("apart", 4 * (S // UN) * (k - 1) + 4 * i + q + 1))
                        act.activation(hot_b[:, q % 2, 0, :], apart[:, q % 2, :], ACT.Relu, bias=ones[:, 0:1], scale=-1.0).then_inc(done("hot_s"), 1)

            def indices(g):
                with act.Fori(0, S // AU) as i:
                    for h in range(AU // HU):
                        act.wait_ge(step_mm, S * g + AU * i + HU * h + HU)
                        act.activation(idx_a[:, h * HU:h * HU + HU], src_x[:, bass.ds(i * AU + h * HU, HU)],
                                       ACT.Copy).then_inc(idx_ready, 1)

            def weights_of(k, H):
                for h in range(H):
                    act.wait_ge(*count(f"peak_t{k}", h + 1))
                    act.activation(peak[:, :, h], ps[:, h % 4, 0:S], ACT.Copy).then_inc(done(f"peak_ev{k}"), 1)
                act.wait_ge(*count(f"alpha_sub{k}", 1))
                act.activation(alpha[:, :, 0:H], alpha[:, :, 0:H], ACT.Exp).then_inc(done(f"exp{k}"), 1)

            turned("l0n", NT, P, 2, neigh_t)
            root("ln0")
            turned("x1", NT, P, 2, cols)
            rows_out("l1", D)
            act.wait_ge(*count("scores0", 1))
            encoded()
            weights_of(0, 8)
            indices(0)
            root("deg")
            root("ln1")
            turned("x2", NT, P, 2, cols)
            act.wait_ge(*count("dinv", 1))
            rows_out("gcn", 64, lambda t: deg[:, t, 1:2])
            indices(1)
            turned("gcnt", NT, 64, 1, cols)
            root("bn_gcn")
            act.wait_ge(*count("bnsc_gcn", 1))
            act.activation(cols[0:64, 0, :], cols[0:64, 0, :], ACT.Identity, bias=bnsc[0:64, 0, 1:2],
                           scale=bnsc[0:64, 0, 0:1]).then_inc(done("gat_in1"), 1)
            for k in (1, 2):
                rows_out(f"gat{k}", D)
                src_one_hots(k)
                weights_of(k, 4)
                indices(k + 1)
                act.wait_ge(*count(f"self_sub{k}", 1))
                act.activation(small[:, :, 0:4], small[:, :, 0:4], ACT.Exp).then_inc(done(f"self_w{k}"), 1)
                turned(f"gatt{k}", NT, P, 2, cols)
                root(f"bn_gat{k}")
                for c in range(DC):
                    act.wait_ge(*count(f"elu_neg{k}", c + 1))
                    act.activation(accum_t[:, c, :], accum_t[:, c, :], ACT.Exp).then_inc(done(f"elu_exp{k}"), 1)
            root("ln2")
            turned("x3", NT, P, 2, accum_t)

            def biased(name, dst, bias):
                n = 0
                for n0, w in NODE_CHUNKS:
                    for m in range(DC):
                        act.wait_ge(*count(name, n + 1))
                        act.activation(dst[:, m, n0:n0 + w], ps[:, 4 + n % 4, 0:w], ACT.Identity,
                                       bias=vec(bias, m)).then_inc(done(name + "_ev"), 1)
                        n += 1

            def relu_scaled(name, buf, ready):
                act.wait_ge(*count("bnsc_" + name, 1))
                for c in range(DC):
                    last = act.activation(buf[:, c, :], buf[:, c, :], ACT.Relu, bias=bnsc[:, c, 1:2], scale=bnsc[:, c, 0:1])
                last.then_inc(done(ready), 1)

            for l in range(3):
                indices(4 + l)
                biased(f"gin_mm1_{l}", cols, f"L3_gnn_l{l}_b1")
                root(f"bn_gin{l}a")
                relu_scaled(f"gin{l}a", cols, f"gin_z{l}")
                if l < 2:
                    biased(f"gin_mm2_{l}", accum_t, f"L3_gnn_l{l}_b2")
                    root(f"bn_gin{l}b")
                    relu_scaled(f"gin{l}b", accum_t, f"gin_h{l}")
                    for t in range(NT):
                        act.wait_ge(*count(f"gint{l}_tp", t + 1))
                        act.activation(hrows[:, t, 0:D], ps[:, t % 4, 0:D], ACT.Copy).then_inc(done(f"gint{l}_ev"), 1)
            root("ln3")

        @block.vector
        def _(dve):
            chain = [0]

            def link(ins):
                chain[0] += 1
                ins.then_inc(dv, 1)
                dve.wait_ge(dv, chain[0])

            dve.sem_inc(step_acc, HU)
            for name, n in (("src_used", 2), ("dst_used", 2), ("l0_eq", 2), ("l0_msg", 2), ("l0_hot", 2)):
                dve.sem_inc(done(name), n)
            tn_regs = [dve.alloc_register(f"tn{u}") for u in range(HU)]

            dve.wait_ge(*count("iota", 4))
            link(dve.tensor_scalar(ident[:, :], iota[:, 0:P], iota_p[:, :], None, ALU.is_equal))
            link(dve.tensor_scalar(iota_m[:, :], iota_p[:, :], -1.0, None, ALU.mult))
            link(dve.tensor_scalar(before[:, :], iota[:, 0:P], iota_p[:, :], None, ALU.is_lt))
            dve.wait_ge(*count("ld_last", 16))
            link(dve.tensor_scalar(te_last_i[:, :, :], te_last_i[:, :, :], 7, None, ALU.logical_shift_right))
            link(dve.tensor_copy(te_last[:, :], te_last_i[:, :, 0]))
            for b in range(EB):
                link(dve.tensor_scalar(te_last[:, b:b + 1], te_last[:, b:b + 1], iota_p[0:EQ, :], float(EQ * b + 1), ALU.add, ALU.add))
                dve.tensor_scalar(mask_t[:, b, :], iota[0:EQ, :], te_last[:, b:b + 1], None, ALU.is_ge).then_inc(done("step_mask"), 1)
            dve.wait_ge(*count("te_ps", 1))
            dve.tensor_copy(te_i[:, :], ps[0:SQ, 1, 0:SB]).then_inc(done("te"), 1)
            link(dve.tensor_tensor(tn_i[:, :], iota[:, :], ps[:, 0, 0:S], ALU.subtract))
            for b in range(SB):
                link(dve.tensor_scalar(pre4[0:SQ, b:b + 1], ps[0:SQ, 1, b:b + 1], iota_p[0:SQ, :], float(-SQ * b), ALU.subtract, ALU.add))
            link(dve.tensor_scalar(pre4[0:SQ, :], pre4[0:SQ, :], float(P), None, ALU.mult))
            dve.wait_ge(*count("key_rows", 16 * SB))
            dve.wait_ge(*count("src_rows", 16 * SB))
            link(dve.tensor_copy(key, key_i))
            link(dve.tensor_copy(srow, srow_i))
            for b in range(SB):
                link(dve.tensor_scalar(drow[:, b, :], key[:, b, :], pre4[0:SQ, b:b + 1], None, ALU.add))
            link(dve.tensor_copy(drow_b, drow))
            link(dve.tensor_scalar(hi_i, srow_i, P - 1, None, ALU.bitwise_and))
            link(dve.tensor_copy(hi_b, hi_i))
            link(dve.tensor_copy(edge_keys[:, 0, :, :], key[:, :, 0:1].to_broadcast([SQ, SB, 8])))
            dve.tensor_copy(edge_keys[:, 1, :, :], key[:, :, P - 1:P].to_broadcast([SQ, SB, 8])).then_inc(done("keys"), 1)
            dve.wait_ge(*count("attr_rows", 16 * SB))
            for m in range(3):
                last = dve.tensor_copy(attr_b[:, :, m, :], attr_g)
                if m < 2:
                    link(last)
                    link(dve.tensor_tensor(attr_g, attr_g, attr_b[:, :, m, :], ALU.subtract))
            last.then_inc(done("attr_split"), 1)
            dve.wait_ge(*count("ld_attrw", 16))
            link(dve.tensor_copy(attr_wb[:, :], attr_w[:, :]))
            link(dve.tensor_tensor(attr_w[:, :], attr_w[:, :], attr_wb[:, :], ALU.subtract))
            dve.tensor_copy(attr_wb[32:64, :], attr_w[32:64, :])
            link(dve.tensor_copy(attr_wb[64:AK, :], attr_w[64:AK, :]))
            link(dve.tensor_tensor(attr_w[64:AK, :], attr_w[64:AK, :], attr_wb[64:AK, :], ALU.subtract))
            link(dve.tensor_copy(attr_wb[64:AK, :], attr_w[64:AK, :]))
            def barrier_of(out):
                link(dve.tensor_scalar(out, out, 1.0, BIG, ALU.subtract, ALU.mult))

            link(dve.memset(reset_f[:, :, 0:1], 0.0))
            link(dve.memset(reset_r[:, :, P - 1:P], 0.0))
            link(dve.tensor_tensor(reset_f[:, :, 1:P], key[:, :, 1:P], key[:, :, 0:P - 1], ALU.is_equal))
            barrier_of(reset_f[:, :, 1:P])
            link(dve.tensor_copy(reset_r[:, :, 0:P - 1], reset_f[:, :, 1:P]))
            for b in range(SB):
                link(dve.tensor_scalar(with_first[:, b, :], key[:, b, :], key[:, b, 0:1], None, ALU.is_equal))
                link(dve.tensor_scalar(with_last[:, b, :], key[:, b, :], key[:, b, P - 1:P], None, ALU.is_equal))
            barrier_of(with_first[:, :, :])
            barrier_of(with_last[:, :, :])
            dve.wait_ge(*count("steps_ps", 1))
            link(dve.tensor_copy(src_x[:, :], ps[:, 2, 0:S]))
            link(dve.tensor_copy(src_xf[:, 0:S], ps[:, 2, 0:S]))
            link(dve.tensor_copy(ew_x[:, :], ps[:, 3, 0:S]))
            link(dve.tensor_scalar(lo_i, src_x[:, :], 7, None, ALU.logical_shift_right))
            link(dve.tensor_copy(src_lo[:, :], lo_i))
            link(dve.tensor_copy(drel[:, :], ps[:, 4, 0:S]))
            link(dve.tensor_copy(carry[:, 0:S], ps[0:8, 5, 0:S]))
            link(dve.tensor_tensor(carry2[:, :], carry[:, 0:S], ps[0:8, 6, 0:S], ALU.is_equal))
            link(dve.memset(carry_ok[:, :], 0.0))
            link(dve.tensor_tensor(carry_ok[:, 1:S], carry[:, 1:S], ps[0:8, 6, 0:S - 1], ALU.is_equal))
            link(dve.tensor_tensor(through_f[:, :], carry_ok[:, 0:S], carry2[:, :], ALU.mult))
            link(dve.tensor_tensor(through_r[:, :], carry_ok[:, 1:S + 1], carry2[:, :], ALU.mult))
            barrier_of(carry_ok[:, :])
            barrier_of(through_f[:, :])
            barrier_of(through_r[:, :])
            dve.tensor_scalar(trash_p, iota_p[:, :], float(TRASH), None, ALU.add).then_inc(done("pre"), 1)
            dve.wait_ge(*count("pre", 1))

            def l0_hot(k, h):
                dve.wait_ge(wide0_in[h], 8 * (k - h) + 16)
                dve.wait_ge(*count("l0_x", k + 1))
                dve.tensor_scalar(hot_t0[:, h, :], wide0[:, h, :], iota_p[:, :], None, ALU.is_equal).then_inc(done("l0_hot"), 1)

            def l0_quarter(k, q, last=False):
                h = q % 2
                half = slice(h * L0H, h * L0H + L0H)
                now = bass.ds(k * L0H, L0H)
                if not last:
                    l0_hot(k + 1, 1 - h)
                dve.wait_ge(src_in[h], 8 * (k - h) + 16)
                dve.wait_ge(*count("l0_pre", k + 1))
                dve.tensor_tensor(eq[:, half, :], wide_src[:, h, :].rearrange("p (u e) -> p u e", u=L0H),
                                  src_xf[:, now].unsqueeze(2).to_broadcast([P, L0H, P]), ALU.is_equal).then_inc(done("l0_eq"), 1)
                dve.wait_ge(*count("l0_x", k + 3))
                for u in range(0, L0H, 2):
                    two = slice(h * L0H + u, h * L0H + u + 2)
                    msgs = dve.tensor_tensor(slots[:, two, 0:D], ps[:, 2 * h + u // 2, :].rearrange("p (j d) -> p j d", j=2),
                                             ew_x[:, bass.ds(k * L0H + u, 2)].unsqueeze(2).to_broadcast([P, 2, D]), ALU.mult)
                msgs.then_inc(done("l0_msg"), 1)
                dve.wait_ge(*count("l0_eq", k + 3))
                v = tmp[:, 0:L0H * P].rearrange("p (u e) -> p u e", u=L0H)
                dve.tensor_tensor(v, eq[:, half, :], before[:, :].unsqueeze(1).to_broadcast([P, L0H, P]), ALU.mult).then_inc(done("l0_dv"), 1)
                dve.wait_ge(*count("l0_dv", 4 * k + 1))
                dve.tensor_reduce(cnt, v, AX.X, ALU.add).then_inc(done("l0_dv"), 1)
                dve.tensor_scalar(l0d, src_xf[:, now], -1.0, trash_p, ALU.mult, ALU.add).then_inc(done("l0_dv"), 1)
                dve.wait_ge(*count("l0_dv", 4 * k + 3))
                dve.scalar_tensor_tensor(l0m, cnt, 1.0, l0d, ALU.min, ALU.mult).then_inc(done("l0_dv"), 1)
                dve.wait_ge(*count("l0_dv", 4 * k + 4))
                dve.wait_ge(*count("l0_prev", k + 1))
                dve.tensor_tensor(idx_b[:, q * L0H:q * L0H + L0H], l0m, src_xf[:, now], ALU.add).then_inc(done("l0_sidx"), 1)

            l0_hot(0, 0)
            with dve.Fori(0, L0IT - 1) as i:
                for q in range(L0N):
                    l0_quarter(L0N * i + q, q)
            for q in range(L0N):
                l0_quarter(L0K - L0N + q, q, last=(q == L0N - 1))

            sums = flat_a[:, 0:NT * D]
            for k in range(1, NACC):
                dve.wait_ge(*count(f"ld_neigh{k}", 16))
                if k == 1:
                    dve.wait_ge(*count("ld_neigh0", 16))
                else:
                    dve.wait_ge(*count("l0_summed", k - 1))
                dve.tensor_tensor(sums, sums, flat_h[:, 0:NT * D], ALU.add).then_inc(done("l0_summed"), 1)
            dve.wait_ge(*count("ld_xrow", 16))
            dve.wait_ge(*count("ld_rows", 16))
            all_rows = lambda v, w=D: v.unsqueeze(1).to_broadcast([P, NT, w])
            link(dve.tensor_tensor(resid[:, :, :], resid[:, :, :], all_rows(row("L0_gnn_bias")), ALU.add))
            for t in range(NT):
                dve.wait_ge(*count("l0_mm", t + 1))
                dve.tensor_tensor(resid[:, t, :], resid[:, t, :], ps[:, 4 + t % 4, 0:D], ALU.add).then_inc(done("l0_ev"), 1)
            dve.wait_ge(*count("l0_ev", NT))

            def layer_norm(k):
                for t in range(NT):
                    last = dve.bn_stats(stats[:, t, 0:6], resid[:, t, :])
                link(last)
                for t in range(NT):
                    last = dve.bn_aggr(mv[:, t, :], stats[:, t, 0:6])
                link(last)
                dve.tensor_scalar(small[:, :, 0], mv[:, :, 1], LN_EPS, None, ALU.add).then_inc(done(f"var_ln{k}"), 1)
                dve.wait_ge(*count(f"std_ln{k}", 1))
                link(dve.reciprocal(small[:, :, 2], small[:, :, 1]))
                for t in range(NT):
                    last = dve.tensor_scalar(resid[:, t, :], resid[:, t, :], mv[:, t, 0:1], small[:, t, 2:3], ALU.subtract, ALU.mult)
                last.then_inc(done(f"ln{k}"), 1)

            def node_scores(k, H, src_row, dst_row, name):
                dve.wait_ge(*count(name, NT))
                prod = flat_a[:, 0:NT * D].rearrange("p (t d) -> p t d", t=NT)
                for n, r in enumerate((src_row, dst_row)):
                    link(dve.tensor_tensor(prod, hrows[:, :, 0:D], all_rows(row(r)), ALU.mult))
                    link(dve.tensor_reduce(node_s[:, :, 8 * n:8 * n + H], prod.rearrange("p t (h d) -> p t h d", h=H), AX.X, ALU.add))
                if H == 8:
                    link(dve.memset(attr_c[:, :, :, :], 0.0))
                    dve.tensor_copy(hrows[:, :, D:D + 16], node_s[:, :, :]).then_inc(done(f"scores{k}"), 1)
                else:
                    link(dve.tensor_tensor(node_s[:, :, 12:16], node_s[:, :, 0:4], node_s[:, :, 8:12], ALU.add))
                    link(dve.scalar_tensor_tensor(node_s[:, :, 12:16], node_s[:, :, 12:16], 0.2, node_s[:, :, 12:16], ALU.mult, ALU.max))
                    link(dve.tensor_copy(node_b[:, 0, :, :], node_s[:, :, :]))
                    link(dve.tensor_tensor(rest, node_s[:, :, :], node_b[:, 0, :, :], ALU.subtract))
                    link(dve.tensor_copy(node_b[:, 1, :, :], rest))
                    link(dve.tensor_tensor(rest, rest, node_b[:, 1, :, :], ALU.subtract))
                    dve.tensor_copy(node_b[:, 2, :, :], rest).then_inc(done(f"scores{k}"), 1)

            def edge_scores(k, H):
                per = 5 if k == 0 else 2
                with dve.Fori(0, S // UN) as i:
                    for q in range(UN // QU):
                        n = 4 * (S // UN) * k + 4 * i + q
                        linked = (0 if k == 0 else 5 * 4 * (S // UN) + 2 * 4 * (S // UN) * (k - 1)) + per * (4 * i + q)
                        now = bass.ds(i * UN + q * QU, QU)
                        part = picked[:, 0:QU * NT * H]
                        dve.tensor_tensor(lo_hot, iota[:, 0:NT].unsqueeze(1).to_broadcast([P, QU, NT]),
                                          src_lo[:, now].unsqueeze(2).to_broadcast([P, QU, NT]), ALU.is_equal).then_inc(done("sc_dv"), 1)
                        dve.wait_ge(*count("sc_dv", linked + 1))
                        dve.wait_ge(*count("src_mm", n + 3))
                        if k == 0:
                            for b in range(2):
                                last = dve.tensor_tensor(part[:, b * 2 * NT * H:(b + 1) * 2 * NT * H].rearrange("p (u t h) -> p u t h", u=2, t=NT),
                                                         ps[:, b, 0:2 * NT * H].rearrange("p (u t h) -> p u t h", u=2, t=NT),
                                                         lo_hot[:, 2 * b:2 * b + 2, :].unsqueeze(3).to_broadcast([P, 2, NT, H]), ALU.mult)
                        else:
                            last = dve.tensor_tensor(part.rearrange("p (u t h) -> p u t h", u=QU, t=NT),
                                                     ps[:, q % 2, 0:QU * NT * H].rearrange("p (u t h) -> p u t h", u=QU, t=NT),
                                                     lo_hot.unsqueeze(3).to_broadcast([P, QU, NT, H]), ALU.mult)
                        last.then_inc(done("src_used"), 1)
                        dve.wait_ge(*count("src_used", n + 3))
                        dve.tensor_reduce(as_now[:, :, 0:H], part.rearrange("p (u t h) -> p u h t", u=QU, t=NT), AX.X, ALU.add).then_inc(done("sc_dv"), 1)
                        if k == 0:
                            dve.wait_ge(*count("enc_done", 4 * i + q + 3))
                            dve.wait_ge(*count("dst_mm", n + 3))
                            e4 = enc[:, q * QU:q * QU + QU, :]
                            dve.tensor_tensor(e4, e4, ps[:, 4:8, 0:D], ALU.mult).then_inc(done("sc_dv"), 1)
                            dve.wait_ge(*count("sc_dv", linked + 2))
                            dve.tensor_tensor(as_now, as_now, ps[:, 4:8, D + 8:D + 16], ALU.add).then_inc(done("dst_used"), 1)
                            dve.wait_ge(*count("sc_dv", linked + 3))
                            v = peak[:, now, :]
                            dve.tensor_reduce(v, e4.rearrange("p u (h d) -> p u h d", h=8), AX.X, ALU.add).then_inc(done("sc_dv"), 1)
                            dve.wait_ge(*count("sc_dv", linked + 4))
                            dve.wait_ge(*count("dst_used", n + 3))
                            dve.tensor_tensor(alpha[:, now, :], v, as_now, ALU.add).then_inc(done("sc_dv"), 1)
                        else:
                            dve.wait_ge(*count("sc_dv", linked + 2))
                            dve.wait_ge(*count("dst_mm", n + 3))
                            d4 = ps[:, 2 + q % 2, 0:8 * QU].rearrange("p (u h) -> p u h", u=QU)
                            dve.tensor_copy(peak[:, now, 4:8], d4[:, :, 4:8])
                            last = dve.tensor_tensor(alpha[:, now, 0:4], as_now[:, :, 0:4], d4[:, :, 0:4], ALU.add)
                            last.then_inc(done("dst_used"), 1)
                if k == 0:
                    dve.wait_ge(*count("sc_dv", 5 * 4 * (S // UN)))
                dve.wait_ge(*count("dst_used", 4 * (S // UN) * (k + 1) + 2))

            def softmax(k, H):
                al = alpha[:, :, 0:H]
                dve.scalar_tensor_tensor(al, al, 0.2, al, ALU.mult, ALU.max).then_inc(done(f"lrelu{k}"), 1)
                dve.wait_ge(*count(f"lrelu{k}", 1))
                for h in range(H):
                    dve.wait_ge(*count(f"al_t{k}", h + 1))
                    for b in range(SB):
                        last = dve.tensor_tensor_scan(segs[:, h, b, :], reset_f[:, b, :], ps[0:SQ, h % 4, b * P:(b + 1) * P], -BIG, ALU.add, ALU.max)
                    last.then_inc(done(f"scan_f{k}"), 1)
                dve.wait_ge(*count(f"scan_f{k}", H))
                for way in (0, 1):
                    dve.wait_ge(*count(f"ends{k}", way + 1))
                    if way == 0:
                        link(dve.memset(carry[:, 0:1], -BIG))
                        link(dve.tensor_tensor_scan(carry[0:H, 1:S + 1], through_f[0:H, :], ps[0:H, 4, 0:S], -BIG, ALU.add, ALU.max))
                        dve.tensor_tensor(carry2[0:H, :], carry[0:H, 0:S], carry_ok[0:H, 0:S], ALU.add).then_inc(done(f"carried{k}"), 1)
                    else:
                        link(dve.memset(carry[:, S:S + 1], -BIG))
                        link(dve.tensor_tensor_scan(carry[0:H, S - 1::-1], through_r[0:H, ::-1], ps[0:H, 4, S - 1::-1], -BIG, ALU.add, ALU.max))
                        dve.tensor_tensor(carry2[0:H, :], carry[0:H, 1:S + 1], carry_ok[0:H, 1:S + 1], ALU.add).then_inc(done(f"carried{k}"), 1)
                    dve.wait_ge(*count(f"carry_t{k}", way + 1))
                    link(dve.tensor_copy(carry_c[:, :, 0:H], ps[0:SQ, 5, 0:8 * SB].rearrange("p (b h) -> p b h", b=SB)[:, :, 0:H]))
                    same = with_first if way == 0 else with_last
                    for h in range(H):
                        for b in range(SB):
                            last = dve.scalar_tensor_tensor(segs[:, h, b, :], same[:, b, :], carry_c[:, b, h:h + 1], segs[:, h, b, :], ALU.add, ALU.max)
                    if way == 1:
                        last.then_inc(done(f"segs_done{k}"), 1)
                        break
                    link(last)
                    for h in range(H):
                        for b in range(SB):
                            last = dve.tensor_tensor_scan(segs[:, h, b, ::-1], reset_r[:, b, ::-1], segs[:, h, b, ::-1], -BIG, ALU.add, ALU.max)
                    last.then_inc(done(f"scan_r{k}"), H)
                    dve.wait_ge(*count(f"scan_r{k}", H))
                dve.wait_ge(*count(f"peak_ev{k}", H))
                if H == 4:
                    link(dve.tensor_tensor(peak[:, :, 0:4], peak[:, :, 0:4], peak[:, :, 4:8], ALU.max))
                dve.tensor_tensor(al, al, peak[:, :, 0:H], ALU.subtract).then_inc(done(f"alpha_sub{k}"), 1)
                dve.wait_ge(*count(f"exp{k}", 1))
                if H == 4:
                    link(dve.tensor_tensor(peak[:, :, 4:8], al, peak[:, :, 0:4], ALU.mult))
                link(dve.memset(accum[:, :, :], 0.0))

            def add_up(g, w, weighted, H=8, transposed=False):
                def prepare(i, h):
                    half, pair = slice(h * HU, h * HU + HU), slice(h % 2 * HU, h % 2 * HU + HU)
                    now = bass.ds(i * AU + h * HU, HU)
                    dve.wait_ge(step_mm, S * g + AU * i + HU * h + HU + AU - UN)
                    dve.tensor_tensor(onehot[:, pair, :], iota[:, 0:P].unsqueeze(1).to_broadcast([P, HU, P]),
                                      drel[:, now].unsqueeze(2).to_broadcast([P, HU, P]), ALU.is_equal).then_inc(oh_ready, 1)
                    if weighted is not None:
                        for u in range(h * HU, h * HU + HU):
                            dve.wait_ge(gath[u], gath_base(g) + 16 * i + 16)
                        v = slots[:, half, 0:D].rearrange("p u (h d) -> p u h d", h=H)
                        dve.tensor_tensor(v, v, alpha[:, now, 0:H].unsqueeze(3).to_broadcast([P, HU, H, D // H]), ALU.mult)
                        last = dve.tensor_copy(slots[:, half, D:D + H], alpha[:, now, 0:H])
                        if H == 4:
                            last = dve.tensor_copy(slots[:, half, D + 4:D + 8], peak[:, now, 4:8])
                        last.then_inc(msg_ready, 1)

                def add(i, h):
                    dve.load(tn_regs, tn_i[0:1, bass.ds(i * AU + h * HU, HU)])
                    for u in range(HU):
                        at = dve.snap(tn_regs[u], min_val=0, max_val=NT - 1)
                        dve.wait_ge(step_mm, S * g + AU * i + HU * h + u + AU + 1)
                        dve.wait_ge(step_acc, S * g + AU * i + HU * h + u + HU)
                        bank = ps[:, u % 8, 0:w]
                        if transposed:
                            to = accum_t[:, :, bass.ds(at * P, P)]
                            bank = bank.rearrange("p (c n) -> p c n", c=DC)
                        else:
                            to = accum[:, bass.ds(at, 1), 0:w]
                            bank = bank.unsqueeze(1)
                        dve.tensor_tensor(to, to, bank, ALU.add).then_inc(step_acc, 1)

                halves = AU // HU
                prepare(0, 0)
                with dve.Fori(0, S // AU - 1) as i:
                    for h in range(halves):
                        prepare(i + (h + 1) // halves, (h + 1) % halves)
                        add(i, h)
                i = S // AU - 1
                for h in range(halves):
                    if h < halves - 1:
                        prepare(i, h + 1)
                    add(i, h)
                dve.wait_ge(step_acc, S * (g + 1) + HU)

            heads = lambda v, H, w: v.unsqueeze(3).to_broadcast([P, NT, H, w])

            def batch_norm(name, buf, p, n_c, g, be):
                for c in range(n_c):
                    for j, (n0, w) in enumerate(BN_CHUNKS):
                        last = dve.bn_stats(bnst[0:p, c, j, :], buf[0:p, c, n0:n0 + w])
                link(last)
                for c in range(n_c):
                    last = dve.bn_aggr(bnmv[0:p, c, :], bnst[0:p, c, :, :].rearrange("p j s -> p (j s)"))
                link(last)
                dve.tensor_scalar(bnsc[0:p, 0:n_c, 2], bnmv[0:p, 0:n_c, 1], BN_EPS, None, ALU.add).then_inc(done(f"var_bn_{name}"), 1)
                dve.wait_ge(*count(f"std_bn_{name}", 1))
                link(dve.reciprocal(bnsc[0:p, 0:n_c, 2], bnsc[0:p, 0:n_c, 3]))
                gi, bi = COL[g], COL[be]
                link(dve.tensor_tensor(bnsc[0:p, 0:n_c, 0], bnsc[0:p, 0:n_c, 2], vecs[0:p, gi, 0:n_c], ALU.mult))
                link(dve.tensor_tensor(bnsc[0:p, 0:n_c, 2], bnsc[0:p, 0:n_c, 0], bnmv[0:p, 0:n_c, 0], ALU.mult))
                dve.tensor_tensor(bnsc[0:p, 0:n_c, 1], vecs[0:p, bi, 0:n_c], bnsc[0:p, 0:n_c, 2], ALU.subtract).then_inc(done(f"bnsc_{name}"), 1)
                dve.wait_ge(*count(f"bnsc_{name}", 1))

            layer_norm(0)
            node_scores(0, 8, "L1_gnn_a_src", "L1_gnn_a_dst", "l1_ev")
            edge_scores(0, 8)
            softmax(0, 8)
            link(dve.memset(slots[:, :, D + 8:D + 9], 1.0))
            add_up(0, D + 9, 0, 8)
            link(dve.tensor_scalar(small[:, :, :], accum[:, :, D:D + 8], 1e-10, None, ALU.max))
            link(dve.reciprocal(small[:, :, :], small[:, :, :]))
            acc4 = accum[:, :, 0:D].rearrange("p t (h d) -> p t h d", h=8)
            link(dve.tensor_tensor(acc4, acc4, heads(small[:, :, :], 8, 32), ALU.mult))
            link(dve.tensor_tensor(accum[:, :, 0:D], accum[:, :, 0:D], all_rows(row("L1_gnn_bias")), ALU.add))
            link(dve.tensor_tensor(resid[:, :, :], resid[:, :, :], accum[:, :, 0:D], ALU.add))
            link(dve.tensor_scalar(deg[:, :, 0], accum[:, :, D + 8], 1.0, 1.0, ALU.add, ALU.max))
            dve.sem_inc(done("var_deg"), 1)
            layer_norm(1)
            dve.wait_ge(*count("std_deg", 1))
            dve.reciprocal(deg[:, :, 1], deg[:, :, 1]).then_inc(done("dinv"), 1)
            link(dve.memset(accum[:, :, :], 0.0))
            add_up(1, 64, None)
            g64 = accum[:, :, 0:64]
            link(dve.tensor_tensor(g64, g64, hrows[:, :, 0:64], ALU.add))
            link(dve.tensor_tensor(g64, g64, deg[:, :, 1:2].to_broadcast([P, NT, 64]), ALU.mult))
            link(dve.tensor_tensor(g64, g64, all_rows(row("L2_gnn_b_gcn", 64), 64), ALU.add))
            dve.tensor_scalar(g64, g64, 0.0, None, ALU.max).then_inc(done("gcn_out"), 1)
            dve.wait_ge(*count("gcnt_ev", NT))
            batch_norm("gcn", cols, 64, 1, "L2_gnn_g0", "L2_gnn_beta0")
            for k in (1, 2):
                node_scores(k, 4, f"L2_gnn_a_src{k}", f"L2_gnn_a_dst{k}", f"gat{k}_ev")
                edge_scores(k, 4)
                softmax(k, 4)
                add_up(k + 1, D + 8, k, 4)
                self_s, m = node_s[:, :, 12:16], small[:, :, 4:8]
                link(dve.tensor_scalar(small[:, :, 0:4], accum[:, :, D:D + 4], 1e-30, None, ALU.max))
                link(dve.reciprocal(small[:, :, 0:4], small[:, :, 0:4]))
                link(dve.tensor_tensor(m, accum[:, :, D + 4:D + 8], small[:, :, 0:4], ALU.mult))
                link(dve.tensor_scalar(small[:, :, 0:4], accum[:, :, D:D + 4], 0.0, None, ALU.is_gt))
                link(dve.tensor_tensor(m, m, self_s, ALU.subtract))
                link(dve.tensor_tensor(m, m, small[:, :, 0:4], ALU.mult))
                link(dve.tensor_scalar(small[:, :, 0:4], m, 0.0, -1.0, ALU.max, ALU.mult))
                dve.sem_inc(done(f"self_sub{k}"), 1)
                dve.wait_ge(*count(f"self_w{k}", 1))
                h4 = hrows[:, :, 0:D].rearrange("p t (h d) -> p t h d", h=4)
                a4 = accum[:, :, 0:D].rearrange("p t (h d) -> p t h d", h=4)
                link(dve.tensor_tensor(h4, h4, heads(small[:, :, 0:4], 4, 64), ALU.mult))
                link(dve.tensor_tensor(a4, a4, h4, ALU.add))
                link(dve.tensor_tensor(m, accum[:, :, D:D + 4], small[:, :, 0:4], ALU.add))
                link(dve.reciprocal(m, m))
                link(dve.tensor_tensor(a4, a4, heads(m, 4, 64), ALU.mult))
                dve.tensor_tensor(accum[:, :, 0:D], accum[:, :, 0:D], all_rows(row(f"L2_gnn_b{k}")), ALU.add).then_inc(done(f"gat_out{k}"), 1)
                dve.wait_ge(*count(f"gatt{k}_ev", NT))
                batch_norm(f"gat{k}", cols, P, 2, f"L2_gnn_g{k}", f"L2_gnn_beta{k}")
                for c in range(DC):
                    link(dve.tensor_scalar(cols[:, c, :], cols[:, c, :], bnsc[:, c, 0:1], bnsc[:, c, 1:2], ALU.mult, ALU.add))
                    dve.tensor_scalar(accum_t[:, c, :], cols[:, c, :], 0.0, None, ALU.min).then_inc(done(f"elu_neg{k}"), 1)
                for c in range(DC):
                    link(dve.tensor_scalar(cols[:, c, :], cols[:, c, :], 0.0, None, ALU.max))
                    dve.wait_ge(*count(f"elu_exp{k}", c + 1))
                    link(dve.scalar_tensor_tensor(cols[:, c, :], accum_t[:, c, :], -1.0, cols[:, c, :], ALU.add, ALU.add))
                dve.sem_inc(done("gat_in2" if k == 1 else "elu2"), 1)
            for t in range(NT):
                dve.wait_ge(*count("l2r_tp", t + 1))
                dve.tensor_tensor(resid[:, t, :], resid[:, t, :], ps[:, t % 4, 0:D], ALU.add).then_inc(done("l2r_ev"), 1)
            dve.wait_ge(*count("l2r_ev", NT))
            layer_norm(2)
            dve.wait_ge(*count("x3_ev", NT))
            for l in range(3):
                add_up(4 + l, D, None, transposed=True)
                dve.wait_ge(*count(f"gin_mm1_{l}_ev", 2 * len(NODE_CHUNKS)))
                batch_norm(f"gin{l}a", cols, P, 2, f"L3_gnn_l{l}_g1", f"L3_gnn_l{l}_be1")
                if l < 2:
                    dve.wait_ge(*count(f"gin_mm2_{l}_ev", 2 * len(NODE_CHUNKS)))
                    batch_norm(f"gin{l}b", accum_t, P, 2, f"L3_gnn_l{l}_g2", f"L3_gnn_l{l}_be2")
                    dve.wait_ge(*count(f"gin_h{l}", 1))
            link(dve.tensor_tensor(resid[:, :, :], resid[:, :, :], all_rows(row("L3_gnn_l2_b2")), ALU.add))
            for t in range(NT):
                dve.wait_ge(*count("gin_last_mm", t + 1))
                dve.tensor_tensor(resid[:, t, :], resid[:, t, :], ps[:, 4 + t % 4, 0:D], ALU.add).then_inc(done("gin_last_ev"), 1)
            dve.wait_ge(*count("gin_last_ev", NT))
            layer_norm(3)


def kernel(**inputs):
    import numpy as np
    import concourse.bacc as bacc
    from concourse.bass_utils import run_bass_kernel_spmd

    v = {k: np.ascontiguousarray(x) for k, x in inputs.items()}
    arrays = {}

    def tiles(x, fill, n):
        out = np.full((n * P,) + x.shape[1:], fill, x.dtype)
        out[:E] = x
        return out.reshape((n, P) + x.shape[1:])

    src, dst = v["src"].astype(np.int32), v["dst"].astype(np.int32)
    arrays["src2"] = tiles(src, NP - 1, ET)
    arrays["dst2"] = tiles(dst, NP - 1, ET)
    arrays["ew2"] = tiles(v["edge_weight"], 0, ET)
    attr = np.ones((ET, 4, P), np.float32)
    attr[:, 0:3, :] = tiles(v["edge_attr_3"], 0, ET).transpose(0, 2, 1)
    arrays["attr"] = attr.reshape(ET, 4 * P)
    arrays["attr_w"] = np.zeros((AK, D), np.float32)
    for b in range(3):
        arrays["attr_w"][32 * b:32 * b + 12] = np.tile(np.concatenate([v["L1_gnn_edge_W"].T, v["L1_gnn_edge_b"][None]], 0), (3, 1))
    xp = np.zeros((NP, D), np.float32)
    xp[:N] = v["x"]
    arrays["x_pad"] = xp
    arrays["x_cols"] = np.ascontiguousarray(xp.T)
    rows = np.zeros((len(ROWS), D), np.float32)
    for i, name in enumerate(ROWS):
        rows[i, :v[name].size] = v[name].reshape(-1)
    arrays["rows"] = np.ascontiguousarray(np.broadcast_to(rows, (P,) + rows.shape))
    vecs = np.zeros((P, len(COLS), 2), np.float32)
    for i, name in enumerate(COLS):
        f = v[name].reshape(-1, P).T if v[name].size == D else v[name].reshape(-1, 1)
        vecs[:f.shape[0], i, :f.shape[1]] = f
    arrays["vecs"] = vecs
    arrays["L1_gnn_W"] = np.ascontiguousarray(v["L1_gnn_W"].T)
    for name in ["L0_gnn_weight", "L2_gnn_W_gcn", "L2_gnn_W1", "L2_gnn_W2"] + [f"L3_gnn_l{l}_w{j}" for l in range(3) for j in (1, 2)]:
        arrays[name] = v[name]
    nc = bacc.Bacc("TRN2", target_bir_lowering=False, num_devices=1)
    aps = {k: nc.dram_tensor("in_" + k, x.shape, mybir.dt.from_np(x.dtype), kind="ExternalInput").ap() for k, x in arrays.items()}
    aps["out"] = nc.dram_tensor("out_0", (N, D), F32, kind="ExternalOutput").ap()
    build(nc, aps)
    r = run_bass_kernel_spmd(nc, [{"in_" + k: x for k, x in arrays.items()}], core_ids=[0])
    return r.results[0]["out_0"]
```
